# Optimizing a Trainium2 kernel written in Bass

```python
import numpy as np
import jax
import jax.numpy as jnp

def _softmax(x, axis=-1):
    return jax.nn.softmax(x, axis=axis)

def _gelu(x):
    return jax.nn.gelu(x, approximate=True)

def _silu(x):
    return jax.nn.silu(x)

def _sigmoid(x):
    return jax.nn.sigmoid(x)

def _layernorm(x, axis=-1, eps=1e-05):
    m = jnp.mean(x, axis=axis, keepdims=True)
    v = jnp.var(x, axis=axis, keepdims=True)
    return (x - m) / jnp.sqrt(v + eps)

def _scatter_add(tgt, idx, src, axis=0):
    return tgt.at[idx].add(src)

def _segment_sum(src, seg, n):
    return jax.ops.segment_sum(src, seg, n)
kernel_name = 'mk_decoder_postln_d2_seqx_r4_fa11b4'

def setup_inputs(seed: int=0):
    np.random.seed(seed)
    _w = jnp.asarray

    def _rec_inputs():
        import jax
        import jax.numpy as jnp
        _rk = jax.random.key(seed)
        x = -0.0002928 + 1 * jax.random.normal(jax.random.fold_in(_rk, 1), (16, 256, 256), jnp.float32)
        _lenS = 256 - jax.random.randint(jax.random.fold_in(_rk, 7), (16,), 0, max(1, 256 // 4) + 1, jnp.int32)
        _lenS2 = 120 - jax.random.randint(jax.random.fold_in(_rk, 8), (16,), 0, max(1, 120 // 4) + 1, jnp.int32)
        _ctx_512P = jax.random.normal(jax.random.fold_in(_rk, 11), (16, 16, 128), jnp.float32)
        _ctx_512c = jax.random.dirichlet(jax.random.fold_in(_rk, 511), 0.3 * jnp.ones((16,), jnp.float32), (16, 120))
        _ctx_512t = jnp.einsum('bsk,bkd->bsd', _ctx_512c, _ctx_512P)
        _ctx_512t = _ctx_512t * jax.lax.rsqrt(jnp.mean(jnp.square(_ctx_512t)) + 1e-12) * 0.953939
        ctx_512 = -0.000514642 + 1.00011 * (_ctx_512t + 0.3 * jax.random.normal(jax.random.fold_in(_rk, 611), (16, 120, 128), jnp.float32))
        return (x, ctx_512)
    x, ctx_512 = _rec_inputs()

    def _L0_attn_setup():
        import jax, jax.numpy as jnp
        import numpy as np
        B, T, D, H, S = (2, 512, 256, 16, 16)
        HD = D // H
        key = jax.random.key(seed)
        ks = jax.random.split(key, 8)
        x = jax.random.normal(ks[0], (B, T, D), dtype=jnp.float32)
        splat_centers = jax.random.normal(ks[1], (H, S, HD), dtype=jnp.float32) * 0.2
        splat_deltas = jnp.zeros((H, S, HD), dtype=jnp.float32)
        splat_log_scales = jax.random.normal(ks[2], (H, S), dtype=jnp.float32) * 0.2 + np.log(0.5).astype(np.float32)
        splat_log_amplitudes = jax.random.normal(ks[3], (H, S), dtype=jnp.float32) * 0.1 - 0.5
        movement_scale = jnp.asarray(0.08, dtype=jnp.float32)
        temperature = jnp.asarray(1.0, dtype=jnp.float32)
        lim_qkv = 0.5 * np.sqrt(6.0 / (D + 3 * D))
        qkv_w = jax.random.uniform(ks[4], (3 * D, D), dtype=jnp.float32, minval=-lim_qkv, maxval=lim_qkv)
        lim_out = 0.5 * np.sqrt(6.0 / (D + D))
        out_w = jax.random.uniform(ks[5], (D, D), dtype=jnp.float32, minval=-lim_out, maxval=lim_out)
        return {'x': x, 'splat_centers': splat_centers, 'splat_deltas': splat_deltas, 'splat_log_scales': splat_log_scales, 'splat_log_amplitudes': splat_log_amplitudes, 'movement_scale': movement_scale, 'temperature': temperature, 'qkv_w': qkv_w, 'out_w': out_w}
    _L0_attn_all = _L0_attn_setup()
    _L0_attn_in = {k: v for k, v in _L0_attn_all.items() if k in ('splat_centers', 'splat_deltas', 'splat_log_scales', 'splat_log_amplitudes', 'movement_scale', 'temperature', 'qkv_w', 'out_w')}
    del _L0_attn_all

    def _L0_xattn_setup():
        import jax, jax.numpy as jnp
        import numpy as np
        DIM = 256
        LATENT_DIM = 128
        NUM_HEADS = 16
        HEAD_DIM = DIM // NUM_HEADS
        SCALE = HEAD_DIM ** (-0.5)
        key = jax.random.key(seed)
        k1, k2, k3, k4, k5 = jax.random.split(key, 5)
        B, xN, zN = (2, 512, 512)
        x = jax.random.normal(k1, (B, xN, DIM), dtype=jnp.float32)
        z = jax.random.normal(k2, (B, zN, LATENT_DIM), dtype=jnp.float32)
        Wq = jax.random.normal(k3, (DIM, DIM), dtype=jnp.float32) * DIM ** (-0.5)
        Wkv = jax.random.normal(k4, (2 * DIM, LATENT_DIM), dtype=jnp.float32) * LATENT_DIM ** (-0.5)
        Wo = jax.random.normal(k5, (DIM, DIM), dtype=jnp.float32) * DIM ** (-0.5)
        return {'x': x, 'z': z, 'Wq': Wq, 'Wkv': Wkv, 'Wo': Wo}
    _L0_xattn_all = _L0_xattn_setup()
    _L0_xattn_in = {k: v for k, v in _L0_xattn_all.items() if k in ('Wq', 'Wkv', 'Wo')}
    del _L0_xattn_all

    def _L0_ffn_setup():
        import jax, jax.numpy as jnp
        import numpy as np
        B, S, H, E = (4, 512, 256, 8)
        key = jax.random.key(seed)
        k1, k2, k3 = jax.random.split(key, 3)
        scale_w = 1.0 / np.sqrt(H)
        return {'x': jax.random.normal(k1, (B, S, H), dtype=jnp.float32), 'router_w': jax.random.normal(k2, (H, E), dtype=jnp.float32) * scale_w, 'router_b': jnp.zeros((E,), dtype=jnp.float32), 'expert_w': jax.random.normal(k3, (E, H, H), dtype=jnp.float32) * scale_w, 'expert_b': jnp.zeros((E, H), dtype=jnp.float32)}
    _L0_ffn_all = _L0_ffn_setup()
    _L0_ffn_in = {k: v for k, v in _L0_ffn_all.items() if k in ('router_w', 'router_b', 'expert_w', 'expert_b')}
    del _L0_ffn_all

    def _L1_attn_setup():
        import jax, jax.numpy as jnp
        import numpy as np
        D_MODEL = 256
        N_HEAD = 16
        HEAD_DIM = D_MODEL // N_HEAD
        key = jax.random.key(seed)
        k1, k2, k3 = jax.random.split(key, 3)
        B, T = (2, 512)
        s = 1.0 / np.sqrt(D_MODEL)
        return {'x': jax.random.normal(k1, (B, T, D_MODEL), dtype=jnp.float32), 'w_qkv': jax.random.normal(k2, (D_MODEL, 3 * D_MODEL), dtype=jnp.float32) * s, 'b_qkv': jnp.zeros((3 * D_MODEL,), dtype=jnp.float32), 'w_out': jax.random.normal(k3, (D_MODEL, D_MODEL), dtype=jnp.float32) * s, 'b_out': jnp.zeros((D_MODEL,), dtype=jnp.float32)}
    _L1_attn_all = _L1_attn_setup()
    _L1_attn_in = {k: v for k, v in _L1_attn_all.items() if k in ('w_qkv', 'b_qkv', 'w_out', 'b_out')}
    del _L1_attn_all

    def _L1_xattn_setup():
        import jax, jax.numpy as jnp
        import numpy as np
        H, D, C1, C2, S, M, B, W = (16, 32, 256, 128, 512, 128, 2, 4)

        def _ln(x, g, b):
            m = jnp.mean(x, -1, keepdims=True)
            v = jnp.var(x, -1, keepdims=True)
            return (x - m) * jax.lax.rsqrt(v + 1e-05) * g + b

        def _mha(x, y, wq, wk, wv, li1_w, li1_b, lnx_g, lnx_b, lny_g, lny_b, ln3_g, ln3_b, li2_w, li2_b, li3_w, li3_b, causal):
            xn = _ln(x, lnx_g, lnx_b)
            yn = _ln(y, lny_g, lny_b)
            q = jnp.einsum('bsc,hcd->bhsd', xn, wq)
            k = jnp.einsum('btc,hcd->bhtd', yn, wk)
            v = jnp.einsum('btc,hcd->bhtd', yn, wv)
            a = jax.nn.softmax(jnp.einsum('bhsd,bhtd->bhst', q, k) * D ** (-0.5), axis=-1)
            if causal:
                s, t = (a.shape[-2], a.shape[-1])
                mask = (jnp.arange(t)[None, :] > jnp.arange(s)[:, None]).astype(a.dtype)
                a = a * mask
            o = jnp.einsum('bhst,bhtd->bhsd', a, v)
            o = o.transpose(0, 2, 1, 3).reshape(x.shape[0], x.shape[1], H * D)
            x_out = x + o @ li1_w + li1_b
            h = jax.nn.gelu(_ln(x_out, ln3_g, ln3_b) @ li2_w + li2_b, approximate=False)
            return x_out + h @ li3_w + li3_b
        key = jax.random.key(seed)
        ks = iter(jax.random.split(key, 64))

        def w(shape, scale=0.02):
            return jax.random.normal(next(ks), shape, jnp.float32) * scale
        inp = {'xx': jax.random.normal(next(ks), (B, S, C1), jnp.float32), 'ee': jax.random.normal(next(ks), (B, M, C2), jnp.float32), 'ln1_g': jnp.ones(C1, jnp.float32), 'ln1_b': jnp.zeros(C1, jnp.float32), 'ln2_g': jnp.ones(C1, jnp.float32), 'ln2_b': jnp.zeros(C1, jnp.float32)}
        for pfx, cy in (('a1', C1), ('a2', C2)):
            inp[pfx + '_wq'] = w((H, C1, D))
            inp[pfx + '_wk'] = w((H, cy, D))
            inp[pfx + '_wv'] = w((H, cy, D))
            inp[pfx + '_li1_w'] = w((H * D, C1))
            inp[pfx + '_li1_b'] = jnp.zeros(C1, jnp.float32)
            inp[pfx + '_lnx_g'] = jnp.ones(C1, jnp.float32)
            inp[pfx + '_lnx_b'] = jnp.zeros(C1, jnp.float32)
            inp[pfx + '_lny_g'] = jnp.ones(cy, jnp.float32)
            inp[pfx + '_lny_b'] = jnp.zeros(cy, jnp.float32)
            inp[pfx + '_ln3_g'] = jnp.ones(C1, jnp.float32)
            inp[pfx + '_ln3_b'] = jnp.zeros(C1, jnp.float32)
            inp[pfx + '_li2_w'] = w((C1, C1 * W))
            inp[pfx + '_li2_b'] = jnp.zeros(C1 * W, jnp.float32)
            inp[pfx + '_li3_w'] = w((C1 * W, C1))
            inp[pfx + '_li3_b'] = jnp.zeros(C1, jnp.float32)
        inp['training'] = 0
        return inp
    _L1_xattn_all = _L1_xattn_setup()
    _L1_xattn_in = {k: v for k, v in _L1_xattn_all.items() if k in ('ln1_g', 'ln1_b', 'ln2_g', 'ln2_b', 'a1_wq', 'a1_wk', 'a1_wv', 'a1_li1_w', 'a1_li1_b', 'a1_lnx_g', 'a1_lnx_b', 'a1_lny_g', 'a1_lny_b', 'a1_ln3_g', 'a1_ln3_b', 'a1_li2_w', 'a1_li2_b', 'a1_li3_w', 'a1_li3_b', 'a2_wq', 'a2_wk', 'a2_wv', 'a2_li1_w', 'a2_li1_b', 'a2_lnx_g', 'a2_lnx_b', 'a2_lny_g', 'a2_lny_b', 'a2_ln3_g', 'a2_ln3_b', 'a2_li2_w', 'a2_li2_b', 'a2_li3_w', 'a2_li3_b')}
    del _L1_xattn_all

    def _L1_ffn_setup():
        import jax, jax.numpy as jnp
        import numpy as np
        DMODEL = 256
        N_EXPERTS = 16
        EXPERT_SIZE = 64
        K = 4
        key = jax.random.key(seed)
        k1, k2, k3, k4 = jax.random.split(key, 4)
        std_sel = 1.0 / np.sqrt(DMODEL)
        std_val = 1.0 / np.sqrt(N_EXPERTS * EXPERT_SIZE)
        return {'x': jax.random.normal(k1, (4, 512, DMODEL), dtype=jnp.float32), 'expert_sel': jax.random.normal(k2, (N_EXPERTS, DMODEL), dtype=jnp.float32) * std_sel, 'keys': jax.random.normal(k3, (N_EXPERTS, DMODEL, EXPERT_SIZE), dtype=jnp.float32) * std_sel, 'values': jax.random.normal(k4, (N_EXPERTS, EXPERT_SIZE, DMODEL), dtype=jnp.float32) * std_val, 'route_scale': jnp.ones((1,), dtype=jnp.float32)}
    _L1_ffn_all = _L1_ffn_setup()
    _L1_ffn_in = {k: v for k, v in _L1_ffn_all.items() if k in ('expert_sel', 'keys', 'values', 'route_scale')}
    del _L1_ffn_all
    return {'x': x, 'ctx_512': ctx_512, 'L0_attn_splat_centers': _L0_attn_in['splat_centers'], 'L0_attn_splat_deltas': _L0_attn_in['splat_deltas'], 'L0_attn_splat_log_scales': _L0_attn_in['splat_log_scales'], 'L0_attn_splat_log_amplitudes': _L0_attn_in['splat_log_amplitudes'], 'L0_attn_movement_scale': _L0_attn_in['movement_scale'], 'L0_attn_temperature': _L0_attn_in['temperature'], 'L0_attn_qkv_w': _L0_attn_in['qkv_w'], 'L0_attn_out_w': _L0_attn_in['out_w'], 'L0_xattn_Wq': _L0_xattn_in['Wq'], 'L0_xattn_Wkv': _L0_xattn_in['Wkv'], 'L0_xattn_Wo': _L0_xattn_in['Wo'], 'L0_ffn_router_w': _L0_ffn_in['router_w'], 'L0_ffn_router_b': _L0_ffn_in['router_b'], 'L0_ffn_expert_w': _L0_ffn_in['expert_w'], 'L0_ffn_expert_b': _L0_ffn_in['expert_b'], 'L1_attn_w_qkv': _L1_attn_in['w_qkv'], 'L1_attn_b_qkv': _L1_attn_in['b_qkv'], 'L1_attn_w_out': _L1_attn_in['w_out'], 'L1_attn_b_out': _L1_attn_in['b_out'], 'L1_xattn_ln1_g': _L1_xattn_in['ln1_g'], 'L1_xattn_ln1_b': _L1_xattn_in['ln1_b'], 'L1_xattn_ln2_g': _L1_xattn_in['ln2_g'], 'L1_xattn_ln2_b': _L1_xattn_in['ln2_b'], 'L1_xattn_a1_wq': _L1_xattn_in['a1_wq'], 'L1_xattn_a1_wk': _L1_xattn_in['a1_wk'], 'L1_xattn_a1_wv': _L1_xattn_in['a1_wv'], 'L1_xattn_a1_li1_w': _L1_xattn_in['a1_li1_w'], 'L1_xattn_a1_li1_b': _L1_xattn_in['a1_li1_b'], 'L1_xattn_a1_lnx_g': _L1_xattn_in['a1_lnx_g'], 'L1_xattn_a1_lnx_b': _L1_xattn_in['a1_lnx_b'], 'L1_xattn_a1_lny_g': _L1_xattn_in['a1_lny_g'], 'L1_xattn_a1_lny_b': _L1_xattn_in['a1_lny_b'], 'L1_xattn_a1_ln3_g': _L1_xattn_in['a1_ln3_g'], 'L1_xattn_a1_ln3_b': _L1_xattn_in['a1_ln3_b'], 'L1_xattn_a1_li2_w': _L1_xattn_in['a1_li2_w'], 'L1_xattn_a1_li2_b': _L1_xattn_in['a1_li2_b'], 'L1_xattn_a1_li3_w': _L1_xattn_in['a1_li3_w'], 'L1_xattn_a1_li3_b': _L1_xattn_in['a1_li3_b'], 'L1_xattn_a2_wq': _L1_xattn_in['a2_wq'], 'L1_xattn_a2_wk': _L1_xattn_in['a2_wk'], 'L1_xattn_a2_wv': _L1_xattn_in['a2_wv'], 'L1_xattn_a2_li1_w': _L1_xattn_in['a2_li1_w'], 'L1_xattn_a2_li1_b': _L1_xattn_in['a2_li1_b'], 'L1_xattn_a2_lnx_g': _L1_xattn_in['a2_lnx_g'], 'L1_xattn_a2_lnx_b': _L1_xattn_in['a2_lnx_b'], 'L1_xattn_a2_lny_g': _L1_xattn_in['a2_lny_g'], 'L1_xattn_a2_lny_b': _L1_xattn_in['a2_lny_b'], 'L1_xattn_a2_ln3_g': _L1_xattn_in['a2_ln3_g'], 'L1_xattn_a2_ln3_b': _L1_xattn_in['a2_ln3_b'], 'L1_xattn_a2_li2_w': _L1_xattn_in['a2_li2_w'], 'L1_xattn_a2_li2_b': _L1_xattn_in['a2_li2_b'], 'L1_xattn_a2_li3_w': _L1_xattn_in['a2_li3_w'], 'L1_xattn_a2_li3_b': _L1_xattn_in['a2_li3_b'], 'L1_ffn_expert_sel': _L1_ffn_in['expert_sel'], 'L1_ffn_keys': _L1_ffn_in['keys'], 'L1_ffn_values': _L1_ffn_in['values'], 'L1_ffn_route_scale': _L1_ffn_in['route_scale']}

def reference(x, ctx_512, L0_attn_splat_centers, L0_attn_splat_deltas, L0_attn_splat_log_scales, L0_attn_splat_log_amplitudes, L0_attn_movement_scale, L0_attn_temperature, L0_attn_qkv_w, L0_attn_out_w, L0_xattn_Wq, L0_xattn_Wkv, L0_xattn_Wo, L0_ffn_router_w, L0_ffn_router_b, L0_ffn_expert_w, L0_ffn_expert_b, L1_attn_w_qkv, L1_attn_b_qkv, L1_attn_w_out, L1_attn_b_out, L1_xattn_ln1_g, L1_xattn_ln1_b, L1_xattn_ln2_g, L1_xattn_ln2_b, L1_xattn_a1_wq, L1_xattn_a1_wk, L1_xattn_a1_wv, L1_xattn_a1_li1_w, L1_xattn_a1_li1_b, L1_xattn_a1_lnx_g, L1_xattn_a1_lnx_b, L1_xattn_a1_lny_g, L1_xattn_a1_lny_b, L1_xattn_a1_ln3_g, L1_xattn_a1_ln3_b, L1_xattn_a1_li2_w, L1_xattn_a1_li2_b, L1_xattn_a1_li3_w, L1_xattn_a1_li3_b, L1_xattn_a2_wq, L1_xattn_a2_wk, L1_xattn_a2_wv, L1_xattn_a2_li1_w, L1_xattn_a2_li1_b, L1_xattn_a2_lnx_g, L1_xattn_a2_lnx_b, L1_xattn_a2_lny_g, L1_xattn_a2_lny_b, L1_xattn_a2_ln3_g, L1_xattn_a2_ln3_b, L1_xattn_a2_li2_w, L1_xattn_a2_li2_b, L1_xattn_a2_li3_w, L1_xattn_a2_li3_b, L1_ffn_expert_sel, L1_ffn_keys, L1_ffn_values, L1_ffn_route_scale):
    import jax
    import jax.numpy as jnp

    def _L0_attn_ref(x, splat_centers, splat_deltas, splat_log_scales, splat_log_amplitudes, movement_scale, temperature, qkv_w, out_w):
        import jax, jax.numpy as jnp
        import numpy as np
        B, T, D, H, S = (2, 512, 256, 16, 16)
        HD = D // H
        Bx, Tx, Dx = x.shape
        Hx, Sx, hd = splat_centers.shape
        qkv = (x @ qkv_w.T).reshape(Bx, Tx, 3, Hx, hd)
        q, k, v = (qkv[:, :, 0], qkv[:, :, 1], qkv[:, :, 2])
        centers = splat_centers + splat_deltas * jax.nn.sigmoid(movement_scale) * 0.2
        scales = jnp.clip(jnp.exp(splat_log_scales), 0.01, 2.0)
        amplitudes = jnp.clip(jnp.exp(splat_log_amplitudes), 1e-06, 10.0)
        inv_var = -0.5 / (scales ** 2 + 1e-08)
        q_dists = jnp.sum((q[:, :, :, None, :] - centers[None, None]) ** 2, axis=-1)
        k_dists = jnp.sum((k[:, :, :, None, :] - centers[None, None]) ** 2, axis=-1)
        q_weights = jnp.exp(q_dists * inv_var)
        k_weights = jnp.exp(k_dists * inv_var)
        logits = jnp.einsum('bihs,bjhs,hs->bijh', q_weights, k_weights, amplitudes)
        temp = jnp.clip(temperature, 0.1, 10.0)
        attention = jax.nn.softmax(logits / temp, axis=2)
        out = jnp.einsum('bijh,bjhd->bihd', attention, v).reshape(Bx, Tx, Dx)
        return out @ out_w.T

    def _L0_xattn_ref(x, z, Wq, Wkv, Wo):
        import jax, jax.numpy as jnp
        import numpy as np
        DIM = 256
        LATENT_DIM = 128
        NUM_HEADS = 16
        HEAD_DIM = DIM // NUM_HEADS
        SCALE = HEAD_DIM ** (-0.5)
        B, xN, _ = x.shape
        _, zN, _ = z.shape
        Q = (x @ Wq.T).reshape(B, xN, NUM_HEADS, HEAD_DIM)
        KV = (z @ Wkv.T).reshape(B, zN, 2, NUM_HEADS, HEAD_DIM)
        K = KV[:, :, 0]
        V = KV[:, :, 1]
        attn = jnp.einsum('bqhd,bkhd->bhqk', Q, K) * SCALE
        attn = jax.nn.softmax(attn, axis=-1)
        O = jnp.einsum('bhqk,bkhd->bqhd', attn, V).reshape(B, xN, DIM)
        return O @ Wo.T

    def _L0_ffn_ref(x, router_w, router_b, expert_w, expert_b):
        import jax, jax.numpy as jnp
        import numpy as np
        B, S, H, E = (4, 512, 256, 8)
        b, s, h = x.shape
        xt = x.reshape(b * s, h)
        logits = xt @ router_w + router_b
        probs = jax.nn.softmax(logits, axis=-1)
        gate = jnp.max(probs, axis=-1)
        idx = jnp.argmax(probs, axis=-1)
        out_all = jnp.einsum('th,ehd->ted', xt, expert_w) + expert_b[None, :, :]
        e_out = jnp.take_along_axis(out_all, idx[:, None, None], axis=1)[:, 0, :]
        y = gate[:, None] * e_out
        return y.reshape(b, s, h)

    def _L1_attn_ref(x, w_qkv, b_qkv, w_out, b_out):
        import jax, jax.numpy as jnp
        import numpy as np
        D_MODEL = 256
        N_HEAD = 16
        HEAD_DIM = D_MODEL // N_HEAD
        B, T, C = x.shape
        qkv = x @ w_qkv + b_qkv
        q, k, v = jnp.split(qkv, 3, axis=-1)

        def to_heads(t):
            return t.reshape(B, T, N_HEAD, HEAD_DIM).transpose(0, 2, 1, 3)
        q, k, v = (to_heads(q), to_heads(k), to_heads(v))
        scale = 1.0 / np.sqrt(HEAD_DIM).astype(np.float32)
        att = jnp.einsum('bhqd,bhkd->bhqk', q, k) * scale
        causal = jnp.tril(jnp.ones((T, T), dtype=bool))
        att = jnp.where(causal, att, -jnp.inf)
        att = jax.nn.softmax(att, axis=-1)
        y = jnp.einsum('bhqk,bhkd->bhqd', att, v)
        y = y.transpose(0, 2, 1, 3).reshape(B, T, C)
        return y @ w_out + b_out

    def _L1_xattn_ref(xx, ee, ln1_g, ln1_b, ln2_g, ln2_b, a1_wq, a1_wk, a1_wv, a1_li1_w, a1_li1_b, a1_lnx_g, a1_lnx_b, a1_lny_g, a1_lny_b, a1_ln3_g, a1_ln3_b, a1_li2_w, a1_li2_b, a1_li3_w, a1_li3_b, a2_wq, a2_wk, a2_wv, a2_li1_w, a2_li1_b, a2_lnx_g, a2_lnx_b, a2_lny_g, a2_lny_b, a2_ln3_g, a2_ln3_b, a2_li2_w, a2_li2_b, a2_li3_w, a2_li3_b, training):
        import jax, jax.numpy as jnp
        import numpy as np
        H, D, C1, C2, S, M, B, W = (16, 32, 256, 128, 512, 128, 2, 4)

        def _ln(x, g, b):
            m = jnp.mean(x, -1, keepdims=True)
            v = jnp.var(x, -1, keepdims=True)
            return (x - m) * jax.lax.rsqrt(v + 1e-05) * g + b

        def _mha(x, y, wq, wk, wv, li1_w, li1_b, lnx_g, lnx_b, lny_g, lny_b, ln3_g, ln3_b, li2_w, li2_b, li3_w, li3_b, causal):
            xn = _ln(x, lnx_g, lnx_b)
            yn = _ln(y, lny_g, lny_b)
            q = jnp.einsum('bsc,hcd->bhsd', xn, wq)
            k = jnp.einsum('btc,hcd->bhtd', yn, wk)
            v = jnp.einsum('btc,hcd->bhtd', yn, wv)
            a = jax.nn.softmax(jnp.einsum('bhsd,bhtd->bhst', q, k) * D ** (-0.5), axis=-1)
            if causal:
                s, t = (a.shape[-2], a.shape[-1])
                mask = (jnp.arange(t)[None, :] > jnp.arange(s)[:, None]).astype(a.dtype)
                a = a * mask
            o = jnp.einsum('bhst,bhtd->bhsd', a, v)
            o = o.transpose(0, 2, 1, 3).reshape(x.shape[0], x.shape[1], H * D)
            x_out = x + o @ li1_w + li1_b
            h = jax.nn.gelu(_ln(x_out, ln3_g, ln3_b) @ li2_w + li2_b, approximate=False)
            return x_out + h @ li3_w + li3_b
        x = _ln(xx, ln1_g, ln1_b)
        x = x + _mha(x, x, a1_wq, a1_wk, a1_wv, a1_li1_w, a1_li1_b, a1_lnx_g, a1_lnx_b, a1_lny_g, a1_lny_b, a1_ln3_g, a1_ln3_b, a1_li2_w, a1_li2_b, a1_li3_w, a1_li3_b, causal=True)
        x = _ln(x, ln2_g, ln2_b)
        return x + _mha(x, ee, a2_wq, a2_wk, a2_wv, a2_li1_w, a2_li1_b, a2_lnx_g, a2_lnx_b, a2_lny_g, a2_lny_b, a2_ln3_g, a2_ln3_b, a2_li2_w, a2_li2_b, a2_li3_w, a2_li3_b, causal=False)

    def _L1_ffn_ref(x, expert_sel, keys, values, route_scale):
        import jax, jax.numpy as jnp
        import numpy as np
        DMODEL = 256
        N_EXPERTS = 16
        EXPERT_SIZE = 64
        K = 4
        sel_logits = jnp.einsum('btd,ed->bte', x, expert_sel)
        sel_probs = jax.nn.sigmoid(sel_logits)
        _, sel_index = jax.lax.top_k(sel_probs, K)
        sel_val = jnp.take_along_axis(sel_probs, sel_index, axis=-1)
        sel_val = sel_val / jnp.clip(sel_val.sum(-1, keepdims=True), 1e-09)
        sel_val = sel_val * route_scale
        scores_all = jax.nn.relu(jnp.einsum('btd,edh->bteh', x, keys))
        values_all = jnp.einsum('bteh,ehv->btev', scores_all, values)
        sel_idx_exp = sel_index[..., None]
        selected = jnp.take_along_axis(values_all, sel_idx_exp, axis=2)
        out = (selected * sel_val[..., None]).sum(axis=2)
        return out
    x = _layernorm(x + _L0_attn_ref(x, L0_attn_splat_centers, L0_attn_splat_deltas, L0_attn_splat_log_scales, L0_attn_splat_log_amplitudes, L0_attn_movement_scale, L0_attn_temperature, L0_attn_qkv_w, L0_attn_out_w), axis=-1)
    x = _layernorm(x + _L0_xattn_ref(x, ctx_512, L0_xattn_Wq, L0_xattn_Wkv, L0_xattn_Wo), axis=-1)
    x = _layernorm(x + _L0_ffn_ref(x, L0_ffn_router_w, L0_ffn_router_b, L0_ffn_expert_w, L0_ffn_expert_b), axis=-1)
    x = _layernorm(x + _L1_attn_ref(x, L1_attn_w_qkv, L1_attn_b_qkv, L1_attn_w_out, L1_attn_b_out), axis=-1)
    x = _layernorm(x + _L1_xattn_ref(x, ctx_512, L1_xattn_ln1_g, L1_xattn_ln1_b, L1_xattn_ln2_g, L1_xattn_ln2_b, L1_xattn_a1_wq, L1_xattn_a1_wk, L1_xattn_a1_wv, L1_xattn_a1_li1_w, L1_xattn_a1_li1_b, L1_xattn_a1_lnx_g, L1_xattn_a1_lnx_b, L1_xattn_a1_lny_g, L1_xattn_a1_lny_b, L1_xattn_a1_ln3_g, L1_xattn_a1_ln3_b, L1_xattn_a1_li2_w, L1_xattn_a1_li2_b, L1_xattn_a1_li3_w, L1_xattn_a1_li3_b, L1_xattn_a2_wq, L1_xattn_a2_wk, L1_xattn_a2_wv, L1_xattn_a2_li1_w, L1_xattn_a2_li1_b, L1_xattn_a2_lnx_g, L1_xattn_a2_lnx_b, L1_xattn_a2_lny_g, L1_xattn_a2_lny_b, L1_xattn_a2_ln3_g, L1_xattn_a2_ln3_b, L1_xattn_a2_li2_w, L1_xattn_a2_li2_b, L1_xattn_a2_li3_w, L1_xattn_a2_li3_b, 0), axis=-1)
    x = _layernorm(x + _L1_ffn_ref(x, L1_ffn_expert_sel, L1_ffn_keys, L1_ffn_values, L1_ffn_route_scale), axis=-1)
    return x

_drawn_inputs = setup_inputs


def setup_inputs(seed=0):
    import zlib

    import numpy as np

    out = dict(_drawn_inputs(seed))
    spreads = {'L0_attn_splat_deltas': (0.0, 0.8),
     'L0_ffn_router_b': (0.0, 0.1),
     'L0_ffn_expert_b': (0.0, 0.1),
     'L1_attn_b_qkv': (0.0, 0.1),
     'L1_attn_b_out': (0.0, 0.1),
     'L1_xattn_ln1_g': (1.0, 0.2),
     'L1_xattn_ln1_b': (0.0, 0.1),
     'L1_xattn_ln2_g': (1.0, 0.2),
     'L1_xattn_ln2_b': (0.0, 0.1),
     'L1_xattn_a1_li1_b': (0.0, 0.271),
     'L1_xattn_a1_lnx_g': (1.0, 0.6),
     'L1_xattn_a1_lnx_b': (0.0, 0.8),
     'L1_xattn_a1_lny_g': (1.0, 0.6),
     'L1_xattn_a1_lny_b': (0.0, 0.8),
     'L1_xattn_a1_ln3_g': (1.0, 0.6),
     'L1_xattn_a1_ln3_b': (0.0, 0.8),
     'L1_xattn_a1_li2_b': (0.0, 0.543),
     'L1_xattn_a1_li3_b': (0.0, 0.269),
     'L1_xattn_a2_li1_b': (0.0, 0.1),
     'L1_xattn_a2_lnx_g': (1.0, 0.6),
     'L1_xattn_a2_lnx_b': (0.0, 0.8),
     'L1_xattn_a2_lny_g': (1.0, 0.6),
     'L1_xattn_a2_lny_b': (0.0, 0.8),
     'L1_xattn_a2_ln3_g': (1.0, 0.6),
     'L1_xattn_a2_ln3_b': (0.0, 0.8),
     'L1_xattn_a2_li2_b': (0.0, 0.521),
     'L1_xattn_a2_li3_b': (0.0, 0.1)}
    factors = {'L0_attn_splat_centers': 8.0,
     'L0_attn_splat_log_scales': 8.0,
     'L0_attn_splat_log_amplitudes': 8.0,
     'L1_xattn_a1_wq': 8.0,
     'L1_xattn_a1_wk': 8.0,
     'L1_xattn_a1_wv': 3.085,
     'L1_xattn_a1_li1_w': 3.044,
     'L1_xattn_a2_wq': 8.0,
     'L1_xattn_a2_wk': 8.0}
    for name, (base, spread) in spreads.items():
        noise = np.random.default_rng([zlib.crc32(name.encode()), seed]).standard_normal(out[name].shape)
        drawn = base * np.exp(spread * noise) if base else spread * noise
        out[name] = jnp.asarray(drawn.astype(out[name].dtype))
    for name, factor in factors.items():
        out[name] = (out[name] * factor).astype(out[name].dtype)
    return out
```

```python
from contextlib import ExitStack

import concourse.bass as bass
from concourse import mybir

F32 = mybir.dt.float32
F32R = mybir.dt.float32r
BF16 = mybir.dt.bfloat16
ALU = mybir.AluOpType
ACT = mybir.ActivationFunctionType
AX = mybir.AxisListType

P = 128
BATCH, TOK, DM, CTX_TOK, CTX_DIM = 16, 256, 256, 120, 128
STREAMS = 2
HEADS = 16
NT = TOK // P
KT = DM // P
GROUPS = 2
HG = HEADS // GROUPS
EPS = 1e-5
EXPERTS, TOP_EXPERTS, TOP_DIM, TOP_K = 8, 16, 64, 4
HID = 1024
NEG = -1.0e30
LOW, MARK = -3.0e38, 3.0e38
RING = 3
PBUF = 4
MBUF = 3
GROUP0_AT = 11
MAX_LAG, PV_LAG = 2, 2


class Attn:

    def __init__(self, name, dim, keys, scale, causal=False, keep_after=False, splat=False):
        self.name, self.dim, self.keys, self.scale = name, dim, keys, scale
        self.causal, self.keep_after, self.splat = causal, keep_after, splat
        self.tiles = HEADS * dim // P
        self.key_tiles = [(0, min(keys, P))] + ([(P, keys - P)] if keys > P else [])

    def at(self, h):
        if self.dim == 32:
            return h // 4, 32 * (h % 4), h // 4
        return h // 8, 32 * ((h % 8) // 2), 2 * (h % 2) + h // 8


ATTNS = [
    Attn("splat", 16, TOK, 1.0, splat=True),
    Attn("cross0", 16, CTX_TOK, 0.25),
    Attn("causal", 16, TOK, 0.25, causal=True),
    Attn("self1", 32, TOK, 32 ** -0.5, keep_after=True),
    Attn("cross1", 32, CTX_TOK, 32 ** -0.5),
]
SPLAT, CROSS0, CAUSAL, SELF1, CROSS1 = ATTNS


class Counts:

    def __init__(self):
        self.increments, self.awaited = {}, {}

    def one(self, sem):
        self.increments[sem.num] = self.increments.get(sem.num, 0) + 1
        return 1

    def sent(self, sem):
        return self.increments.get(sem.num, 0)

    def upcoming(self, engine, sem, n=1):
        key = (str(engine.engine), sem.num)
        self.awaited[key] = self.awaited.get(key, 0) + n
        return self.awaited[key]

    def bank_of(self, engine, full):
        return (self.awaited[(str(engine.engine), full.num)] - 1) % RING


def decoder(nc, io, out):
    with ExitStack() as ctx:
        def sb(name, shape, dt=F32):
            return ctx.enter_context(nc.sbuf_tensor(name, shape, dt))

        def semaphore(name):
            return ctx.enter_context(nc.semaphore(name))

        w_qkv0 = sb("w_qkv0", [P, KT, 3 * DM])
        w_o0 = sb("w_o0", [P, KT, DM])
        w_q1 = sb("w_q1", [P, KT, DM])
        w_kv1 = sb("w_kv1", [P, 2 * DM])
        w_o1 = sb("w_o1", [P, KT, DM])
        w_router = sb("w_router", [P, KT, EXPERTS])
        w_exp = sb("w_exp", [P, EXPERTS, KT, DM])
        b_exp = sb("b_exp", [EXPERTS, DM])
        w_qkv2 = sb("w_qkv2", [P, KT, 3 * DM])
        w_o2 = sb("w_o2", [P, KT, DM])
        bq2 = sb("bq2", [P, 6])
        w_aq = [sb(f"w_aq{a}", [P, KT, 512]) for a in range(2)]
        w_ak = [sb("w_ak0", [P, KT, 512]), sb("w_ak1", [P, 1, 512])]
        w_av = [sb("w_av0", [P, KT, 512]), sb("w_av1", [P, 1, 512])]
        w_li1 = [sb(f"w_li1_{a}", [P, 4, DM]) for a in range(2)]
        w_li2 = [sb(f"w_li2_{a}", [P, KT, HID]) for a in range(2)]
        w_li3 = [sb(f"w_li3_{a}", [P, HID // P, DM]) for a in range(2)]
        b_li2 = [sb(f"b_li2_{a}", [P, HID // P]) for a in range(2)]
        gx = [sb(f"gx{a}", [P, KT]) for a in range(2)]
        bx = [sb(f"bx{a}", [P, KT]) for a in range(2)]
        gy = [sb("gy0", [P, KT]), sb("gy1", [P, 1])]
        by = [sb("by0", [P, KT]), sb("by1", [P, 1])]
        g3 = [sb(f"g3{a}", [P, KT]) for a in range(2)]
        b3 = [sb(f"b3{a}", [P, KT]) for a in range(2)]
        w_sel = sb("w_sel", [P, KT, TOP_EXPERTS])
        w_keys = sb("w_keys", [P, KT, HID])
        w_vals = sb("w_vals", [P, HID // P, DM])
        r_bo2 = sb("r_bo2", [P, DM])
        r_li1 = [sb(f"r_li1_{a}", [P, DM]) for a in range(2)]
        r_li3 = [sb(f"r_li3_{a}", [P, DM]) for a in range(2)]
        r_g = [sb(f"r_g{a}", [P, DM]) for a in range(2)]
        r_b = [sb(f"r_b{a}", [P, DM]) for a in range(2)]
        r_router = sb("r_router", [P, EXPERTS])
        r_route = sb("r_route", [P, 1])

        ident = sb("ident", [P, P])
        ident_r = sb("ident_r", [P, P], F32R)
        ident_b = sb("ident_b", [P, P], BF16)
        mask_q = sb("mask_q", [P, NT, TOK], BF16)
        mask_k = sb("mask_k", [P, P], BF16)
        block16 = sb("block16", [P, 8, 16])
        minus2c = sb("minus2c", [P, KT, P])
        parity = sb("parity", [P, 2])
        spread = sb("spread", [TOP_EXPERTS, HID // P, P])
        zero_one = sb("zero_one", [P, 33])
        inv_var = sb("inv_var", [P, KT])
        w_bias = sb("w_bias", [P, KT])
        k_scale = sb("k_scale", [P, 2, KT])
        s_small = sb("s_small", [P, 16])
        cen = sb("cen", [P, 2, KT, 16])
        dlt = sb("dlt", [P, 2, KT, 16])
        minus_half = sb("minus_half", [P, NT])

        x = [sb(f"x{s}", [P, NT, DM]) for s in range(STREAMS)]
        xa = [sb(f"xa{s}", [P, NT, DM]) for s in range(STREAMS)]
        xo = [sb(f"xo{s}", [P, NT, DM]) for s in range(STREAMS)]
        z = [sb(f"z{s}", [P, NT, DM]) for s in range(STREAMS)]
        cx = [sb(f"cx{s}", [P, CTX_DIM]) for s in range(STREAMS)]
        cxT = [sb(f"cxT{s}", [P, CTX_TOK]) for s in range(STREAMS)]
        xT = sb("xT", [P, KT, TOK])
        yT = sb("yT", [P, KT, TOK])
        raw = sb("raw", [P, 8, TOK])
        qh = sb("qh", [P, 4, TOK], F32R)
        ql = sb("ql", [P, 4, TOK], F32R)
        kh = sb("kh", [P, 4, TOK], F32R)
        kl = sb("kl", [P, 4, TOK], F32R)
        v16 = sb("v16", [P, NT, HEADS, 17])
        v32 = sb("v32", [P, NT, HEADS, 33])
        o_tok = sb("o_tok", [P, NT, 512])
        oT = sb("oT", [P, 4, TOK])
        prob = sb("prob", [P, PBUF, NT * TOK])
        probm = sb("probm", [P, MBUF, NT, P])
        negm = sb("negm", [P, HEADS * NT], F32R)
        recip = sb("recip", [P, NT, HG])
        stats = sb("stats", [P, NT, 6])
        mv = sb("mv", [P, NT, 2])
        veps = sb("veps", [P, NT])
        rstd = sb("rstd", [P, NT])
        lg = sb("lg", [P, NT, 16])
        lgv = sb("lgv", [P, NT, 8])
        top8 = sb("top8", [P, NT, 8])
        mr = sb("mr", [P, NT, 24])
        nmax = sb("nmax", [P, NT])
        esum = sb("esum", [P, NT])
        ex = sb("ex", [P, NT, 16])
        gate = sb("gate", [P, NT])
        gm = sb("gm", [P, NT, 16])
        gmT = sb("gmT", [16, TOK])
        pe16 = sb("pe16", [P, NT, 24])
        pv = sb("pv", [P, NT, 8])

        bank = [ctx.enter_context(nc.psum_tensor(f"bank{i}", [P, 512], F32)) for i in range(8)]

        ring_a, ring_v, o_bank = bank[0:3], bank[3:6], bank[6:8]

        w_ready = [semaphore(f"w_ready{i}") for i in range(8)]
        w_count = [0] * 8
        s_sp = semaphore("s_sp")
        s_const = semaphore("s_const")
        first = semaphore("first_of_loop")
        a_full, v_full, o_full = semaphore("a_full"), semaphore("v_full"), semaphore("o_full")
        a_done, v_done, o_done = semaphore("a_done"), semaphore("v_done"), semaphore("o_done")
        x_in, c_in = semaphore("x_in"), semaphore("c_in")
        sq_ready = semaphore("sq_ready")
        qk_ready = semaphore("qk_ready")
        pm_ready = semaphore("pm_ready")
        z_ready = semaphore("z_ready")
        zo_ready = semaphore("zo_ready")
        zc_ready = semaphore("zc_ready")
        var_ready = semaphore("var_ready")
        rstd_ready = semaphore("rstd_ready")
        nmax_ready = semaphore("nmax_ready")
        exps_ready = semaphore("exps_ready")
        gm_ready = semaphore("gm_ready")
        xo_ready, xa_ready = semaphore("xo_ready"), semaphore("xa_ready")
        dve_step = semaphore("dve_step")
        out_ready, out_done = semaphore("out_ready"), semaphore("out_done")
        last_sem = semaphore("last_of_loop")
        loop_sems = range(first.num, last_sem.num + 1)
        counts = Counts()
        one, sent, upcoming, bank_of = counts.one, counts.sent, counts.upcoming, counts.bank_of

        def load(e, i, dst, src):
            e.dma_start(dst, src).then_inc(w_ready[i], 16)
            w_count[i] += 16

        def rows(ap, kt):
            return ap.rearrange("(t p) n -> p t n", p=P) if kt > 1 else ap

        def spread_row(ap):
            return ap.rearrange("(a n) -> a n", a=1).broadcast_to([P, ap.shape[0]])

        with nc.Block() as block:
            @block.sync
            def _(e):
                load(e, 0, cen[:, 0], io["centers"].rearrange("(t p) d -> p t d", p=P))
                load(e, 0, cen[:, 1], io["centers_t"].rearrange("(t p) d -> p t d", p=P))
                load(e, 0, dlt[:, 0], io["deltas"].rearrange("(t p) d -> p t d", p=P))
                load(e, 0, dlt[:, 1], io["deltas_t"].rearrange("(t p) d -> p t d", p=P))
                load(e, 0, s_small[:, 0:2], io["log_scales"])
                load(e, 0, s_small[:, 2:4], io["log_amps"])
                load(e, 0, s_small[:, 4:5], spread_row(io["movement"]))
                load(e, 0, s_small[:, 5:6], spread_row(io["temperature"]))
                load(e, 1, w_qkv0[:, :, :], rows(io["qkv0"], 2))
                load(e, 1, w_o0[:, :, :], rows(io["o0"], 2))
                load(e, 2, w_q1[:, :, :], rows(io["q1"], 2))
                load(e, 2, w_kv1[:, :], io["kv1"])
                load(e, 2, w_o1[:, :, :], rows(io["o1"], 2))
                load(e, 3, w_router[:, :, :], rows(io["router"], 2))
                load(e, 3, b_exp[:, :], io["expert_b"])
                load(e, 3, r_router[:, :], spread_row(io["router_b"]))
                for x_ in range(EXPERTS):
                    load(e, 3, w_exp[:, x_], rows(io["expert_w"][x_], 2))
                load(e, 4, w_qkv2[:, :, :], rows(io["qkv2"], 2))
                load(e, 4, w_o2[:, :, :], rows(io["o2"], 2))
                load(e, 4, bq2[:, :], io["bqkv2"])
                load(e, 4, r_bo2[:, :], spread_row(io["bo2"]))
                for a in range(2):
                    kt = KT if a == 0 else 1
                    load(e, 5 + a, gx[a][:, :], io[f"lnx_g{a}"])
                    load(e, 5 + a, bx[a][:, :], io[f"lnx_b{a}"])
                    load(e, 5 + a, gy[a][:, :], io[f"lny_g{a}"])
                    load(e, 5 + a, by[a][:, :], io[f"lny_b{a}"])
                    load(e, 5 + a, g3[a][:, :], io[f"ln3_g{a}"])
                    load(e, 5 + a, b3[a][:, :], io[f"ln3_b{a}"])
                    load(e, 5 + a, b_li2[a][:, :], io[f"li2_b{a}"])
                    load(e, 5 + a, r_li1[a][:, :], spread_row(io[f"li1_b{a}"]))
                    load(e, 5 + a, r_li3[a][:, :], spread_row(io[f"li3_b{a}"]))
                    load(e, 5 + a, r_g[a][:, :], spread_row(io[f"ln_g{a}"]))
                    load(e, 5 + a, r_b[a][:, :], spread_row(io[f"ln_b{a}"]))
                    load(e, 5 + a, w_aq[a][:, :, :], rows(io[f"wq{a}"], 2))
                    load(e, 5 + a, w_ak[a][:, :, :] if kt > 1 else w_ak[a][:, 0], rows(io[f"wk{a}"], kt))
                    load(e, 5 + a, w_av[a][:, :, :] if kt > 1 else w_av[a][:, 0], rows(io[f"wv{a}"], kt))
                    load(e, 5 + a, w_li1[a][:, :, :], rows(io[f"li1_{a}"], 4))
                    load(e, 5 + a, w_li2[a][:, :, :], rows(io[f"li2_{a}"], 2))
                    load(e, 5 + a, w_li3[a][:, :, :], rows(io[f"li3_{a}"], 8))
                load(e, 7, w_sel[:, :, :], rows(io["sel"], 2))
                load(e, 7, w_keys[:, :, :], rows(io["keys"], 2))
                load(e, 7, w_vals[:, :, :], rows(io["values"], 8))
                load(e, 7, r_route[:, :], spread_row(io["route"]))

            @block.gpsimd
            def _(e):
                g = nc.gpsimd
                made = [0]

                def step(instruction):
                    made[0] += 1
                    instruction.then_inc(s_const, 1)
                    e.wait_ge(s_const, made[0])

                for t in (ident, ident_b, mask_k, mask_q):
                    step(g.memset(t[:], 0.0))
                for t in (block16, spread, minus_half, zero_one):
                    step(g.memset(t[:], 1.0))
                for t in (ident, ident_b):
                    step(g.affine_select(out=t[:, :], in_=t[:, :], compare_op=ALU.not_equal, fill=1.0,
                                         base=0, pattern=[[-1, P]], channel_multiplier=1))
                step(g.affine_select(out=mask_k[:, :], in_=mask_k[:, :], compare_op=ALU.is_ge, fill=NEG,
                                     base=0, pattern=[[1, P]], channel_multiplier=-1))
                step(g.affine_select(out=mask_q[:, :, :], in_=mask_q[:, :, :], compare_op=ALU.is_ge, fill=NEG,
                                     base=0, pattern=[[P, NT], [-1, TOK]], channel_multiplier=1))
                step(g.affine_select(out=block16[:, :, :], in_=block16[:, :, :], compare_op=ALU.is_ge, fill=0.0,
                                     base=0, pattern=[[-16, 8], [0, 16]], channel_multiplier=1))
                step(g.affine_select(out=block16[:, :, :], in_=block16[:, :, :], compare_op=ALU.is_ge, fill=0.0,
                                     base=15, pattern=[[16, 8], [0, 16]], channel_multiplier=-1))
                step(g.affine_select(out=spread[:, :, :], in_=spread[:, :, :], compare_op=ALU.is_ge, fill=0.0,
                                     base=0, pattern=[[P, HID // P], [1, P]], channel_multiplier=-TOP_DIM))
                step(g.affine_select(out=spread[:, :, :], in_=spread[:, :, :], compare_op=ALU.is_ge, fill=0.0,
                                     base=TOP_DIM - 1, pattern=[[-P, HID // P], [-1, P]],
                                     channel_multiplier=TOP_DIM))
                step(g.memset(zero_one[:, 0:32], 0.0))
                step(g.memset(minus_half[:, :], -0.5))
                step(g.memset(v16[:, :, :, 16:17], 1.0))
                step(g.memset(v32[:, :, :, 32:33], 1.0))
                step(g.memset(lg[:, :, 8:16], LOW))
                step(g.memset(lgv[:, :, :], LOW))
                step(g.memset(pe16[:, :, 16:24], -1.0))
                step(g.memset(pv[:, :, :], -1.0))
                step(g.memset(gm[:, :, :], 0.0))
                g.memset(s_small[:, 14:15], 0.0).then_inc(s_sp, 1)
            n_const = 27

            s_act = semaphore("s_act")
            s_dv = semaphore("s_dv")

            @block.scalar
            def _(e):
                e.wait_ge(w_ready[0], w_count[0])
                nc.scalar.activation(s_small[:, 6:10], s_small[:, 0:4], ACT.Exp).then_inc(s_act, 1)
                nc.scalar.activation(s_small[:, 10:11], s_small[:, 4:5], ACT.Exp, scale=-1.0).then_inc(s_act, 1)

            @block.vector
            def _(e):
                v = nc.vector
                made = [0]

                def step(instruction):
                    made[0] += 1
                    instruction.then_inc(s_dv, 1)
                    e.wait_ge(s_dv, made[0])

                e.wait_ge(s_sp, 1)
                e.wait_ge(w_ready[0], w_count[0])
                step(v.tensor_copy(ident_r[:, :], ident[:, :]))
                e.wait_ge(s_act, 2)
                step(v.tensor_scalar(s_small[:, 6:8], s_small[:, 6:8], 0.01, 2.0, ALU.max, ALU.min))
                step(v.tensor_scalar(s_small[:, 8:10], s_small[:, 8:10], 1e-6, 10.0, ALU.max, ALU.min))
                step(v.tensor_tensor(s_small[:, 6:8], s_small[:, 6:8], s_small[:, 6:8], ALU.mult))
                step(v.tensor_scalar(s_small[:, 6:8], s_small[:, 6:8], 1e-8, None, ALU.add))
                step(v.reciprocal(s_small[:, 6:8], s_small[:, 6:8]))
                step(v.tensor_scalar(inv_var[:, :], s_small[:, 6:8], -0.5, None, ALU.mult))
                step(v.tensor_scalar(s_small[:, 10:11], s_small[:, 10:11], 1.0, None, ALU.add))
                step(v.reciprocal(s_small[:, 10:11], s_small[:, 10:11]))
                step(v.tensor_scalar(dlt[:, :, :, :], dlt[:, :, :, :], s_small[:, 10:11], 0.2, ALU.mult, ALU.mult))
                step(v.tensor_tensor(cen[:, :, :, :], cen[:, :, :, :], dlt[:, :, :, :], ALU.add))
                step(v.tensor_tensor(dlt[:, 0], cen[:, 0], cen[:, 0], ALU.mult))
                step(v.tensor_reduce(w_bias[:, :], dlt[:, 0], AX.X, ALU.add))
                step(v.tensor_tensor(w_bias[:, :], w_bias[:, :], inv_var[:, :], ALU.mult))
                step(v.tensor_scalar(s_small[:, 5:6], s_small[:, 5:6], 0.1, 10.0, ALU.max, ALU.min))
                step(v.reciprocal(s_small[:, 5:6], s_small[:, 5:6]))
                step(v.tensor_scalar(s_small[:, 8:10], s_small[:, 8:10], s_small[:, 5:6], None, ALU.mult))
                for o in range(2):
                    step(v.tensor_reduce(parity[:, o:o + 1], block16[:, o::2, 0], AX.X, ALU.add))
                    step(v.tensor_scalar(k_scale[:, o], s_small[:, 8:10], parity[:, o:o + 1], None, ALU.mult))
                step(v.tensor_scalar(cen[:, 1], cen[:, 1], -2.0, None, ALU.mult))
                for t in range(KT):
                    step(v.tensor_tensor(minus2c[:, t].rearrange("p (h s) -> p h s", s=16), block16[:, :, :],
                                         cen[:, 1, t:t + 1, :].broadcast_to([P, 8, 16]), ALU.mult))

        with nc.Fori(0, BATCH // STREAMS) as pair:
            with nc.Block() as block:
                @block.sync
                def _(e):
                    for s in range(STREAMS):
                        b = pair * STREAMS + s
                        e.dma_start(x[s][:, :, :], io["x"][bass.ds(b, 1)].rearrange("a (t p) f -> p (a t) f", p=P)
                                    ).then_inc(x_in, 16)
                        e.dma_start(cxT[s][:, :], io["ctx_t"][bass.ds(b, 1)].rearrange("a f t -> f (a t)")
                                    ).then_inc(c_in, 16)
                        e.dma_start(cx[s][0:CTX_TOK, :], io["ctx"][bass.ds(b, 1)].rearrange("a t f -> (a t) f")
                                    ).then_inc(c_in, 16)
                    for s in range(STREAMS):
                        b = pair * STREAMS + s
                        e.wait_ge(out_ready, upcoming(e, out_ready))
                        e.dma_start(out[bass.ds(b, 1)].rearrange("a (t p) f -> p (a t) f", p=P), x[s][:, :, :]
                                    ).then_inc(out_done, 16)
                    e.wait_ge(out_done, 16 * STREAMS)

                number = {}
                at = [0, 0]

                def moved(*what):
                    return number[(at[0], at[1], *what)] + 1


                @block.tensor
                def _(e):
                    mm = nc.tensor.matmul
                    used = {"a": 0, "v": 0}

                    def slot(which, what=None):
                        n = used[which]
                        used[which] += 1
                        number[(at[0], at[1], what)] = n
                        if which == "a":
                            if n >= RING:
                                e.wait_ge(a_done, n + 1 - RING)
                            return ring_a[n % RING]
                        if n >= RING:
                            e.wait_ge(v_done, n + 1 - RING)
                        return ring_v[n % RING]

                    def transposes(src, n_feat, what):
                        ps = slot("a", what)
                        for f in range(n_feat):
                            for t in range(NT):
                                last = nc.tensor.transpose(ps[:, f * TOK + t * P:f * TOK + t * P + P],
                                                           src[:, t, f * P:f * P + P], ident[:, :])
                        last.then_inc(a_full, one(a_full))

                    def to_xT(src, ready, what="xT"):
                        if ready is not None:
                            e.wait_ge(ready, upcoming(e, ready))
                        transposes(src, KT, what)
                        e.wait_ge(a_done, moved(what))

                    def feature_major(ws, col, tiles, src, n_in, n_tok, what):
                        for m in range(0, tiles, 2):
                            ps = slot("a", what)
                            for i in range(2):
                                for k in range(n_in):
                                    last = mm(ps[:, i * TOK:i * TOK + n_tok],
                                              ws[:, k, col + (m + i) * P:col + (m + i + 1) * P],
                                              src[:, k, 0:n_tok], start=k == 0, stop=k == n_in - 1)
                            last.then_inc(a_full, one(a_full))

                    def token_major(ws, col, cols, src, n_in, tiles, which, what=None):
                        ps = slot(which, what)
                        for i, (t0, n) in enumerate(tiles):
                            for k in range(n_in):
                                last = mm(ps[0:n, i * cols:(i + 1) * cols], src[:, k, t0:t0 + n],
                                          ws[:, k, col:col + cols], start=k == 0, stop=k == n_in - 1)
                        full = a_full if which == "a" else v_full
                        last.then_inc(full, one(full))

                    token_tiles = [(t * P, P) for t in range(NT)]

                    def values(a, ws, col, src, n_in):
                        if a.dim == 16:
                            token_major(ws, col, 256, src, n_in, a.key_tiles, "a", "v")
                        else:
                            for tile in a.key_tiles:
                                token_major(ws, col, 512, src, n_in, [tile], "a", "v")

                    def row_scores(a, h):
                        t, q0, kx = a.at(h)
                        ps = slot("v", ("max", h))
                        for i in range(NT):
                            o = ps[:, i * TOK:i * TOK + a.keys]
                            last = mm(o, qh[q0:q0 + 32, t, i * P:i * P + P], kh[q0:q0 + 32, kx, 0:a.keys],
                                      start=True, stop=not a.causal)
                            if a.causal:
                                last = mm(o, ident_b[:, :], mask_q[:, i, :], start=False, stop=True)
                        last.then_inc(v_full, one(v_full))

                    def exact_scores(a, h):
                        t, q0, kx = a.at(h)
                        ps = slot("a", ("p", h))
                        e.wait_ge(v_done, moved(("max", h)))
                        for j, (k0, n) in enumerate(a.key_tiles):
                            i0 = j * P if a.causal else 0
                            c0 = j * TOK
                            o = ps[0:n, c0:c0 + TOK - i0]
                            hi, lo = kh[q0:q0 + 32, kx, k0:k0 + n], kl[q0:q0 + 32, kx, k0:k0 + n]
                            mm(o, hi, qh[q0:q0 + 32, t, i0:TOK], start=True, stop=False)
                            mm(o, hi, ql[q0:q0 + 32, t, i0:TOK], start=False, stop=False)
                            mm(o, lo, qh[q0:q0 + 32, t, i0:TOK], start=False, stop=False)
                            if a.causal:
                                mm(ps[0:n, c0:c0 + P], ident_b[:, :], mask_k[:, :], start=False, stop=False)
                            for i in range(i0 // P, NT):
                                c = c0 + i * P - i0
                                last = mm(ps[0:n, c:c + P], negm[:, h * NT + i:h * NT + i + 1].broadcast_to([P, n]),
                                          ident_r[:, :], start=False, stop=i == NT - 1)
                        last.then_inc(a_full, one(a_full))

                    def weighted_values(a, h):
                        D = a.dim
                        v = v16 if D == 16 else v32
                        if h % HG == 0 and sent(o_full) > 0:
                            e.wait_ge(o_done, sent(o_full))
                        e.wait_ge(a_done, moved(("p", h)))
                        if a.keep_after:
                            e.wait_ge(pm_ready, upcoming(e, pm_ready))
                        pr = prob[:, h % PBUF]
                        c = (h % HG) * (D + 1)
                        for i in range(NT):
                            o = o_bank[i][:, c:c + D + 1]
                            if a.keep_after:
                                mm(o, pr[:, i * P:i * P + P], zero_one[:, :], start=True, stop=False)
                                if i == 0:
                                    mm(o, pr[:, TOK:TOK + P], v[:, 1, h, :], start=False, stop=False)
                                else:
                                    mm(o, pr[:, TOK + P:TOK + 2 * P], zero_one[:, :], start=False, stop=False)
                                last = mm(o_bank[i][:, c:c + D], probm[:, h % MBUF, i, :], v[:, i, h, 0:D],
                                          start=False, stop=True)
                                continue
                            js = [j for j in range(len(a.key_tiles)) if not (a.causal and j > i)]
                            for j in js:
                                n = a.key_tiles[j][1]
                                c1 = j * TOK + i * P - (j * P if a.causal else 0)
                                last = mm(o, pr[0:n, c1:c1 + P], v[0:n, j, h, :], start=j == 0, stop=j == js[-1])
                        if h % HG == HG - 1:
                            last.then_inc(o_full, one(o_full))
                            number[(at[0], at[1], ("o", h // HG))] = sent(o_full) - 1

                    def group_to_features(a, g):
                        e.wait_ge(o_done, number[(at[0], at[1], ("o", g))] + 1)
                        n = a.tiles // GROUPS
                        ps = slot("a", ("oT", g))
                        for f in range(n):
                            for t in range(NT):
                                c = (g * n + f) * P
                                last = nc.tensor.transpose(ps[:, f * TOK + t * P:f * TOK + t * P + P],
                                                           o_tok[:, t, c:c + P], ident[:, :])
                        last.then_inc(a_full, one(a_full))

                    def attend(a, w_out, n_out):
                        e.wait_ge(qk_ready, upcoming(e, qk_ready, 2))
                        e.wait_ge(a_done, moved("v"))
                        for n in range(HEADS + MAX_LAG + PV_LAG):
                            if n < HEADS:
                                row_scores(a, n)
                            if 0 <= n - MAX_LAG < HEADS:
                                exact_scores(a, n - MAX_LAG)
                            h = n - MAX_LAG - PV_LAG
                            if 0 <= h < HEADS:
                                weighted_values(a, h)
                                if h == GROUP0_AT:
                                    group_to_features(a, 0)
                        group_to_features(a, 1)
                        e.wait_ge(a_done, moved(("oT", 1)))
                        token_major(w_out, 0, DM, oT, n_out, token_tiles, "v")

                    for stage in range(7):
                        e.wait_ge(w_ready[stage + 1], w_count[stage + 1])
                        for s in range(STREAMS):
                            at[:] = stage, s
                            if stage == 0:
                                e.wait_ge(x_in, 16 * STREAMS)
                                to_xT(x[s], None)
                                feature_major(w_qkv0, 0, 2, xT, KT, TOK, "q")
                                feature_major(w_qkv0, DM, 2, xT, KT, TOK, "k")
                                values(SPLAT, w_qkv0, 2 * DM, xT, KT)
                                for part in range(2):
                                    e.wait_ge(sq_ready, upcoming(e, sq_ready))
                                    ps = slot("a", ("w", part))
                                    for t in range(KT):
                                        o = ps[:, t * TOK:(t + 1) * TOK]
                                        mm(o, minus2c[:, t], raw[:, 4 * part + t], start=True, stop=False)
                                        last = mm(o, block16[:, :, :].rearrange("p a b -> p (a b)"),
                                                  oT[:, 2 * part + t], start=False, stop=True)
                                    last.then_inc(a_full, one(a_full))
                                attend(SPLAT, w_o0, KT)
                            elif stage == 1:
                                e.wait_ge(c_in, 32 * STREAMS)
                                to_xT(x[s], z_ready)
                                context = cxT[s][:, :].rearrange("p (a n) -> p a n", a=1)
                                w_kv = w_kv1[:, :].rearrange("p (a n) -> p a n", a=1)
                                feature_major(w_q1, 0, 2, xT, KT, TOK, "q")
                                feature_major(w_kv, 0, 2, context, 1, CTX_TOK, "k")
                                values(CROSS0, w_kv, DM, context, 1)
                                attend(CROSS0, w_o1, KT)
                            elif stage == 2:
                                to_xT(x[s], z_ready)
                                token_major(w_router, 0, EXPERTS, xT, KT, token_tiles, "v")
                                e.wait_ge(gm_ready, upcoming(e, gm_ready))
                                ps = slot("a", "gmT")
                                for t in range(NT):
                                    last = nc.tensor.transpose(ps[0:EXPERTS, t * P:t * P + P],
                                                               gm[:, t, 0:EXPERTS], ident[:, :])
                                last.then_inc(a_full, one(a_full))
                                e.wait_ge(a_done, moved("gmT"))
                                ps = slot("v")
                                for t in range(NT):
                                    last = mm(ps[:, t * DM:(t + 1) * DM], gmT[0:EXPERTS, t * P:t * P + P],
                                              b_exp[:, :], start=True, stop=True)
                                last.then_inc(v_full, one(v_full))
                                for n in range(EXPERTS):
                                    token_major(w_exp[:, n], 0, DM, xT, KT, token_tiles, "v")
                            elif stage == 3:
                                to_xT(x[s], z_ready)
                                feature_major(w_qkv2, 0, 2, xT, KT, TOK, "q")
                                feature_major(w_qkv2, DM, 2, xT, KT, TOK, "k")
                                values(CAUSAL, w_qkv2, 2 * DM, xT, KT)
                                attend(CAUSAL, w_o2, KT)
                            elif stage in (4, 5):
                                i = stage - 4
                                a = (SELF1, CROSS1)[i]
                                to_xT(z[s], z_ready)
                                feature_major(w_aq[i], 0, 4, xT, KT, TOK, "q")
                                if i == 0:
                                    feature_major(w_ak[i], 0, 4, yT, KT, TOK, "k")
                                    values(a, w_av[i], 0, yT, KT)
                                else:
                                    e.wait_ge(zc_ready, upcoming(e, zc_ready))
                                    ps = slot("a", "yT")
                                    nc.tensor.transpose(
                                        ps[:, 0:CTX_TOK], o_tok[0:CTX_TOK, 0, 0:CTX_DIM],
                                        ident[0:CTX_TOK, 0:CTX_TOK]).then_inc(a_full, one(a_full))
                                    e.wait_ge(a_done, moved("yT"))
                                    feature_major(w_ak[i], 0, 4, yT, 1, CTX_TOK, "k")
                                    values(a, w_av[i], 0, yT, 1)
                                attend(a, w_li1[i], 4)
                                to_xT(z[s], zo_ready, "xoT")
                                for m in range(HID // P):
                                    ps = slot("a", "hidden")
                                    for k in range(KT):
                                        last = mm(ps[:, 0:TOK], w_li2[i][:, k, m * P:m * P + P], xT[:, k, :],
                                                  start=k == 0, stop=k == KT - 1)
                                    last.then_inc(a_full, one(a_full))
                                e.wait_ge(a_done, moved("hidden"))
                                token_major(w_li3[i], 0, DM, raw, HID // P, token_tiles, "v")
                            else:
                                to_xT(x[s], z_ready)
                                token_major(w_sel, 0, TOP_EXPERTS, xT, KT, token_tiles, "a", "sel")
                                e.wait_ge(gm_ready, upcoming(e, gm_ready))
                                ps = slot("a", "gmT")
                                for t in range(NT):
                                    last = nc.tensor.transpose(ps[0:TOP_EXPERTS, t * P:t * P + P],
                                                               gm[:, t, :], ident[:, :])
                                last.then_inc(a_full, one(a_full))
                                e.wait_ge(a_done, moved("gmT"))
                                for m in range(HID // P):
                                    ps = slot("a", ("relu", m))
                                    for k in range(KT):
                                        last = mm(ps[:, 0:TOK], w_keys[:, k, m * P:m * P + P], xT[:, k, :],
                                                  start=k == 0, stop=k == KT - 1)
                                    last.then_inc(a_full, one(a_full))
                                    ps = slot("v", "mix")
                                    mm(ps[:, 0:TOK], spread[:, m, :], gmT[:, :],
                                                      start=True, stop=True).then_inc(v_full, one(v_full))
                                e.wait_ge(v_done, moved("mix"))
                                token_major(w_vals, 0, DM, raw, HID // P, token_tiles, "v")

                @block.scalar
                def _(e):
                    act = nc.scalar.activation

                    def to_features(ps, dst, gain=None, offset=None):
                        for k in range(KT):
                            src = ps[:, k * TOK:(k + 1) * TOK]
                            if gain is None:
                                last = act(dst[:, k, :], src, ACT.Copy)
                            else:
                                last = act(dst[:, k, :], src, ACT.Identity,
                                           bias=offset[:, k:k + 1], scale=gain[:, k:k + 1])
                        return last

                    def raw_tiles(base, tiles, n_tok, bias=None):
                        for m in range(0, tiles, 2):
                            e.wait_ge(a_full, upcoming(e, a_full))
                            ps = ring_a[bank_of(e, a_full)]
                            for i in range(2):
                                src = ps[:, i * TOK:i * TOK + n_tok]
                                dst = raw[:, base + m + i, 0:n_tok]
                                if bias is None:
                                    last = act(dst, src, ACT.Copy)
                                else:
                                    last = act(dst, src, ACT.Identity, bias=bias[:, m + i:m + i + 1])
                            last.then_inc(a_done, one(a_done))

                    def value_tiles(a):
                        D = a.dim
                        v = v16 if D == 16 else v32
                        if D == 16:
                            e.wait_ge(a_full, upcoming(e, a_full))
                            ps = ring_a[bank_of(e, a_full)]
                            for j, (_, n) in enumerate(a.key_tiles):
                                last = act(v[0:n, j, :, 0:D], ps[0:n, j * 256:(j + 1) * 256].rearrange(
                                    "p (h d) -> p h d", d=D), ACT.Copy)
                            last.then_inc(a_done, one(a_done))
                        else:
                            for j, (_, n) in enumerate(a.key_tiles):
                                e.wait_ge(a_full, upcoming(e, a_full))
                                ps = ring_a[bank_of(e, a_full)]
                                act(v[0:n, j, :, 0:D], ps[0:n, :].rearrange("p (h d) -> p h d", d=D), ACT.Copy).then_inc(a_done, one(a_done))

                    def attend(a, bias=None):
                        def to_oT(g):
                            n = a.tiles // GROUPS
                            e.wait_ge(a_full, upcoming(e, a_full))
                            ps = ring_a[bank_of(e, a_full)]
                            for f in range(n):
                                src = ps[:, f * TOK:(f + 1) * TOK]
                                dst = oT[:, g * n + f, :]
                                if bias is None:
                                    last = act(dst, src, ACT.Copy)
                                else:
                                    last = act(dst, src, ACT.Identity, bias=bias[:, g * n + f:g * n + f + 1])
                            last.then_inc(a_done, one(a_done))

                        for h in range(HEADS):
                            e.wait_ge(a_full, upcoming(e, a_full))
                            ps = ring_a[bank_of(e, a_full)]
                            n = a.key_tiles[0][1]
                            cols = TOK * len(a.key_tiles) - (P if a.causal else 0)
                            act(prob[0:n, h % PBUF, 0:cols], ps[0:n, 0:cols], ACT.Exp, scale=a.scale).then_inc(a_done, one(a_done))
                            if h == GROUP0_AT + PV_LAG:
                                to_oT(0)
                        to_oT(1)

                    for stage in range(7):
                        e.wait_ge(w_ready[stage + 1], w_count[stage + 1])
                        for s in range(STREAMS):
                            if stage in (0, 1, 2, 3, 6):
                                e.wait_ge(a_full, upcoming(e, a_full))
                                to_features(ring_a[bank_of(e, a_full)], xT).then_inc(a_done, one(a_done))
                            if stage == 0:
                                raw_tiles(0, 2, TOK)
                                raw_tiles(4, 2, TOK)
                                value_tiles(SPLAT)
                                for part in range(2):
                                    e.wait_ge(a_full, upcoming(e, a_full))
                                    ps = ring_a[bank_of(e, a_full)]
                                    for t in range(KT):
                                        last = act(raw[:, part * 4 + t, :], ps[:, t * TOK:(t + 1) * TOK], ACT.Exp,
                                                   bias=w_bias[:, t:t + 1], scale=inv_var[:, t:t + 1])
                                    last.then_inc(a_done, one(a_done))
                                attend(SPLAT)
                            elif stage == 1:
                                raw_tiles(0, 2, TOK)
                                raw_tiles(4, 2, CTX_TOK)
                                value_tiles(CROSS0)
                                attend(CROSS0)
                            elif stage == 2:
                                e.wait_ge(nmax_ready, upcoming(e, nmax_ready))
                                for t in range(NT):
                                    last = act(ex[:, t, 0:EXPERTS], lg[:, t, 0:EXPERTS], ACT.Exp,
                                               bias=nmax[:, t:t + 1], accum_out=esum[:, t:t + 1])
                                last.then_inc(exps_ready, one(exps_ready))
                                e.wait_ge(a_full, upcoming(e, a_full))
                                act(gmT[0:EXPERTS, :], ring_a[bank_of(e, a_full)][0:EXPERTS, 0:TOK], ACT.Copy).then_inc(a_done, one(a_done))
                            elif stage == 3:
                                raw_tiles(0, 2, TOK, bq2[:, 0:2])
                                raw_tiles(4, 2, TOK, bq2[:, 2:4])
                                value_tiles(CAUSAL)
                                attend(CAUSAL, bq2[:, 4:6])
                            elif stage in (4, 5):
                                i = stage - 4
                                a = (SELF1, CROSS1)[i]
                                e.wait_ge(a_full, upcoming(e, a_full))
                                ps = ring_a[bank_of(e, a_full)]
                                last = to_features(ps, xT, gx[i], bx[i])
                                if i == 0:
                                    last = to_features(ps, yT, gy[i], by[i])
                                last.then_inc(a_done, one(a_done))
                                raw_tiles(0, 4, TOK)
                                if i == 1:
                                    e.wait_ge(a_full, upcoming(e, a_full))
                                    act(yT[:, 0, 0:CTX_TOK], ring_a[bank_of(e, a_full)][:, 0:CTX_TOK], ACT.Identity,
                                             bias=by[i][:, 0:1], scale=gy[i][:, 0:1]).then_inc(a_done, one(a_done))
                                raw_tiles(4, 4, a.keys)
                                value_tiles(a)
                                attend(a)
                                e.wait_ge(a_full, upcoming(e, a_full))
                                to_features(ring_a[bank_of(e, a_full)], xT, g3[i], b3[i]).then_inc(a_done, one(a_done))
                                for m in range(HID // P):
                                    e.wait_ge(a_full, upcoming(e, a_full))
                                    act(raw[:, m, :], ring_a[bank_of(e, a_full)][:, 0:TOK], ACT.Gelu, bias=b_li2[i][:, m:m + 1]).then_inc(a_done, one(a_done))
                            else:
                                e.wait_ge(a_full, upcoming(e, a_full))
                                act(ex[:, :, :], ring_a[bank_of(e, a_full)][:, 0:NT * TOP_EXPERTS].rearrange(
                                    "p (t n) -> p t n", t=NT), ACT.Exp, scale=-1.0).then_inc(a_done, one(a_done))
                                e.wait_ge(a_full, upcoming(e, a_full))
                                act(gmT[:, :], ring_a[bank_of(e, a_full)][0:TOP_EXPERTS, 0:TOK], ACT.Copy).then_inc(a_done, one(a_done))
                                hr = prob[:, :, :].rearrange("p a (b n) -> p (a b) n", n=TOK)
                                for m in range(HID // P):
                                    e.wait_ge(a_full, upcoming(e, a_full))
                                    act(hr[:, m, :], ring_a[bank_of(e, a_full)][:, 0:TOK], ACT.Relu).then_inc(a_done, one(a_done))

                @block.vector
                def _(e):
                    v = nc.vector

                    def flat(t):
                        return t[:, :, :].rearrange("p t f -> p (t f)")

                    def norm(src, dst, ready=dve_step, n=P, nt=NT):
                        for t in range(nt):
                            v.bn_stats(stats[0:n, t], src[0:n, t, :]).then_inc(dve_step, one(dve_step))
                        e.wait_ge(dve_step, sent(dve_step))
                        for t in range(nt):
                            v.bn_aggr(mv[0:n, t], stats[0:n, t]).then_inc(dve_step, one(dve_step))
                        e.wait_ge(dve_step, sent(dve_step))
                        v.tensor_scalar(veps[0:n, 0:nt], mv[0:n, 0:nt, 1], EPS, None, ALU.add).then_inc(var_ready, one(var_ready))
                        e.wait_ge(rstd_ready, upcoming(e, rstd_ready))
                        for t in range(nt):
                            signal = dve_step if t < nt - 1 else ready
                            v.tensor_scalar(dst[0:n, t, :], src[0:n, t, :], mv[0:n, t, 0:1], rstd[0:n, t:t + 1],
                                            ALU.subtract, ALU.mult).then_inc(signal, one(signal))
                        e.wait_ge(dve_step, sent(dve_step))
                        e.wait_ge(ready, sent(ready))

                    def gain(s, i):
                        for op, row in ((ALU.mult, r_g[i]), (ALU.add, r_b[i])):
                            v.tensor_tensor(xa[s][:, :, :], xa[s][:, :, :],
                                                 row[:, :].rearrange("p (a n) -> p a n", a=1)
                                                 .broadcast_to([P, NT, DM]), op).then_inc(dve_step, one(dve_step))
                            e.wait_ge(dve_step, sent(dve_step))

                    def split(src, hi, lo, scale=None):
                        if scale is None:
                            v.tensor_copy(hi, src).then_inc(dve_step, one(dve_step))
                            e.wait_ge(dve_step, sent(dve_step))
                            return v.tensor_tensor(lo, src, hi.bitcast(F32), ALU.subtract)
                        v.tensor_scalar(hi, src, scale, None, ALU.mult).then_inc(dve_step, one(dve_step))
                        e.wait_ge(dve_step, sent(dve_step))
                        return v.scalar_tensor_tensor(lo, src, scale, hi.bitcast(F32), ALU.mult, ALU.subtract)

                    def split_queries(a):
                        e.wait_ge(a_done, moved(("w", 0) if a.splat else "q"))
                        split(raw[:, 0:a.tiles, :], qh[:, 0:a.tiles, :], ql[:, 0:a.tiles, :]).then_inc(qk_ready, one(qk_ready))

                    def split_keys(a):
                        e.wait_ge(a_done, moved(("w", 1) if a.splat else "k"))
                        n = a.keys
                        src = raw[:, 4:4 + a.tiles, 0:n]
                        if a.dim == 32:
                            last = split(src, kh[:, :, 0:n], kl[:, :, 0:n])
                        else:
                            for o in range(2):
                                if a.splat:
                                    for t in range(KT):
                                        last = split(raw[:, 4 + t, 0:n], kh[:, 2 * o + t, 0:n],
                                                     kl[:, 2 * o + t, 0:n], k_scale[:, o, t:t + 1])
                                else:
                                    last = split(src, kh[:, 2 * o:2 * o + 2, 0:n], kl[:, 2 * o:2 * o + 2, 0:n],
                                                 parity[:, o:o + 1])
                        last.then_inc(qk_ready, one(qk_ready))

                    def attend(a):
                        D = a.dim

                        def normalise(g):
                            e.wait_ge(o_full, upcoming(e, o_full))
                            views = [o_bank[i][:, 0:HG * (D + 1)].rearrange("p (h d) -> p h d", d=D + 1)
                                     for i in range(NT)]
                            for i, o in enumerate(views):
                                v.reciprocal(recip[:, i], o[:, :, D]).then_inc(dve_step, one(dve_step))
                                e.wait_ge(dve_step, sent(dve_step))
                            for i, o in enumerate(views):
                                dst = o_tok[:, i, g * HG * D:(g + 1) * HG * D].rearrange("p (h d) -> p h d", d=D)
                                last = v.tensor_tensor(dst, o[:, :, 0:D], recip[:, i].rearrange(
                                    "p (h a) -> p h a", a=1).broadcast_to([P, HG, D]), ALU.mult)
                            last.then_inc(o_done, one(o_done))

                        for h in range(HEADS):
                            e.wait_ge(v_full, upcoming(e, v_full))
                            ps = ring_v[bank_of(e, v_full)]
                            v.tensor_reduce(
                                negm[:, h * NT:(h + 1) * NT],
                                ps[:, :].rearrange("p (t n) -> p t n", t=NT)[:, :, 0:a.keys],
                                AX.X, ALU.max, negate=True).then_inc(v_done, one(v_done))
                            if h == HG - 1 + MAX_LAG + PV_LAG:
                                normalise(0)
                        normalise(1)

                    def add_bank(dst, other):
                        e.wait_ge(v_full, upcoming(e, v_full))
                        v.tensor_tensor(flat(dst), ring_v[bank_of(e, v_full)][:, :], flat(other), ALU.add).then_inc(v_done, one(v_done))
                        e.wait_ge(v_done, sent(v_done))

                    for stage in range(7):
                        e.wait_ge(w_ready[stage + 1], w_count[stage + 1])
                        for s in range(STREAMS):
                            at[:] = stage, s
                            if stage == 0:
                                for part, what in enumerate(("q", "k")):
                                    e.wait_ge(a_done, moved(what))
                                    v.tensor_tensor(
                                        oT[:, 2 * part:2 * part + 2, :], raw[:, 4 * part:4 * part + 2, :],
                                        raw[:, 4 * part:4 * part + 2, :], ALU.mult).then_inc(sq_ready, one(sq_ready))
                                split_queries(SPLAT)
                                split_keys(SPLAT)
                                attend(SPLAT)
                                add_bank(x[s], x[s])
                                norm(x[s], x[s], z_ready)
                            elif stage == 1:
                                split_queries(CROSS0)
                                split_keys(CROSS0)
                                attend(CROSS0)
                                add_bank(x[s], x[s])
                                norm(x[s], x[s], z_ready)
                            elif stage == 2:
                                e.wait_ge(v_full, upcoming(e, v_full))
                                v.tensor_tensor(
                                    lg[:, :, 0:EXPERTS], ring_v[bank_of(e, v_full)][:, 0:NT * EXPERTS].rearrange("p (t n) -> p t n", t=NT),
                                    r_router[:, :].rearrange("p (a n) -> p a n", a=1).broadcast_to([P, NT, EXPERTS]),
                                    ALU.add).then_inc(v_done, one(v_done))
                                e.wait_ge(v_done, sent(v_done))
                                for t in range(NT):
                                    v.max(top8[:, t], lg[:, t, 0:EXPERTS]).then_inc(dve_step, one(dve_step))
                                    e.wait_ge(dve_step, sent(dve_step))
                                v.tensor_copy(lgv[:, :, 0:1], top8[:, :, 0:1]).then_inc(dve_step, one(dve_step))
                                e.wait_ge(dve_step, sent(dve_step))
                                v.tensor_scalar(nmax[:, :], top8[:, :, 0], -1.0, None, ALU.mult).then_inc(nmax_ready, one(nmax_ready))
                                for t in range(NT):
                                    v.match_replace(mr[:, t, 0:16], lgv[:, t], lg[:, t], MARK).then_inc(dve_step, one(dve_step))
                                    e.wait_ge(dve_step, sent(dve_step))
                                v.tensor_scalar(gm[:, :, 0:EXPERTS], mr[:, :, 0:EXPERTS], MARK, None, ALU.is_equal).then_inc(dve_step, one(dve_step))
                                e.wait_ge(dve_step, sent(dve_step))
                                e.wait_ge(exps_ready, upcoming(e, exps_ready))
                                v.reciprocal(gate[:, :], esum[:, :]).then_inc(dve_step, one(dve_step))
                                e.wait_ge(dve_step, sent(dve_step))
                                for t in range(NT):
                                    signal = dve_step if t < NT - 1 else gm_ready
                                    v.tensor_scalar(gm[:, t, 0:EXPERTS], gm[:, t, 0:EXPERTS], gate[:, t:t + 1],
                                                         None, ALU.mult).then_inc(signal, one(signal))
                                    e.wait_ge(signal, sent(signal))
                                add_bank(x[s], x[s])
                                for n in range(EXPERTS):
                                    e.wait_ge(v_full, upcoming(e, v_full))
                                    ps = ring_v[bank_of(e, v_full)]
                                    for t in range(NT):
                                        signal = dve_step if t < NT - 1 else v_done
                                        v.scalar_tensor_tensor(x[s][:, t, :], ps[:, t * DM:(t + 1) * DM],
                                                                    gm[:, t, n:n + 1], x[s][:, t, :],
                                                                    ALU.mult, ALU.add).then_inc(signal, one(signal))
                                        e.wait_ge(signal, sent(signal))
                                norm(x[s], x[s], z_ready)
                            elif stage == 3:
                                split_queries(CAUSAL)
                                split_keys(CAUSAL)
                                attend(CAUSAL)
                                e.wait_ge(xo_ready, upcoming(e, xo_ready))
                                add_bank(x[s], xo[s])
                                norm(x[s], x[s])
                                norm(x[s], xa[s])
                                gain(s, 0)
                                norm(xa[s], z[s], z_ready)
                            elif stage in (4, 5):
                                i = stage - 4
                                a = (SELF1, CROSS1)[i]
                                split_queries(a)
                                if i == 1:
                                    norm(cx[s][:, :].rearrange("p (a f) -> p a f", a=1),
                                         o_tok[:, 0:1, 0:CTX_DIM], zc_ready, n=CTX_TOK, nt=1)
                                split_keys(a)
                                attend(a)
                                e.wait_ge(xo_ready, upcoming(e, xo_ready))
                                add_bank(xo[s], xo[s])
                                norm(xo[s], z[s], zo_ready)
                                e.wait_ge(xa_ready, upcoming(e, xa_ready, 2))
                                add_bank(xa[s], xa[s])
                                if i == 0:
                                    norm(xa[s], xa[s])
                                    gain(s, 1)
                                    norm(xa[s], z[s], z_ready)
                                else:
                                    v.tensor_tensor(flat(x[s]), flat(x[s]), flat(xa[s]), ALU.add).then_inc(dve_step, one(dve_step))
                                    e.wait_ge(dve_step, sent(dve_step))
                                    norm(x[s], x[s], z_ready)
                            else:
                                e.wait_ge(a_done, moved("sel"))
                                v.tensor_scalar(ex[:, :, :], ex[:, :, :], 1.0, None, ALU.add).then_inc(dve_step, one(dve_step))
                                e.wait_ge(dve_step, sent(dve_step))
                                v.reciprocal(pe16[:, :, 0:16], ex[:, :, :]).then_inc(dve_step, one(dve_step))
                                e.wait_ge(dve_step, sent(dve_step))
                                for t in range(NT):
                                    v.max(top8[:, t], pe16[:, t, 0:16]).then_inc(dve_step, one(dve_step))
                                    e.wait_ge(dve_step, sent(dve_step))
                                v.tensor_copy(pv[:, :, 0:TOP_K], top8[:, :, 0:TOP_K]).then_inc(dve_step, one(dve_step))
                                e.wait_ge(dve_step, sent(dve_step))
                                for t in range(NT):
                                    v.match_replace(mr[:, t], pv[:, t], pe16[:, t], 2.0).then_inc(dve_step, one(dve_step))
                                    e.wait_ge(dve_step, sent(dve_step))
                                v.tensor_reduce(gate[:, :], top8[:, :, 0:TOP_K], AX.X, ALU.add).then_inc(dve_step, one(dve_step))
                                e.wait_ge(dve_step, sent(dve_step))
                                v.tensor_scalar(gate[:, :], gate[:, :], 1e-9, None, ALU.max).then_inc(dve_step, one(dve_step))
                                e.wait_ge(dve_step, sent(dve_step))
                                v.reciprocal(gate[:, :], gate[:, :]).then_inc(dve_step, one(dve_step))
                                e.wait_ge(dve_step, sent(dve_step))
                                v.tensor_scalar(gate[:, :], gate[:, :], r_route[:, 0:1], None, ALU.mult).then_inc(dve_step, one(dve_step))
                                e.wait_ge(dve_step, sent(dve_step))
                                v.scalar_tensor_tensor(gm[:, :, :], mr[:, :, 0:16], 2.0, pe16[:, :, 0:16],
                                                            ALU.is_equal, ALU.mult).then_inc(dve_step, one(dve_step))
                                e.wait_ge(dve_step, sent(dve_step))
                                for t in range(NT):
                                    signal = dve_step if t < NT - 1 else gm_ready
                                    v.tensor_scalar(gm[:, t, :], gm[:, t, :], gate[:, t:t + 1], None, ALU.mult).then_inc(signal, one(signal))
                                    e.wait_ge(signal, sent(signal))
                                hr = prob[:, :, :].rearrange("p a (b n) -> p (a b) n", n=TOK)
                                for m in range(HID // P):
                                    e.wait_ge(a_done, moved(("relu", m)))
                                    e.wait_ge(v_full, upcoming(e, v_full))
                                    v.tensor_tensor(raw[:, m, :], ring_v[bank_of(e, v_full)][:, 0:TOK], hr[:, m, :],
                                                                   ALU.mult).then_inc(v_done, one(v_done))
                                add_bank(x[s], x[s])
                                norm(x[s], x[s], out_ready)

                @block.gpsimd
                def _(e):
                    g = nc.gpsimd

                    def root(n=P, nt=NT):
                        e.wait_ge(var_ready, upcoming(e, var_ready))
                        g.tensor_tensor(rstd[0:n, 0:nt], veps[0:n, 0:nt],
                                                           minus_half[0:n, 0:nt], ALU.pow).then_inc(rstd_ready, one(rstd_ready))

                    def add_row(dst, src, row):
                        return g.tensor_tensor(dst[:, :, :], src[:, :, :],
                                               row[:, :].rearrange("p (a n) -> p a n", a=1)
                                               .broadcast_to([P, NT, DM]), ALU.add)

                    for stage in range(7):
                        e.wait_ge(w_ready[stage + 1], w_count[stage + 1])
                        for s in range(STREAMS):
                            if stage in (3, 4, 5):
                                e.wait_ge(z_ready, (stage - 1) * STREAMS + s + 1)
                                if stage == 3:
                                    last = add_row(xo[s], x[s], r_bo2)
                                else:
                                    last = add_row(xo[s], xa[s], r_li1[stage - 4])
                                last.then_inc(xo_ready, one(xo_ready))
                            if stage == 5:
                                root(CTX_TOK, 1)
                            if stage == 4:
                                for h in range(HEADS):
                                    e.wait_ge(a_done, number[(stage, s, ("p", h))] + 1)
                                    for t in range(NT):
                                        c = t * TOK + t * P
                                        last = g.affine_select(out=probm[:, h % MBUF, t, :],
                                                               in_=prob[:, h % PBUF, c:c + P],
                                                               compare_op=ALU.is_gt, fill=0.0, base=0,
                                                               pattern=[[-1, P]], channel_multiplier=1)
                                    last.then_inc(pm_ready, one(pm_ready))
                            root()
                            if stage == 3:
                                root()
                                root()
                            if stage in (4, 5):
                                e.wait_ge(zo_ready, (stage - 4) * STREAMS + s + 1)
                                g.tensor_tensor(xa[s][:, :, :], xa[s][:, :, :], xo[s][:, :, :],
                                                                 ALU.add).then_inc(xa_ready, one(xa_ready))
                                e.wait_ge(xa_ready, sent(xa_ready))
                                add_row(xa[s], xa[s], r_li3[stage - 4]).then_inc(xa_ready, one(xa_ready))
                                root()
                                if stage == 4:
                                    root()

            nc.gpsimd.sem_clear(loop_sems)
            nc.all_engine_barrier()


def laid_out(i):
    import numpy as np

    def np_(name):
        return np.asarray(i[name])

    def per_head(name):
        w = np_(name)
        return w.transpose(1, 0, 2).reshape(w.shape[1], -1)

    d = {
        "x": np_("x"),
        "ctx": np_("ctx_512"),
        "ctx_t": np_("ctx_512").transpose(0, 2, 1),
        "centers": np_("L0_attn_splat_centers").reshape(DM, 16),
        "centers_t": np_("L0_attn_splat_centers").transpose(0, 2, 1).reshape(DM, 16),
        "deltas": np_("L0_attn_splat_deltas").reshape(DM, 16),
        "deltas_t": np_("L0_attn_splat_deltas").transpose(0, 2, 1).reshape(DM, 16),
        "log_scales": np_("L0_attn_splat_log_scales").reshape(-1),
        "log_amps": np_("L0_attn_splat_log_amplitudes").reshape(-1),
        "movement": np_("L0_attn_movement_scale").reshape(1),
        "temperature": np_("L0_attn_temperature").reshape(1),
        "qkv0": np_("L0_attn_qkv_w").T,
        "o0": np_("L0_attn_out_w").T,
        "q1": np_("L0_xattn_Wq").T,
        "kv1": np_("L0_xattn_Wkv").T,
        "o1": np_("L0_xattn_Wo").T,
        "router": np_("L0_ffn_router_w"),
        "router_b": np_("L0_ffn_router_b"),
        "expert_w": np_("L0_ffn_expert_w"),
        "expert_b": np_("L0_ffn_expert_b"),
        "qkv2": np_("L1_attn_w_qkv"),
        "bqkv2": np_("L1_attn_b_qkv"),
        "o2": np_("L1_attn_w_out"),
        "bo2": np_("L1_attn_b_out"),
        "sel": np_("L1_ffn_expert_sel").T,
        "keys": per_head("L1_ffn_keys"),
        "values": np_("L1_ffn_values").reshape(HID, DM),
        "route": np_("L1_ffn_route_scale"),
    }
    for a in range(2):
        pre = f"L1_xattn_a{a + 1}_"
        d[f"ln_g{a}"] = np_(f"L1_xattn_ln{a + 1}_g")
        d[f"ln_b{a}"] = np_(f"L1_xattn_ln{a + 1}_b")
        for w in ("wq", "wk", "wv"):
            d[f"{w}{a}"] = per_head(pre + w)
        for w in ("li1", "li2", "li3"):
            d[f"{w}_{a}"] = np_(f"{pre}{w}_w")
            d[f"{w}_b{a}"] = np_(f"{pre}{w}_b")
        for w in ("lnx", "lny", "ln3"):
            d[f"{w}_g{a}"] = np_(f"{pre}{w}_g")
            d[f"{w}_b{a}"] = np_(f"{pre}{w}_b")
    for name in ["log_scales", "log_amps", "bqkv2"] + [
            f"{n}{a}" for n in ("lnx_g", "lnx_b", "lny_g", "lny_b", "ln3_g", "ln3_b", "li2_b") for a in range(2)]:
        d[name] = d[name].reshape(-1, P).T
    return {k: np.ascontiguousarray(v) for k, v in d.items()}


def kernel(**inputs):
    import concourse.bacc as _bacc
    from concourse import mybir as _mybir
    from concourse.bass_utils import run_bass_kernel_spmd as _run

    nc = _bacc.Bacc("TRN2", target_bir_lowering=False, num_devices=1)
    data = laid_out(inputs)
    arrays = {f"in_{name}": a for name, a in data.items()}
    io = {name: nc.dram_tensor(f"in_{name}", a.shape, _mybir.dt.from_np(a.dtype), kind="ExternalInput").ap()
          for name, a in data.items()}
    out = nc.dram_tensor("out_0", (BATCH, TOK, DM), _mybir.dt.float32, kind="ExternalOutput").ap()
    decoder(nc, io, out)
    r = _run(nc, [arrays], core_ids=[0])
    return r.results[0]["out_0"]
```

```python
from contextlib import ExitStack

import concourse.bass as bass
from concourse import mybir

F32 = mybir.dt.float32
F16 = mybir.dt.float16
BF16 = mybir.dt.bfloat16
ALU = mybir.AluOpType
ACT = mybir.ActivationFunctionType
AX = mybir.AxisListType

P = 128
BATCH, TOK, DM, CTX_TOK, CTX_DIM = 16, 256, 256, 120, 128
STREAMS = 2
HEADS = 16
NT = TOK // P
KT = DM // P
GROUPS = 2
HG = HEADS // GROUPS
EPS = 1e-5
EXPERTS, TOP_EXPERTS, TOP_DIM, TOP_K = 8, 16, 64, 4
HID = 1024
NEG = -1.0e30
LOW, MARK = -3.0e38, 3.0e38
RING = 3
PBUF = 4
MBUF = 4
GROUP0_AT = 9
W_SCALE = 64.0
P_LOG = 4.1588830833596715
PARTS = ((0, 0), (1, 0), (0, 1))
STAGING = 8
LOW_LAG = 3
MAX_LAG, PV_LAG = 2, 3


class Attn:

    def __init__(self, name, dim, keys, scale, causal=False, keep_after=False, splat=False):
        self.name, self.dim, self.keys, self.scale = name, dim, keys, scale
        self.causal, self.keep_after, self.splat = causal, keep_after, splat
        self.tiles = HEADS * dim // P
        self.key_tiles = [(0, min(keys, P))] + ([(P, keys - P)] if keys > P else [])

    def at(self, h):
        if self.dim == 32:
            return h // 4, 32 * (h % 4), h // 4
        return h // 8, 32 * ((h % 8) // 2), 2 * (h % 2) + h // 8


ATTNS = [
    Attn("splat", 16, TOK, 1.0, splat=True),
    Attn("cross0", 16, CTX_TOK, 0.25),
    Attn("causal", 16, TOK, 0.25, causal=True),
    Attn("self1", 32, TOK, 32 ** -0.5, keep_after=True),
    Attn("cross1", 32, CTX_TOK, 32 ** -0.5),
]
SPLAT, CROSS0, CAUSAL, SELF1, CROSS1 = ATTNS


class Counts:

    def __init__(self):
        self.increments, self.awaited = {}, {}

    def one(self, sem):
        self.increments[sem.num] = self.increments.get(sem.num, 0) + 1
        return 1

    def sent(self, sem):
        return self.increments.get(sem.num, 0)

    def upcoming(self, engine, sem, n=1):
        key = (str(engine.engine), sem.num)
        self.awaited[key] = self.awaited.get(key, 0) + n
        return self.awaited[key]

    def bank_of(self, engine, full):
        return (self.awaited[(str(engine.engine), full.num)] - 1) % RING


def decoder(nc, io, out):
    with ExitStack() as ctx:
        def sb(name, shape, dt=F32):
            return ctx.enter_context(nc.sbuf_tensor(name, shape, dt))

        def semaphore(name):
            return ctx.enter_context(nc.semaphore(name))

        def pair(name, tiles, n, partitions=P):
            return sb(name, [partitions, 2, tiles, n], F16)

        w_qkv0 = pair("w_qkv0", KT, 3 * DM)
        w_o0 = pair("w_o0", KT, DM)
        w_q1 = pair("w_q1", KT, DM)
        w_kv1 = pair("w_kv1", 1, 2 * DM)
        w_o1 = pair("w_o1", KT, DM)
        w_router = pair("w_router", KT, EXPERTS)
        w_exp = pair("w_exp", EXPERTS * KT, DM)
        b_exp = sb("b_exp", [EXPERTS, DM])
        w_qkv2 = pair("w_qkv2", KT, 3 * DM)
        w_o2 = pair("w_o2", KT, DM)
        bq2 = sb("bq2", [P, 6])
        w_aq = [pair(f"w_aq{a}", KT, 512) for a in range(2)]
        w_ak = [pair("w_ak0", KT, 512), pair("w_ak1", 1, 512)]
        w_av = [pair("w_av0", KT, 512), pair("w_av1", 1, 512)]
        w_li1 = [pair(f"w_li1_{a}", 4, DM) for a in range(2)]
        w_li2 = [pair(f"w_li2_{a}", KT, HID) for a in range(2)]
        w_li3 = [pair(f"w_li3_{a}", HID // P, DM) for a in range(2)]
        b_li2 = [sb(f"b_li2_{a}", [P, HID // P]) for a in range(2)]
        gx = [sb(f"gx{a}", [P, KT]) for a in range(2)]
        bx = [sb(f"bx{a}", [P, KT]) for a in range(2)]
        gy = [sb("gy0", [P, KT]), sb("gy1", [P, 1])]
        by = [sb("by0", [P, KT]), sb("by1", [P, 1])]
        g3 = [sb(f"g3{a}", [P, KT]) for a in range(2)]
        b3 = [sb(f"b3{a}", [P, KT]) for a in range(2)]
        w_sel = pair("w_sel", KT, TOP_EXPERTS)
        w_keys = pair("w_keys", KT, HID)
        w_vals = pair("w_vals", HID // P, DM)
        r_bo2 = sb("r_bo2", [P, DM])
        r_li1 = [sb(f"r_li1_{a}", [P, DM]) for a in range(2)]
        r_li3 = [sb(f"r_li3_{a}", [P, DM]) for a in range(2)]
        r_g = [sb(f"r_g{a}", [P, DM]) for a in range(2)]
        r_b = [sb(f"r_b{a}", [P, DM]) for a in range(2)]
        r_router = sb("r_router", [P, EXPERTS])
        r_route = sb("r_route", [P, 1])

        ident = sb("ident", [P, P])
        ident_h = sb("ident_h", [P, P], F16)
        mask_q = sb("mask_q", [P, NT, TOK], BF16)
        mask_k = sb("mask_k", [P, P], BF16)
        block16 = sb("block16", [P, 8, 16])
        minus2c = sb("minus2c", [P, KT, P])
        parity = sb("parity", [P, 2])
        spread = sb("spread", [TOP_EXPERTS, HID // P, P])
        zero_one = sb("zero_one", [P, 33], F16)
        inv_var = sb("inv_var", [P, KT])
        w_bias = sb("w_bias", [P, KT])
        k_scale = sb("k_scale", [P, 2, KT])
        s_small = sb("s_small", [P, 16])
        cen = sb("cen", [P, 2, KT, 16])
        dlt = sb("dlt", [P, 2, KT, 16])
        minus_half = sb("minus_half", [P, NT])
        p_log = sb("p_log", [P, 1])

        x = [sb(f"x{s}", [P, NT, DM]) for s in range(STREAMS)]
        xa = [sb(f"xa{s}", [P, NT, DM]) for s in range(STREAMS)]
        xo = [sb(f"xo{s}", [P, NT, DM]) for s in range(STREAMS)]
        z = [sb(f"z{s}", [P, NT, DM]) for s in range(STREAMS)]
        cx = [sb(f"cx{s}", [P, CTX_DIM]) for s in range(STREAMS)]
        cxT = [sb(f"cxT{s}", [P, CTX_TOK]) for s in range(STREAMS)]
        xT = pair("xT", KT, TOK)
        yT = pair("yT", KT, TOK)
        raw = sb("raw", [P, 8, TOK])
        q = pair("q", 4, TOK)
        k = pair("k", 4, TOK)
        v16 = pair("v16", NT * HEADS, 17)
        v32 = pair("v32", NT * HEADS, 33)
        o_tok = sb("o_tok", [P, NT, 512])
        oT = pair("oT", 4, TOK)
        p32 = sb("p32", [P, PBUF, NT * TOK])
        prob = sb("prob", [P, 2, PBUF, NT * TOK], F16)
        probm = sb("probm", [P, 2, MBUF, NT, P], F16)
        squares = p32[:, 0:2, :].rearrange("p a (b n) -> p (a b) n", n=TOK)
        relus = p32[:, :, :].rearrange("p a (b n) -> p (a b) n", n=TOK)
        hidT = prob[:, :, :, :].rearrange("p c a (b n) -> p c (a b) n", n=TOK)
        negm = sb("negm", [P, HEADS * NT], F16)
        recip = sb("recip", [P, NT, HG])
        stats = sb("stats", [P, NT, 6])
        mv = sb("mv", [P, NT, 2])
        veps = sb("veps", [P, NT])
        rstd = sb("rstd", [P, NT])
        lg = sb("lg", [P, NT, 16])
        lgv = sb("lgv", [P, NT, 8])
        top8 = sb("top8", [P, NT, 8])
        mr = sb("mr", [P, NT, 24])
        nmax = sb("nmax", [P, NT])
        esum = sb("esum", [P, NT])
        ex = sb("ex", [P, NT, 16])
        gate = sb("gate", [P, NT])
        gm = sb("gm", [P, NT, 16])
        gmw = sb("gmw", [P, NT, EXPERTS])
        gmT = sb("gmT", [16, TOK])
        pe16 = sb("pe16", [P, NT, 24])
        pv = sb("pv", [P, NT, 8])

        bank = [ctx.enter_context(nc.psum_tensor(f"bank{i}", [P, 512], F32)) for i in range(8)]

        ring_a, ring_v, o_bank = bank[0:3], bank[3:6], bank[6:8]

        w_ready = [semaphore("setup_loaded"), semaphore("rows_loaded")]
        w_count = [0] * 2
        staged = [semaphore(f"staged{b}") for b in range(STAGING)]
        high_made = semaphore("high_made")
        low_made = semaphore("low_made")
        s_const = semaphore("s_const")
        first = semaphore("first_of_loop")
        a_full, v_full, o_full = semaphore("a_full"), semaphore("v_full"), semaphore("o_full")
        a_done, v_done, o_done = semaphore("a_done"), semaphore("v_done"), semaphore("o_done")
        x_in, c_in = semaphore("x_in"), semaphore("c_in")
        sq_ready = semaphore("sq_ready")
        xs_ready = semaphore("xs_ready")
        qk_ready = semaphore("qk_ready")
        vs_ready = semaphore("vs_ready")
        ps_ready = semaphore("ps_ready")
        os_ready = semaphore("os_ready")
        hs_ready = semaphore("hs_ready")
        pm_ready = semaphore("pm_ready")
        z_ready = semaphore("z_ready")
        zo_ready = semaphore("zo_ready")
        zc_ready = semaphore("zc_ready")
        var_ready = semaphore("var_ready")
        rstd_ready = semaphore("rstd_ready")
        nmax_ready = semaphore("nmax_ready")
        exps_ready = semaphore("exps_ready")
        gm_ready = semaphore("gm_ready")
        xo_ready, xa_ready = semaphore("xo_ready"), semaphore("xa_ready")
        dve_step = semaphore("dve_step")
        out_ready, out_done = semaphore("out_ready"), semaphore("out_done")
        last_sem = semaphore("last_of_loop")
        loop_sems = range(first.num, last_sem.num + 1)
        counts = Counts()
        one, sent, upcoming, bank_of = counts.one, counts.sent, counts.upcoming, counts.bank_of

        def load(e, i, dst, src):
            e.dma_start(dst, src).then_inc(w_ready[i], 16)
            w_count[i] += 16

        def rows(ap, kt):
            return ap.rearrange("(t p) n -> p t n", p=P) if kt > 1 else ap

        def spread_row(ap):
            return ap.rearrange("(a n) -> a n", a=1).broadcast_to([P, ap.shape[0]])

        buffers = [t[s] for t in (x, xa, xo, z) for s in range(STREAMS)]

        def staging(n, tiles, cols):
            flat = buffers[n % STAGING][:, :, :].rearrange("p a b -> p (a b)")
            return flat[:, 0:tiles * cols].rearrange("p (a b) -> p a b", b=cols)

        chunks = []

        def add_weight(w, src, first=0):
            tiles, n = src.shape[0] // P, src.shape[1]
            view = src.rearrange("(t p) n -> p t n", p=P)
            step_t, step_n = max(1, 512 // n), min(n, 512)
            for t in range(0, tiles, step_t):
                nt = min(step_t, tiles - t)
                for c in range(0, n, step_n):
                    m = min(step_n, n - c)
                    chunks.append((w[:, :, first + t:first + t + nt, c:c + m], view[:, t:t + nt, c:c + m], nt, m))

        for w, name in ((w_qkv0, "qkv0"), (w_o0, "o0"), (w_q1, "q1"), (w_kv1, "kv1"), (w_o1, "o1"),
                        (w_router, "router")):
            add_weight(w, io[name])
        for n in range(EXPERTS):
            add_weight(w_exp, io["expert_w"][n], n * KT)
        for w, name in ((w_qkv2, "qkv2"), (w_o2, "o2")):
            add_weight(w, io[name])
        for a in range(2):
            for w, name in ((w_aq, f"wq{a}"), (w_ak, f"wk{a}"), (w_av, f"wv{a}"), (w_li1, f"li1_{a}"),
                            (w_li2, f"li2_{a}"), (w_li3, f"li3_{a}")):
                add_weight(w[a], io[name])
        for w, name in ((w_sel, "sel"), (w_keys, "keys"), (w_vals, "values")):
            add_weight(w, io[name])
        with nc.Block() as block:
            @block.sync
            def _(e):
                load(e, 0, cen[:, 0], io["centers"].rearrange("(t p) d -> p t d", p=P))
                load(e, 0, cen[:, 1], io["centers_t"].rearrange("(t p) d -> p t d", p=P))
                load(e, 0, dlt[:, 0], io["deltas"].rearrange("(t p) d -> p t d", p=P))
                load(e, 0, dlt[:, 1], io["deltas_t"].rearrange("(t p) d -> p t d", p=P))
                load(e, 0, s_small[:, 0:2], io["log_scales"])
                load(e, 0, s_small[:, 2:4], io["log_amps"])
                load(e, 0, s_small[:, 4:5], spread_row(io["movement"]))
                load(e, 0, s_small[:, 5:6], spread_row(io["temperature"]))
                load(e, 1, b_exp[:, :], io["expert_b"])
                load(e, 1, r_router[:, :], spread_row(io["router_b"]))
                load(e, 1, bq2[:, :], io["bqkv2"])
                load(e, 1, r_bo2[:, :], spread_row(io["bo2"]))
                load(e, 1, r_route[:, :], spread_row(io["route"]))
                for a in range(2):
                    for dst, src in ((gx, "lnx_g"), (bx, "lnx_b"), (gy, "lny_g"), (by, "lny_b"),
                                     (g3, "ln3_g"), (b3, "ln3_b"), (b_li2, "li2_b")):
                        load(e, 1, dst[a][:, :], io[f"{src}{a}"])
                    for dst, src in ((r_li1, "li1_b"), (r_li3, "li3_b"), (r_g, "ln_g"), (r_b, "ln_b")):
                        load(e, 1, dst[a][:, :], spread_row(io[f"{src}{a}"]))
                for n, (_, src, tiles, cols) in enumerate(chunks):
                    if n >= STAGING:
                        e.wait_ge(low_made, n + 1 - STAGING)
                    e.dma_start(staging(n, tiles, cols), src).then_inc(staged[n % STAGING], 16)
                e.wait_ge(w_ready[0], w_count[0])
                e.wait_ge(w_ready[1], w_count[1])

            @block.gpsimd
            def _(e):
                g = nc.gpsimd
                made = [0]

                def step(instruction):
                    made[0] += 1
                    instruction.then_inc(s_const, 1)
                    e.wait_ge(s_const, made[0])

                for t in (ident, ident_h, mask_k, mask_q):
                    step(g.memset(t[:], 0.0))
                for t in (block16, spread, minus_half, zero_one):
                    step(g.memset(t[:], 1.0))
                for t in (ident, ident_h):
                    step(g.affine_select(out=t[:, :], in_=t[:, :], compare_op=ALU.not_equal, fill=1.0,
                                         base=0, pattern=[[-1, P]], channel_multiplier=1))
                step(g.affine_select(out=mask_k[:, :], in_=mask_k[:, :], compare_op=ALU.is_ge, fill=NEG,
                                     base=0, pattern=[[1, P]], channel_multiplier=-1))
                step(g.affine_select(out=mask_q[:, :, :], in_=mask_q[:, :, :], compare_op=ALU.is_ge, fill=NEG,
                                     base=0, pattern=[[P, NT], [-1, TOK]], channel_multiplier=1))
                step(g.affine_select(out=block16[:, :, :], in_=block16[:, :, :], compare_op=ALU.is_ge, fill=0.0,
                                     base=0, pattern=[[-16, 8], [0, 16]], channel_multiplier=1))
                step(g.affine_select(out=block16[:, :, :], in_=block16[:, :, :], compare_op=ALU.is_ge, fill=0.0,
                                     base=15, pattern=[[16, 8], [0, 16]], channel_multiplier=-1))
                step(g.affine_select(out=spread[:, :, :], in_=spread[:, :, :], compare_op=ALU.is_ge, fill=0.0,
                                     base=0, pattern=[[P, HID // P], [1, P]], channel_multiplier=-TOP_DIM))
                step(g.affine_select(out=spread[:, :, :], in_=spread[:, :, :], compare_op=ALU.is_ge, fill=0.0,
                                     base=TOP_DIM - 1, pattern=[[-P, HID // P], [-1, P]],
                                     channel_multiplier=TOP_DIM))
                step(g.memset(zero_one[:, 0:32], 0.0))
                step(g.memset(minus_half[:, :], -0.5))
                step(g.memset(p_log[:, :], P_LOG))
                for part in range(2):
                    step(g.memset(v16[:, part, :, 16:17], 1.0 - part))
                    step(g.memset(v32[:, part, :, 32:33], 1.0 - part))
                step(g.memset(lg[:, :, 8:16], LOW))
                step(g.memset(lgv[:, :, :], LOW))
                step(g.memset(pe16[:, :, 16:24], -1.0))
                step(g.memset(pv[:, :, :], -1.0))
                step(g.memset(gm[:, :, :], 0.0))
            n_const = len("ident ident_h mask_k mask_q".split()) + 4 + 2 + 6

            s_act = semaphore("s_act")
            s_dv = semaphore("s_dv")

            @block.scalar
            def _(e):
                e.wait_ge(w_ready[0], w_count[0])
                nc.scalar.activation(s_small[:, 6:10], s_small[:, 0:4], ACT.Exp).then_inc(s_act, 1)
                nc.scalar.activation(s_small[:, 10:11], s_small[:, 4:5], ACT.Exp, scale=-1.0).then_inc(s_act, 1)
                for n, (parts, _, tiles, cols) in enumerate(chunks):
                    e.wait_ge(staged[n % STAGING], 16 * (n // STAGING + 1))
                    nc.scalar.activation(parts[:, 0], staging(n, tiles, cols), ACT.Copy, scale=W_SCALE
                                         ).then_inc(high_made, 1)

            @block.vector
            def _(e):
                v = nc.vector
                made = [0]

                def step(instruction):
                    made[0] += 1
                    instruction.then_inc(s_dv, 1)
                    e.wait_ge(s_dv, made[0])

                e.wait_ge(s_const, n_const)
                e.wait_ge(w_ready[0], w_count[0])
                e.wait_ge(s_act, 2)
                step(v.tensor_scalar(s_small[:, 6:8], s_small[:, 6:8], 0.01, 2.0, ALU.max, ALU.min))
                step(v.tensor_scalar(s_small[:, 8:10], s_small[:, 8:10], 1e-6, 10.0, ALU.max, ALU.min))
                step(v.tensor_tensor(s_small[:, 6:8], s_small[:, 6:8], s_small[:, 6:8], ALU.mult))
                step(v.tensor_scalar(s_small[:, 6:8], s_small[:, 6:8], 1e-8, None, ALU.add))
                step(v.reciprocal(s_small[:, 6:8], s_small[:, 6:8]))
                step(v.tensor_scalar(inv_var[:, :], s_small[:, 6:8], -0.5, None, ALU.mult))
                step(v.tensor_scalar(s_small[:, 10:11], s_small[:, 10:11], 1.0, None, ALU.add))
                step(v.reciprocal(s_small[:, 10:11], s_small[:, 10:11]))
                step(v.tensor_scalar(dlt[:, :, :, :], dlt[:, :, :, :], s_small[:, 10:11], 0.2, ALU.mult, ALU.mult))
                step(v.tensor_tensor(cen[:, :, :, :], cen[:, :, :, :], dlt[:, :, :, :], ALU.add))
                step(v.tensor_tensor(dlt[:, 0], cen[:, 0], cen[:, 0], ALU.mult))
                step(v.tensor_reduce(w_bias[:, :], dlt[:, 0], AX.X, ALU.add))
                step(v.tensor_tensor(w_bias[:, :], w_bias[:, :], inv_var[:, :], ALU.mult))
                step(v.tensor_scalar(s_small[:, 5:6], s_small[:, 5:6], 0.1, 10.0, ALU.max, ALU.min))
                step(v.reciprocal(s_small[:, 5:6], s_small[:, 5:6]))
                step(v.tensor_scalar(s_small[:, 8:10], s_small[:, 8:10], s_small[:, 5:6], None, ALU.mult))
                for o in range(2):
                    step(v.tensor_reduce(parity[:, o:o + 1], block16[:, o::2, 0], AX.X, ALU.add))
                    step(v.tensor_scalar(k_scale[:, o], s_small[:, 8:10], parity[:, o:o + 1], None, ALU.mult))
                step(v.tensor_scalar(cen[:, 1], cen[:, 1], -2.0, None, ALU.mult))
                for t in range(KT):
                    step(v.tensor_tensor(minus2c[:, t].rearrange("p (h s) -> p h s", s=16), block16[:, :, :],
                                         cen[:, 1, t:t + 1, :].broadcast_to([P, 8, 16]), ALU.mult))
                for n, (parts, _, tiles, cols) in enumerate(chunks):
                    e.wait_ge(staged[n % STAGING], 16 * (n // STAGING + 1))
                    e.wait_ge(high_made, n + 1)
                    v.scalar_tensor_tensor(parts[:, 1], staging(n, tiles, cols), W_SCALE, parts[:, 0],
                                           ALU.mult, ALU.subtract).then_inc(low_made, 1)

        with nc.Fori(0, BATCH // STREAMS) as pair:
            with nc.Block() as block:
                @block.sync
                def _(e):
                    for s in range(STREAMS):
                        b = pair * STREAMS + s
                        e.dma_start(x[s][:, :, :], io["x"][bass.ds(b, 1)].rearrange("a (t p) f -> p (a t) f", p=P)
                                    ).then_inc(x_in, 16)
                        e.dma_start(cxT[s][:, :], io["ctx_t"][bass.ds(b, 1)].rearrange("a f t -> f (a t)")
                                    ).then_inc(c_in, 16)
                        e.dma_start(cx[s][0:CTX_TOK, :], io["ctx"][bass.ds(b, 1)].rearrange("a t f -> (a t) f")
                                    ).then_inc(c_in, 16)
                    for s in range(STREAMS):
                        b = pair * STREAMS + s
                        e.wait_ge(out_ready, upcoming(e, out_ready))
                        e.dma_start(out[bass.ds(b, 1)].rearrange("a (t p) f -> p (a t) f", p=P), x[s][:, :, :]
                                    ).then_inc(out_done, 16)
                    e.wait_ge(out_done, 16 * STREAMS)

                number = {}
                at = [0, 0]

                def moved(*what):
                    return number[(at[0], at[1], *what)] + 1


                @block.tensor
                def _(e):
                    mm = nc.tensor.matmul
                    used = {"a": 0, "v": 0}

                    def slot(which, what=None):
                        n = used[which]
                        used[which] += 1
                        number[(at[0], at[1], what)] = n
                        if which == "a":
                            if n >= RING:
                                e.wait_ge(a_done, n + 1 - RING)
                            return ring_a[n % RING]
                        if n >= RING:
                            e.wait_ge(v_done, n + 1 - RING)
                        return ring_v[n % RING]

                    def product(o, stationary, moving, n_in):
                        for k in range(n_in):
                            for a_, b_ in PARTS:
                                last = mm(o, stationary(a_, k), moving(b_, k), start=(k, a_, b_) == (0, 0, 0),
                                          stop=k == n_in - 1 and (a_, b_) == PARTS[-1])
                        return last

                    def transposes(src, n_feat, what):
                        ps = slot("a", what)
                        for f in range(n_feat):
                            for t in range(NT):
                                last = nc.tensor.transpose(ps[:, f * TOK + t * P:f * TOK + t * P + P],
                                                           src[:, t, f * P:f * P + P], ident[:, :])
                        last.then_inc(a_full, one(a_full))

                    def to_xT(src, ready, what="xT", split=True):
                        if ready is not None:
                            e.wait_ge(ready, upcoming(e, ready))
                        transposes(src, KT, what)
                        if split:
                            e.wait_ge(xs_ready, upcoming(e, xs_ready))

                    def feature_major(ws, col, tiles, src, n_in, n_tok, what):
                        for m in range(0, tiles, 2):
                            ps = slot("a", what)
                            for i in range(2):
                                c = col + (m + i) * P
                                last = product(ps[:, i * TOK:i * TOK + n_tok],
                                               lambda wp, k: ws[:, wp, k, c:c + P],
                                               lambda xp, k: src[:, xp, k, 0:n_tok], n_in)
                            last.then_inc(a_full, one(a_full))

                    def token_major(ws, col, cols, src, n_in, tiles, which, what=None, k0=0):
                        ps = slot(which, what)
                        for i, (t0, n) in enumerate(tiles):
                            last = product(ps[0:n, i * cols:(i + 1) * cols],
                                           lambda xp, k: src[:, xp, k, t0:t0 + n],
                                           lambda wp, k: ws[:, wp, k0 + k, col:col + cols], n_in)
                        full = a_full if which == "a" else v_full
                        last.then_inc(full, one(full))

                    token_tiles = [(t * P, P) for t in range(NT)]

                    def values(a, ws, col, src, n_in):
                        if a.dim == 16:
                            token_major(ws, col, 256, src, n_in, a.key_tiles, "a", "v")
                        else:
                            for tile in a.key_tiles:
                                token_major(ws, col, 512, src, n_in, [tile], "a", "v")

                    def row_scores(a, h):
                        t, q0, kx = a.at(h)
                        ps = slot("v", ("max", h))
                        for i in range(NT):
                            o = ps[:, i * TOK:i * TOK + a.keys]
                            last = mm(o, q[q0:q0 + 32, 0, t, i * P:i * P + P], k[q0:q0 + 32, 0, kx, 0:a.keys],
                                      start=True, stop=not a.causal)
                            if a.causal:
                                last = mm(o, ident_h[:, :], mask_q[:, i, :], start=False, stop=True)
                        last.then_inc(v_full, one(v_full))

                    def exact_scores(a, h):
                        t, q0, kx = a.at(h)
                        ps = slot("a", ("p", h))
                        e.wait_ge(v_done, moved(("max", h)))
                        for j, (k0, n) in enumerate(a.key_tiles):
                            i0 = j * P if a.causal else 0
                            c0 = j * TOK
                            o = ps[0:n, c0:c0 + TOK - i0]
                            for kp, qp in PARTS:
                                mm(o, k[q0:q0 + 32, kp, kx, k0:k0 + n], q[q0:q0 + 32, qp, t, i0:TOK],
                                   start=(kp, qp) == (0, 0), stop=False)
                            if a.causal:
                                mm(ps[0:n, c0:c0 + P], ident_h[:, :], mask_k[:, :], start=False, stop=False)
                            for i in range(i0 // P, NT):
                                c = c0 + i * P - i0
                                last = mm(ps[0:n, c:c + P], negm[:, h * NT + i:h * NT + i + 1].broadcast_to([P, n]),
                                          ident_h[:, :], start=False, stop=i == NT - 1)
                        last.then_inc(a_full, one(a_full))

                    def weighted_values(a, h):
                        D = a.dim
                        v = v16 if D == 16 else v32
                        if h % HG == 0 and sent(o_full) > 0:
                            e.wait_ge(o_done, sent(o_full))
                        if h == 0:
                            e.wait_ge(vs_ready, upcoming(e, vs_ready))
                        e.wait_ge(ps_ready, upcoming(e, ps_ready))
                        if a.keep_after:
                            e.wait_ge(pm_ready, upcoming(e, pm_ready))

                        def pr(part, n, c):
                            return prob[0:n, part, h % PBUF, c:c + P]

                        c = (h % HG) * (D + 1)
                        for i in range(NT):
                            o = o_bank[i][:, c:c + D + 1]
                            if a.keep_after:
                                for part in range(2):
                                    mm(o, pr(part, P, i * P), zero_one[:, :], start=part == 0, stop=False)
                                if i == 0:
                                    for pp, vp in PARTS:
                                        mm(o, pr(pp, P, TOK), v[:, vp, HEADS + h, :], start=False, stop=False)
                                else:
                                    for part in range(2):
                                        mm(o, pr(part, P, TOK + P), zero_one[:, :], start=False, stop=False)
                                for pp, vp in PARTS:
                                    last = mm(o_bank[i][:, c:c + D], probm[:, pp, h % MBUF, i, :],
                                              v[:, vp, i * HEADS + h, 0:D], start=False, stop=(pp, vp) == PARTS[-1])
                                continue
                            js = [j for j in range(len(a.key_tiles)) if not (a.causal and j > i)]
                            for j in js:
                                n = a.key_tiles[j][1]
                                c1 = j * TOK + i * P - (j * P if a.causal else 0)
                                for pp, vp in PARTS:
                                    last = mm(o, pr(pp, n, c1), v[0:n, vp, j * HEADS + h, :],
                                              start=(j, pp, vp) == (0, 0, 0),
                                              stop=j == js[-1] and (pp, vp) == PARTS[-1])
                        if h % HG == HG - 1:
                            last.then_inc(o_full, one(o_full))
                            number[(at[0], at[1], ("o", h // HG))] = sent(o_full) - 1

                    def group_to_features(a, g):
                        e.wait_ge(o_done, number[(at[0], at[1], ("o", g))] + 1)
                        n = a.tiles // GROUPS
                        ps = slot("a", ("oT", g))
                        for f in range(n):
                            for t in range(NT):
                                c = (g * n + f) * P
                                last = nc.tensor.transpose(ps[:, f * TOK + t * P:f * TOK + t * P + P],
                                                           o_tok[:, t, c:c + P], ident[:, :])
                        last.then_inc(a_full, one(a_full))

                    def attend(a, w_out, n_out):
                        e.wait_ge(qk_ready, upcoming(e, qk_ready, 2))
                        for n in range(HEADS + MAX_LAG + PV_LAG):
                            if n < HEADS:
                                row_scores(a, n)
                            if 0 <= n - MAX_LAG < HEADS:
                                exact_scores(a, n - MAX_LAG)
                            h = n - MAX_LAG - PV_LAG
                            if 0 <= h < HEADS:
                                weighted_values(a, h)
                                if h == GROUP0_AT:
                                    group_to_features(a, 0)
                        group_to_features(a, 1)
                        e.wait_ge(os_ready, upcoming(e, os_ready, GROUPS))
                        token_major(w_out, 0, DM, oT, n_out, token_tiles, "v")

                    for stage in range(7):
                        for s in range(STREAMS):
                            at[:] = stage, s
                            if stage == 0:
                                e.wait_ge(x_in, 16 * STREAMS)
                                to_xT(x[s], None)
                                feature_major(w_qkv0, 0, 2, xT, KT, TOK, "q")
                                feature_major(w_qkv0, DM, 2, xT, KT, TOK, "k")
                                values(SPLAT, w_qkv0, 2 * DM, xT, KT)
                                for part in range(2):
                                    e.wait_ge(sq_ready, upcoming(e, sq_ready))
                                    ps = slot("a", ("w", part))
                                    for t in range(KT):
                                        o = ps[:, t * TOK:(t + 1) * TOK]
                                        mm(o, minus2c[:, t], raw[:, 4 * part + t, :], start=True, stop=False)
                                        last = mm(o, block16[:, :, :].rearrange("p a b -> p (a b)"),
                                                  squares[:, 2 * part + t, :], start=False, stop=True)
                                    last.then_inc(a_full, one(a_full))
                                attend(SPLAT, w_o0, KT)
                            elif stage == 1:
                                to_xT(x[s], z_ready)
                                feature_major(w_q1, 0, 2, xT, KT, TOK, "q")
                                feature_major(w_kv1, 0, 2, yT, 1, CTX_TOK, "k")
                                values(CROSS0, w_kv1, DM, yT, 1)
                                attend(CROSS0, w_o1, KT)
                            elif stage == 2:
                                to_xT(x[s], z_ready)
                                token_major(w_router, 0, EXPERTS, xT, KT, token_tiles, "v")
                                e.wait_ge(gm_ready, upcoming(e, gm_ready))
                                ps = slot("a", "gmT")
                                for t in range(NT):
                                    last = nc.tensor.transpose(ps[0:EXPERTS, t * P:t * P + P],
                                                               gm[:, t, 0:EXPERTS], ident[:, :])
                                last.then_inc(a_full, one(a_full))
                                e.wait_ge(a_done, moved("gmT"))
                                ps = slot("v")
                                for t in range(NT):
                                    last = mm(ps[:, t * DM:(t + 1) * DM], gmT[0:EXPERTS, t * P:t * P + P],
                                              b_exp[:, :], start=True, stop=True)
                                last.then_inc(v_full, one(v_full))
                                for n in range(EXPERTS):
                                    token_major(w_exp, 0, DM, xT, KT, token_tiles, "v", k0=n * KT)
                            elif stage == 3:
                                to_xT(x[s], z_ready)
                                feature_major(w_qkv2, 0, 2, xT, KT, TOK, "q")
                                feature_major(w_qkv2, DM, 2, xT, KT, TOK, "k")
                                values(CAUSAL, w_qkv2, 2 * DM, xT, KT)
                                attend(CAUSAL, w_o2, KT)
                            elif stage in (4, 5):
                                i = stage - 4
                                a = (SELF1, CROSS1)[i]
                                to_xT(z[s], z_ready, split=i == 0)
                                if i == 1:
                                    e.wait_ge(zc_ready, upcoming(e, zc_ready))
                                    ps = slot("a", "yT")
                                    nc.tensor.transpose(
                                        ps[:, 0:CTX_TOK], o_tok[0:CTX_TOK, 0, 0:CTX_DIM],
                                        ident[0:CTX_TOK, 0:CTX_TOK]).then_inc(a_full, one(a_full))
                                    e.wait_ge(xs_ready, upcoming(e, xs_ready))
                                n_in = KT if i == 0 else 1
                                feature_major(w_aq[i], 0, 4, xT, KT, TOK, "q")
                                feature_major(w_ak[i], 0, 4, yT, n_in, a.keys, "k")
                                values(a, w_av[i], 0, yT, n_in)
                                attend(a, w_li1[i], 4)
                                to_xT(z[s], zo_ready, "xoT")
                                for m in range(HID // P):
                                    ps = slot("a", ("hidden", m))
                                    last = product(ps[:, 0:TOK], lambda wp, k: w_li2[i][:, wp, k, m * P:m * P + P],
                                                   lambda xp, k: xT[:, xp, k, :], KT)
                                    last.then_inc(a_full, one(a_full))
                                e.wait_ge(hs_ready, upcoming(e, hs_ready, HID // P // 2))
                                token_major(w_li3[i], 0, DM, hidT, HID // P, token_tiles, "v")
                            else:
                                to_xT(x[s], z_ready)
                                token_major(w_sel, 0, TOP_EXPERTS, xT, KT, token_tiles, "a", "sel")
                                e.wait_ge(gm_ready, upcoming(e, gm_ready))
                                ps = slot("a", "gmT")
                                for t in range(NT):
                                    last = nc.tensor.transpose(ps[0:TOP_EXPERTS, t * P:t * P + P],
                                                               gm[:, t, :], ident[:, :])
                                last.then_inc(a_full, one(a_full))
                                e.wait_ge(a_done, moved("gmT"))
                                for m in range(HID // P):
                                    ps = slot("a", ("relu", m))
                                    last = product(ps[:, 0:TOK], lambda wp, k: w_keys[:, wp, k, m * P:m * P + P],
                                                   lambda xp, k: xT[:, xp, k, :], KT)
                                    last.then_inc(a_full, one(a_full))
                                    ps = slot("v", "mix")
                                    mm(ps[:, 0:TOK], spread[:, m, :], gmT[:, :],
                                                      start=True, stop=True).then_inc(v_full, one(v_full))
                                e.wait_ge(hs_ready, upcoming(e, hs_ready, HID // P // 2))
                                token_major(w_vals, 0, DM, hidT, HID // P, token_tiles, "v")

                @block.scalar
                def _(e):
                    act = nc.scalar.activation

                    def to_features(ps, at, gain=None, offset=None):
                        for f in range(KT):
                            src = ps[:, f * TOK:(f + 1) * TOK]
                            if gain is None:
                                last = act(raw[:, at + f, :], src, ACT.Copy)
                            else:
                                last = act(raw[:, at + f, :], src, ACT.Identity,
                                           bias=offset[:, f:f + 1], scale=gain[:, f:f + 1])
                        return last

                    def raw_tiles(base, tiles, n_tok, bias=None):
                        for m in range(0, tiles, 2):
                            e.wait_ge(a_full, upcoming(e, a_full))
                            ps = ring_a[bank_of(e, a_full)]
                            for i in range(2):
                                src = ps[:, i * TOK:i * TOK + n_tok]
                                dst = raw[:, base + m + i, 0:n_tok]
                                if bias is None:
                                    last = act(dst, src, ACT.Copy, scale=1 / W_SCALE)
                                else:
                                    last = act(dst, src, ACT.Identity, bias=bias[:, m + i:m + i + 1],
                                               scale=1 / W_SCALE)
                            last.then_inc(a_done, one(a_done))

                    def value_tiles(a):
                        cols = HEADS * a.dim
                        for group in ([a.key_tiles] if a.dim == 16 else [[t] for t in a.key_tiles]):
                            e.wait_ge(a_full, upcoming(e, a_full))
                            ps = ring_a[bank_of(e, a_full)]
                            for i, (k0, n) in enumerate(group):
                                last = act(o_tok[0:n, k0 // P, 0:cols], ps[0:n, i * cols:(i + 1) * cols],
                                           ACT.Copy, scale=1 / W_SCALE)
                            last.then_inc(a_done, one(a_done))

                    def attend(a, bias=None):
                        def to_oT(g):
                            n = a.tiles // GROUPS
                            e.wait_ge(a_full, upcoming(e, a_full))
                            ps = ring_a[bank_of(e, a_full)]
                            for f in range(n):
                                src = ps[:, f * TOK:(f + 1) * TOK]
                                dst = raw[:, g * n + f, :]
                                if bias is None:
                                    last = act(dst, src, ACT.Copy)
                                else:
                                    last = act(dst, src, ACT.Identity, bias=bias[:, g * n + f:g * n + f + 1])
                            last.then_inc(a_done, one(a_done))

                        for h in range(HEADS):
                            e.wait_ge(a_full, upcoming(e, a_full))
                            ps = ring_a[bank_of(e, a_full)]
                            n = a.key_tiles[0][1]
                            cols = TOK * len(a.key_tiles) - (P if a.causal else 0)
                            act(p32[0:n, h % PBUF, 0:cols], ps[0:n, 0:cols], ACT.Exp, bias=p_log[0:n, :], scale=a.scale)
                            act(prob[0:n, 0, h % PBUF, 0:cols], ps[0:n, 0:cols], ACT.Exp, bias=p_log[0:n, :],
                                scale=a.scale).then_inc(a_done, one(a_done))
                            if h == GROUP0_AT + PV_LAG:
                                to_oT(0)
                        to_oT(1)

                    for stage in range(7):
                        for s in range(STREAMS):
                            if stage in (0, 1, 2, 3, 6):
                                e.wait_ge(a_full, upcoming(e, a_full))
                                to_features(ring_a[bank_of(e, a_full)], 0).then_inc(a_done, one(a_done))
                            if stage == 0:
                                raw_tiles(0, 2, TOK)
                                raw_tiles(4, 2, TOK)
                                value_tiles(SPLAT)
                                for part in range(2):
                                    e.wait_ge(a_full, upcoming(e, a_full))
                                    ps = ring_a[bank_of(e, a_full)]
                                    for t in range(KT):
                                        last = act(raw[:, part * 4 + t, :], ps[:, t * TOK:(t + 1) * TOK], ACT.Exp,
                                                   bias=w_bias[:, t:t + 1], scale=inv_var[:, t:t + 1])
                                    last.then_inc(a_done, one(a_done))
                                attend(SPLAT)
                            elif stage == 1:
                                raw_tiles(0, 2, TOK)
                                raw_tiles(4, 2, CTX_TOK)
                                value_tiles(CROSS0)
                                attend(CROSS0)
                            elif stage == 2:
                                e.wait_ge(nmax_ready, upcoming(e, nmax_ready))
                                for t in range(NT):
                                    last = act(ex[:, t, 0:EXPERTS], lg[:, t, 0:EXPERTS], ACT.Exp,
                                               bias=nmax[:, t:t + 1], accum_out=esum[:, t:t + 1])
                                last.then_inc(exps_ready, one(exps_ready))
                                e.wait_ge(a_full, upcoming(e, a_full))
                                act(gmT[0:EXPERTS, :], ring_a[bank_of(e, a_full)][0:EXPERTS, 0:TOK], ACT.Copy).then_inc(a_done, one(a_done))
                            elif stage == 3:
                                raw_tiles(0, 2, TOK, bq2[:, 0:2])
                                raw_tiles(4, 2, TOK, bq2[:, 2:4])
                                value_tiles(CAUSAL)
                                attend(CAUSAL, bq2[:, 4:6])
                            elif stage in (4, 5):
                                i = stage - 4
                                a = (SELF1, CROSS1)[i]
                                e.wait_ge(a_full, upcoming(e, a_full))
                                ps = ring_a[bank_of(e, a_full)]
                                last = to_features(ps, 0, gx[i], bx[i])
                                if i == 0:
                                    last = to_features(ps, 2, gy[i], by[i])
                                last.then_inc(a_done, one(a_done))
                                if i == 1:
                                    e.wait_ge(a_full, upcoming(e, a_full))
                                    act(raw[:, 4, 0:CTX_TOK], ring_a[bank_of(e, a_full)][:, 0:CTX_TOK], ACT.Identity,
                                             bias=by[i][:, 0:1], scale=gy[i][:, 0:1]).then_inc(a_done, one(a_done))
                                raw_tiles(0, 4, TOK)
                                raw_tiles(4, 4, a.keys)
                                value_tiles(a)
                                attend(a)
                                e.wait_ge(a_full, upcoming(e, a_full))
                                to_features(ring_a[bank_of(e, a_full)], 0, g3[i], b3[i]).then_inc(a_done, one(a_done))
                                for m in range(HID // P):
                                    e.wait_ge(a_full, upcoming(e, a_full))
                                    act(raw[:, m, :], ring_a[bank_of(e, a_full)][:, 0:TOK], ACT.Gelu, bias=b_li2[i][:, m:m + 1],
                                        scale=1 / W_SCALE).then_inc(a_done, one(a_done))
                            else:
                                e.wait_ge(a_full, upcoming(e, a_full))
                                act(ex[:, :, :], ring_a[bank_of(e, a_full)][:, 0:NT * TOP_EXPERTS].rearrange(
                                    "p (t n) -> p t n", t=NT), ACT.Exp, scale=-1 / W_SCALE).then_inc(a_done, one(a_done))
                                e.wait_ge(a_full, upcoming(e, a_full))
                                act(gmT[:, :], ring_a[bank_of(e, a_full)][0:TOP_EXPERTS, 0:TOK], ACT.Copy).then_inc(a_done, one(a_done))
                                for m in range(HID // P):
                                    e.wait_ge(a_full, upcoming(e, a_full))
                                    act(relus[:, m, :], ring_a[bank_of(e, a_full)][:, 0:TOK], ACT.Relu, scale=1 / W_SCALE).then_inc(a_done, one(a_done))

                @block.vector
                def _(e):
                    v = nc.vector

                    def flat(t):
                        return t[:, :, :].rearrange("p t f -> p (t f)")

                    def norm(src, dst, ready=dve_step, n=P, nt=NT):
                        for t in range(nt):
                            v.bn_stats(stats[0:n, t], src[0:n, t, :]).then_inc(dve_step, one(dve_step))
                        e.wait_ge(dve_step, sent(dve_step))
                        for t in range(nt):
                            v.bn_aggr(mv[0:n, t], stats[0:n, t]).then_inc(dve_step, one(dve_step))
                        e.wait_ge(dve_step, sent(dve_step))
                        v.tensor_scalar(veps[0:n, 0:nt], mv[0:n, 0:nt, 1], EPS, None, ALU.add).then_inc(var_ready, one(var_ready))
                        e.wait_ge(rstd_ready, upcoming(e, rstd_ready))
                        for t in range(nt):
                            signal = dve_step if t < nt - 1 else ready
                            v.tensor_scalar(dst[0:n, t, :], src[0:n, t, :], mv[0:n, t, 0:1], rstd[0:n, t:t + 1],
                                            ALU.subtract, ALU.mult).then_inc(signal, one(signal))
                        e.wait_ge(dve_step, sent(dve_step))
                        e.wait_ge(ready, sent(ready))

                    def gain(s, i):
                        for op, row in ((ALU.mult, r_g[i]), (ALU.add, r_b[i])):
                            v.tensor_tensor(xa[s][:, :, :], xa[s][:, :, :],
                                                 row[:, :].rearrange("p (a n) -> p a n", a=1)
                                                 .broadcast_to([P, NT, DM]), op).then_inc(dve_step, one(dve_step))
                            e.wait_ge(dve_step, sent(dve_step))

                    def split(src, high, low, scale=None):
                        if scale is None:
                            v.tensor_copy(high, src).then_inc(dve_step, one(dve_step))
                            e.wait_ge(dve_step, sent(dve_step))
                            return v.tensor_tensor(low, src, high, ALU.subtract)
                        v.tensor_scalar(high, src, scale, None, ALU.mult).then_inc(dve_step, one(dve_step))
                        e.wait_ge(dve_step, sent(dve_step))
                        return v.scalar_tensor_tensor(low, src, scale, high, ALU.mult, ALU.subtract)

                    def split_xT(what, ready=xs_ready):
                        e.wait_ge(a_done, moved(what))
                        split(raw[:, 0:KT, :], xT[:, 0], xT[:, 1]).then_inc(ready, one(ready))

                    def split_queries(a):
                        e.wait_ge(a_done, moved(("w", 0) if a.splat else "q"))
                        n = a.tiles
                        split(raw[:, 0:n, :], q[:, 0, 0:n, :], q[:, 1, 0:n, :]).then_inc(qk_ready, one(qk_ready))

                    def split_keys(a):
                        e.wait_ge(a_done, moved(("w", 1) if a.splat else "k"))
                        n = a.keys
                        src = raw[:, 4:4 + a.tiles, 0:n]
                        if a.dim == 32:
                            last = split(src, k[:, 0, :, 0:n], k[:, 1, :, 0:n])
                        else:
                            for o in range(2):
                                if a.splat:
                                    for t in range(KT):
                                        last = split(raw[:, 4 + t, 0:n], k[:, 0, 2 * o + t, 0:n],
                                                     k[:, 1, 2 * o + t, 0:n], k_scale[:, o, t:t + 1])
                                else:
                                    last = split(src, k[:, 0, 2 * o:2 * o + 2, 0:n], k[:, 1, 2 * o:2 * o + 2, 0:n],
                                                 parity[:, o:o + 1])
                        last.then_inc(qk_ready, one(qk_ready))

                    def split_values(a):
                        e.wait_ge(a_done, moved("v"))
                        to = v16 if a.dim == 16 else v32
                        for j, (_, n) in enumerate(a.key_tiles):
                            heads = slice(j * HEADS, (j + 1) * HEADS)
                            last = split(o_tok[0:n, j, 0:HEADS * a.dim].rearrange("p (h d) -> p h d", d=a.dim),
                                         to[0:n, 0, heads, 0:a.dim], to[0:n, 1, heads, 0:a.dim])
                        last.then_inc(vs_ready, one(vs_ready))

                    def split_hidden(m):
                        split(raw[:, m:m + 2, :], hidT[:, 0, m:m + 2, :], hidT[:, 1, m:m + 2, :]
                              ).then_inc(hs_ready, one(hs_ready))

                    def attend(a):
                        D = a.dim

                        def split_output(g):
                            e.wait_ge(a_done, moved(("oT", g)))
                            n = a.tiles // GROUPS
                            split(raw[:, g * n:(g + 1) * n, :], oT[:, 0, g * n:(g + 1) * n, :],
                                  oT[:, 1, g * n:(g + 1) * n, :]).then_inc(os_ready, one(os_ready))

                        def normalise(g):
                            e.wait_ge(o_full, upcoming(e, o_full))
                            views = [o_bank[i][:, 0:HG * (D + 1)].rearrange("p (h d) -> p h d", d=D + 1)
                                     for i in range(NT)]
                            for i, o in enumerate(views):
                                v.reciprocal(recip[:, i], o[:, :, D]).then_inc(dve_step, one(dve_step))
                                e.wait_ge(dve_step, sent(dve_step))
                            for i, o in enumerate(views):
                                dst = o_tok[:, i, g * HG * D:(g + 1) * HG * D].rearrange("p (h d) -> p h d", d=D)
                                last = v.tensor_tensor(dst, o[:, :, 0:D], recip[:, i].rearrange(
                                    "p (h a) -> p h a", a=1).broadcast_to([P, HG, D]), ALU.mult)
                            last.then_inc(o_done, one(o_done))

                        for n in range(HEADS + LOW_LAG):
                            if n < HEADS:
                                e.wait_ge(v_full, upcoming(e, v_full))
                                ps = ring_v[bank_of(e, v_full)]
                                v.tensor_reduce(
                                    negm[:, n * NT:(n + 1) * NT],
                                    ps[:, :].rearrange("p (t n) -> p t n", t=NT)[:, :, 0:a.keys],
                                    AX.X, ALU.max, negate=True).then_inc(v_done, one(v_done))
                            if n == 1:
                                split_values(a)
                            h = n - LOW_LAG
                            if h >= 0:
                                e.wait_ge(a_done, moved(("p", h)))
                                rows = a.key_tiles[0][1]
                                cols = TOK * len(a.key_tiles) - (P if a.causal else 0)
                                v.tensor_tensor(prob[0:rows, 1, h % PBUF, 0:cols], p32[0:rows, h % PBUF, 0:cols],
                                                prob[0:rows, 0, h % PBUF, 0:cols], ALU.subtract
                                                ).then_inc(ps_ready, one(ps_ready))
                            if n == HG - 1 + MAX_LAG + PV_LAG:
                                normalise(0)
                            if n == HEADS:
                                split_output(0)
                        normalise(1)
                        split_output(1)

                    def add_bank(dst, other, scale=1 / W_SCALE):
                        e.wait_ge(v_full, upcoming(e, v_full))
                        v.scalar_tensor_tensor(flat(dst), ring_v[bank_of(e, v_full)][:, :], scale, flat(other),
                                               ALU.mult, ALU.add).then_inc(v_done, one(v_done))
                        e.wait_ge(v_done, sent(v_done))

                    for stage in range(7):
                        for s in range(STREAMS):
                            at[:] = stage, s
                            if stage == 0:
                                split_xT("xT")
                                for part, what in enumerate(("q", "k")):
                                    e.wait_ge(a_done, moved(what))
                                    v.tensor_tensor(
                                        squares[:, 2 * part:2 * part + 2, :], raw[:, 4 * part:4 * part + 2, :],
                                        raw[:, 4 * part:4 * part + 2, :], ALU.mult).then_inc(sq_ready, one(sq_ready))
                                split_queries(SPLAT)
                                split_keys(SPLAT)
                                attend(SPLAT)
                                add_bank(x[s], x[s])
                                norm(x[s], x[s], z_ready)
                            elif stage == 1:
                                e.wait_ge(c_in, 32 * STREAMS)
                                v.tensor_copy(yT[:, 0, 0, 0:CTX_TOK], cxT[s][:, :]).then_inc(dve_step, one(dve_step))
                                e.wait_ge(dve_step, sent(dve_step))
                                v.tensor_tensor(yT[:, 1, 0, 0:CTX_TOK], cxT[s][:, :], yT[:, 0, 0, 0:CTX_TOK],
                                                ALU.subtract).then_inc(dve_step, one(dve_step))
                                split_xT("xT")
                                split_queries(CROSS0)
                                split_keys(CROSS0)
                                attend(CROSS0)
                                add_bank(x[s], x[s])
                                norm(x[s], x[s], z_ready)
                            elif stage == 2:
                                split_xT("xT")
                                e.wait_ge(v_full, upcoming(e, v_full))
                                v.scalar_tensor_tensor(
                                    lg[:, :, 0:EXPERTS], ring_v[bank_of(e, v_full)][:, 0:NT * EXPERTS].rearrange(
                                        "p (t n) -> p t n", t=NT), 1 / W_SCALE,
                                    r_router[:, :].rearrange("p (a n) -> p a n", a=1).broadcast_to([P, NT, EXPERTS]),
                                    ALU.mult, ALU.add).then_inc(v_done, one(v_done))
                                e.wait_ge(v_done, sent(v_done))
                                for t in range(NT):
                                    v.max(top8[:, t], lg[:, t, 0:EXPERTS]).then_inc(dve_step, one(dve_step))
                                    e.wait_ge(dve_step, sent(dve_step))
                                v.tensor_copy(lgv[:, :, 0:1], top8[:, :, 0:1]).then_inc(dve_step, one(dve_step))
                                e.wait_ge(dve_step, sent(dve_step))
                                v.tensor_scalar(nmax[:, :], top8[:, :, 0], -1.0, None, ALU.mult).then_inc(nmax_ready, one(nmax_ready))
                                for t in range(NT):
                                    v.match_replace(mr[:, t, 0:16], lgv[:, t], lg[:, t], MARK).then_inc(dve_step, one(dve_step))
                                    e.wait_ge(dve_step, sent(dve_step))
                                v.tensor_scalar(gm[:, :, 0:EXPERTS], mr[:, :, 0:EXPERTS], MARK, None, ALU.is_equal).then_inc(dve_step, one(dve_step))
                                e.wait_ge(dve_step, sent(dve_step))
                                e.wait_ge(exps_ready, upcoming(e, exps_ready))
                                v.reciprocal(gate[:, :], esum[:, :]).then_inc(dve_step, one(dve_step))
                                e.wait_ge(dve_step, sent(dve_step))
                                for t in range(NT):
                                    signal = dve_step if t < NT - 1 else gm_ready
                                    v.tensor_scalar(gm[:, t, 0:EXPERTS], gm[:, t, 0:EXPERTS], gate[:, t:t + 1],
                                                         None, ALU.mult).then_inc(signal, one(signal))
                                    e.wait_ge(signal, sent(signal))
                                v.tensor_scalar(gmw[:, :, :], gm[:, :, 0:EXPERTS], 1 / W_SCALE, None, ALU.mult
                                                ).then_inc(dve_step, one(dve_step))
                                e.wait_ge(dve_step, sent(dve_step))
                                add_bank(x[s], x[s], 1.0)
                                for n in range(EXPERTS):
                                    e.wait_ge(v_full, upcoming(e, v_full))
                                    ps = ring_v[bank_of(e, v_full)]
                                    for t in range(NT):
                                        signal = dve_step if t < NT - 1 else v_done
                                        v.scalar_tensor_tensor(x[s][:, t, :], ps[:, t * DM:(t + 1) * DM],
                                                                    gmw[:, t, n:n + 1], x[s][:, t, :],
                                                                    ALU.mult, ALU.add).then_inc(signal, one(signal))
                                        e.wait_ge(signal, sent(signal))
                                norm(x[s], x[s], z_ready)
                            elif stage == 3:
                                split_xT("xT")
                                split_queries(CAUSAL)
                                split_keys(CAUSAL)
                                attend(CAUSAL)
                                e.wait_ge(xo_ready, upcoming(e, xo_ready))
                                add_bank(x[s], xo[s])
                                norm(x[s], x[s])
                                norm(x[s], xa[s])
                                gain(s, 0)
                                norm(xa[s], z[s], z_ready)
                            elif stage in (4, 5):
                                i = stage - 4
                                a = (SELF1, CROSS1)[i]
                                if i == 1:
                                    norm(cx[s][:, :].rearrange("p (a f) -> p a f", a=1),
                                         o_tok[:, 0:1, 0:CTX_DIM], zc_ready, n=CTX_TOK, nt=1)
                                split_xT("xT", dve_step)
                                e.wait_ge(a_done, moved("xT" if i == 0 else "yT"))
                                if i == 0:
                                    last = split(raw[:, 2:4, :], yT[:, 0], yT[:, 1])
                                else:
                                    last = split(raw[:, 4, 0:CTX_TOK], yT[:, 0, 0, 0:CTX_TOK], yT[:, 1, 0, 0:CTX_TOK])
                                last.then_inc(xs_ready, one(xs_ready))
                                split_queries(a)
                                split_keys(a)
                                attend(a)
                                e.wait_ge(xo_ready, upcoming(e, xo_ready))
                                add_bank(xo[s], xo[s])
                                norm(xo[s], z[s], zo_ready)
                                split_xT("xoT")
                                for m in range(0, HID // P, 2):
                                    e.wait_ge(a_done, moved(("hidden", m + 1)))
                                    split_hidden(m)
                                e.wait_ge(xa_ready, upcoming(e, xa_ready, 2))
                                add_bank(xa[s], xa[s])
                                if i == 0:
                                    norm(xa[s], xa[s])
                                    gain(s, 1)
                                    norm(xa[s], z[s], z_ready)
                                else:
                                    v.tensor_tensor(flat(x[s]), flat(x[s]), flat(xa[s]), ALU.add).then_inc(dve_step, one(dve_step))
                                    e.wait_ge(dve_step, sent(dve_step))
                                    norm(x[s], x[s], z_ready)
                            else:
                                split_xT("xT")
                                e.wait_ge(a_done, moved("sel"))
                                v.tensor_scalar(ex[:, :, :], ex[:, :, :], 1.0, None, ALU.add).then_inc(dve_step, one(dve_step))
                                e.wait_ge(dve_step, sent(dve_step))
                                v.reciprocal(pe16[:, :, 0:16], ex[:, :, :]).then_inc(dve_step, one(dve_step))
                                e.wait_ge(dve_step, sent(dve_step))
                                for t in range(NT):
                                    v.max(top8[:, t], pe16[:, t, 0:16]).then_inc(dve_step, one(dve_step))
                                    e.wait_ge(dve_step, sent(dve_step))
                                v.tensor_copy(pv[:, :, 0:TOP_K], top8[:, :, 0:TOP_K]).then_inc(dve_step, one(dve_step))
                                e.wait_ge(dve_step, sent(dve_step))
                                for t in range(NT):
                                    v.match_replace(mr[:, t], pv[:, t], pe16[:, t], 2.0).then_inc(dve_step, one(dve_step))
                                    e.wait_ge(dve_step, sent(dve_step))
                                v.tensor_reduce(gate[:, :], top8[:, :, 0:TOP_K], AX.X, ALU.add).then_inc(dve_step, one(dve_step))
                                e.wait_ge(dve_step, sent(dve_step))
                                v.tensor_scalar(gate[:, :], gate[:, :], 1e-9, None, ALU.max).then_inc(dve_step, one(dve_step))
                                e.wait_ge(dve_step, sent(dve_step))
                                v.reciprocal(gate[:, :], gate[:, :]).then_inc(dve_step, one(dve_step))
                                e.wait_ge(dve_step, sent(dve_step))
                                v.tensor_scalar(gate[:, :], gate[:, :], r_route[:, 0:1], None, ALU.mult).then_inc(dve_step, one(dve_step))
                                e.wait_ge(dve_step, sent(dve_step))
                                v.scalar_tensor_tensor(gm[:, :, :], mr[:, :, 0:16], 2.0, pe16[:, :, 0:16],
                                                            ALU.is_equal, ALU.mult).then_inc(dve_step, one(dve_step))
                                e.wait_ge(dve_step, sent(dve_step))
                                for t in range(NT):
                                    signal = dve_step if t < NT - 1 else gm_ready
                                    v.tensor_scalar(gm[:, t, :], gm[:, t, :], gate[:, t:t + 1], None, ALU.mult).then_inc(signal, one(signal))
                                    e.wait_ge(signal, sent(signal))
                                for m in range(HID // P):
                                    e.wait_ge(a_done, moved(("relu", m)))
                                    e.wait_ge(v_full, upcoming(e, v_full))
                                    v.tensor_tensor(raw[:, m, :], ring_v[bank_of(e, v_full)][:, 0:TOK], relus[:, m, :],
                                                                   ALU.mult).then_inc(v_done, one(v_done))
                                    if m % 2:
                                        e.wait_ge(v_done, sent(v_done))
                                        split_hidden(m - 1)
                                add_bank(x[s], x[s])
                                norm(x[s], x[s], out_ready)

                @block.gpsimd
                def _(e):
                    g = nc.gpsimd

                    def root(n=P, nt=NT):
                        e.wait_ge(var_ready, upcoming(e, var_ready))
                        g.tensor_tensor(rstd[0:n, 0:nt], veps[0:n, 0:nt],
                                                           minus_half[0:n, 0:nt], ALU.pow).then_inc(rstd_ready, one(rstd_ready))

                    def add_row(dst, src, row):
                        return g.tensor_tensor(dst[:, :, :], src[:, :, :],
                                               row[:, :].rearrange("p (a n) -> p a n", a=1)
                                               .broadcast_to([P, NT, DM]), ALU.add)

                    for stage in range(7):
                        for s in range(STREAMS):
                            if stage in (3, 4, 5):
                                e.wait_ge(z_ready, (stage - 1) * STREAMS + s + 1)
                                if stage == 3:
                                    last = add_row(xo[s], x[s], r_bo2)
                                else:
                                    last = add_row(xo[s], xa[s], r_li1[stage - 4])
                                last.then_inc(xo_ready, one(xo_ready))
                            if stage == 5:
                                root(CTX_TOK, 1)
                            if stage == 4:
                                for h in range(HEADS):
                                    e.wait_ge(ps_ready, (3 * STREAMS + s) * HEADS + h + 1)
                                    for part in range(2):
                                        for t in range(NT):
                                            c = t * TOK + t * P
                                            last = g.affine_select(out=probm[:, part, h % MBUF, t, :],
                                                                   in_=prob[:, part, h % PBUF, c:c + P],
                                                                   compare_op=ALU.is_gt, fill=0.0, base=0,
                                                                   pattern=[[-1, P]], channel_multiplier=1)
                                    last.then_inc(pm_ready, one(pm_ready))
                            root()
                            if stage == 3:
                                root()
                                root()
                            if stage in (4, 5):
                                e.wait_ge(zo_ready, (stage - 4) * STREAMS + s + 1)
                                g.tensor_tensor(xa[s][:, :, :], xa[s][:, :, :], xo[s][:, :, :],
                                                                 ALU.add).then_inc(xa_ready, one(xa_ready))
                                e.wait_ge(xa_ready, sent(xa_ready))
                                add_row(xa[s], xa[s], r_li3[stage - 4]).then_inc(xa_ready, one(xa_ready))
                                root()
                                if stage == 4:
                                    root()

            nc.gpsimd.sem_clear(loop_sems)
            nc.all_engine_barrier()


def laid_out(i):
    import numpy as np

    def np_(name):
        return np.asarray(i[name])

    def per_head(name):
        w = np_(name)
        return w.transpose(1, 0, 2).reshape(w.shape[1], -1)

    d = {
        "x": np_("x"),
        "ctx": np_("ctx_512"),
        "ctx_t": np_("ctx_512").transpose(0, 2, 1),
        "centers": np_("L0_attn_splat_centers").reshape(DM, 16),
        "centers_t": np_("L0_attn_splat_centers").transpose(0, 2, 1).reshape(DM, 16),
        "deltas": np_("L0_attn_splat_deltas").reshape(DM, 16),
        "deltas_t": np_("L0_attn_splat_deltas").transpose(0, 2, 1).reshape(DM, 16),
        "log_scales": np_("L0_attn_splat_log_scales").reshape(-1),
        "log_amps": np_("L0_attn_splat_log_amplitudes").reshape(-1),
        "movement": np_("L0_attn_movement_scale").reshape(1),
        "temperature": np_("L0_attn_temperature").reshape(1),
        "qkv0": np_("L0_attn_qkv_w").T,
        "o0": np_("L0_attn_out_w").T,
        "q1": np_("L0_xattn_Wq").T,
        "kv1": np_("L0_xattn_Wkv").T,
        "o1": np_("L0_xattn_Wo").T,
        "router": np_("L0_ffn_router_w"),
        "router_b": np_("L0_ffn_router_b"),
        "expert_w": np_("L0_ffn_expert_w"),
        "expert_b": np_("L0_ffn_expert_b"),
        "qkv2": np_("L1_attn_w_qkv"),
        "bqkv2": np_("L1_attn_b_qkv"),
        "o2": np_("L1_attn_w_out"),
        "bo2": np_("L1_attn_b_out"),
        "sel": np_("L1_ffn_expert_sel").T,
        "keys": per_head("L1_ffn_keys"),
        "values": np_("L1_ffn_values").reshape(HID, DM),
        "route": np_("L1_ffn_route_scale"),
    }
    for a in range(2):
        pre = f"L1_xattn_a{a + 1}_"
        d[f"ln_g{a}"] = np_(f"L1_xattn_ln{a + 1}_g")
        d[f"ln_b{a}"] = np_(f"L1_xattn_ln{a + 1}_b")
        for w in ("wq", "wk", "wv"):
            d[f"{w}{a}"] = per_head(pre + w)
        for w in ("li1", "li2", "li3"):
            d[f"{w}_{a}"] = np_(f"{pre}{w}_w")
            d[f"{w}_b{a}"] = np_(f"{pre}{w}_b")
        for w in ("lnx", "lny", "ln3"):
            d[f"{w}_g{a}"] = np_(f"{pre}{w}_g")
            d[f"{w}_b{a}"] = np_(f"{pre}{w}_b")
    for name in ["log_scales", "log_amps", "bqkv2"] + [
            f"{n}{a}" for n in ("lnx_g", "lnx_b", "lny_g", "lny_b", "ln3_g", "ln3_b", "li2_b") for a in range(2)]:
        d[name] = d[name].reshape(-1, P).T
    return {k: np.ascontiguousarray(v) for k, v in d.items()}


def kernel(**inputs):
    import concourse.bacc as _bacc
    from concourse import mybir as _mybir
    from concourse.bass_utils import run_bass_kernel_spmd as _run

    nc = _bacc.Bacc("TRN2", target_bir_lowering=False, num_devices=1)
    data = laid_out(inputs)
    arrays = {f"in_{name}": a for name, a in data.items()}
    io = {name: nc.dram_tensor(f"in_{name}", a.shape, _mybir.dt.from_np(a.dtype), kind="ExternalInput").ap()
          for name, a in data.items()}
    out = nc.dram_tensor("out_0", (BATCH, TOK, DM), _mybir.dt.float32, kind="ExternalOutput").ap()
    decoder(nc, io, out)
    r = _run(nc, [arrays], core_ids=[0])
    return r.results[0]["out_0"]
```

```python
from contextlib import ExitStack

import concourse.bass as bass
from concourse import mybir

F32 = mybir.dt.float32
F16 = mybir.dt.float16
BF16 = mybir.dt.bfloat16
ALU = mybir.AluOpType
ACT = mybir.ActivationFunctionType
AX = mybir.AxisListType

P = 128
BATCH, TOK, DM, CTX_TOK, CTX_DIM = 16, 256, 256, 120, 128
STREAMS = 2
HEADS = 16
NT = TOK // P
KT = DM // P
EPS = 1e-5
EXPERTS, TOP_EXPERTS, TOP_DIM, TOP_K = 8, 16, 64, 4
HID = 1024
NEG = -1.0e30
LOW, MARK = -3.0e38, 3.0e38
RING = 3
PBUF = 4
PBUF32 = 2
MBUF = 3
W_SCALE = 64.0
P_LOG = 4.1588830833596715
PARTS = ((0, 0), (1, 0), (0, 1))
STAGING = 8
EXACT_LAG = 2
LOW_LAG = 3
PV_LAG = 5
NORM_LAG = 6


class Attn:

    def __init__(self, name, dim, keys, scale, causal=False, keep_after=False, splat=False):
        self.name, self.dim, self.keys, self.scale = name, dim, keys, scale
        self.causal, self.keep_after, self.splat = causal, keep_after, splat
        self.tiles = HEADS * dim // P
        self.group = min(HEADS // 2, TOK // (dim + 1))
        self.key_tiles = [(0, min(keys, P))] + ([(P, keys - P)] if keys > P else [])

    def at(self, h):
        if self.dim == 32:
            return h // 4, 32 * (h % 4), h // 4
        return h // 8, 32 * ((h % 8) // 2), 2 * (h % 2) + h // 8


ATTNS = [
    Attn("splat", 16, TOK, 1.0, splat=True),
    Attn("cross0", 16, CTX_TOK, 0.25),
    Attn("causal", 16, TOK, 0.25, causal=True),
    Attn("self1", 32, TOK, 32 ** -0.5, keep_after=True),
    Attn("cross1", 32, CTX_TOK, 32 ** -0.5),
]
SPLAT, CROSS0, CAUSAL, SELF1, CROSS1 = ATTNS


class Counts:

    def __init__(self):
        self.increments, self.awaited = {}, {}

    def one(self, sem):
        self.increments[sem.num] = self.increments.get(sem.num, 0) + 1
        return 1

    def sent(self, sem):
        return self.increments.get(sem.num, 0)

    def upcoming(self, engine, sem, n=1):
        key = (str(engine.engine), sem.num)
        self.awaited[key] = self.awaited.get(key, 0) + n
        return self.awaited[key]

    def bank_of(self, engine, full):
        return (self.awaited[(str(engine.engine), full.num)] - 1) % RING


ORDER = [(k, s, h) for k in range(len(ATTNS)) for s in range(STREAMS) for h in range(HEADS)]
STEPS = len(ORDER) + NORM_LAG


def ends_group(a, h):
    return h % a.group == a.group - 1 or h == HEADS - 1


TURNS = {(5, "oT"): 3, (5, "out"): 4, (5, "xoT"): 4, (5, "h0"): 4, (5, "h1"): 5, (5, "h2"): 8}


def turns(k, step):
    for _ in range(TURNS.get((k, step), 1)):
        yield True


def turn(between, n, last=False):
    phase, step = divmod(n, HEADS)
    if phase < len(ATTNS) * STREAMS and step >= NORM_LAG:
        k, s = (phase + 1) // STREAMS, (phase + 1) % STREAMS
        if last or k == len(ATTNS):
            next(between[k, s], None)
        if last and step == HEADS - 1 and k < len(ATTNS):
            for _ in between[k, s]:
                pass


def finish(between):
    ends = [between[len(ATTNS), s] for s in range(STREAMS)]
    while ends:
        ends = [end for end in ends if next(end, False)]


def decoder(nc, io, out):
    with ExitStack() as ctx:
        def sb(name, shape, dt=F32):
            return ctx.enter_context(nc.sbuf_tensor(name, shape, dt))

        def semaphore(name):
            return ctx.enter_context(nc.semaphore(name))

        def pair(name, tiles, n, partitions=P):
            return sb(name, [partitions, 2, tiles, n], F16)

        w_qkv0 = pair("w_qkv0", KT, 3 * DM)
        w_o0 = pair("w_o0", KT, DM)
        w_q1 = pair("w_q1", KT, DM)
        w_kv1 = pair("w_kv1", 1, 2 * DM)
        w_o1 = pair("w_o1", KT, DM)
        w_router = pair("w_router", KT, EXPERTS)
        w_exp = pair("w_exp", EXPERTS * KT, DM)
        b_exp = sb("b_exp", [EXPERTS, 2, DM], F16)
        w_qkv2 = pair("w_qkv2", KT, 3 * DM)
        w_o2 = pair("w_o2", KT, DM)
        bq2 = sb("bq2", [P, 6])
        w_aq = [pair(f"w_aq{a}", KT, 512) for a in range(2)]
        w_ak = [pair("w_ak0", KT, 512), pair("w_ak1", 1, 512)]
        w_av = [pair("w_av0", KT, 512), pair("w_av1", 1, 512)]
        w_li1 = [pair(f"w_li1_{a}", 4, DM) for a in range(2)]
        w_li2 = [pair(f"w_li2_{a}", KT, HID) for a in range(2)]
        w_li3 = [pair(f"w_li3_{a}", HID // P, DM) for a in range(2)]
        b_li2 = [sb(f"b_li2_{a}", [P, HID // P]) for a in range(2)]
        gx = [sb(f"gx{a}", [P, KT]) for a in range(2)]
        bx = [sb(f"bx{a}", [P, KT]) for a in range(2)]
        gy = [sb("gy0", [P, KT]), sb("gy1", [P, 1])]
        by = [sb("by0", [P, KT]), sb("by1", [P, 1])]
        g3 = [sb(f"g3{a}", [P, KT]) for a in range(2)]
        b3 = [sb(f"b3{a}", [P, KT]) for a in range(2)]
        w_sel = pair("w_sel", KT, TOP_EXPERTS)
        w_keys = pair("w_keys", KT, HID)
        w_vals = pair("w_vals", HID // P, DM)
        b_rows = sb("b_rows", [5, 2, DM], F16)
        r_g = [sb(f"r_g{a}", [P, DM]) for a in range(2)]
        r_b = [sb(f"r_b{a}", [P, DM]) for a in range(2)]
        r_router = sb("r_router", [P, EXPERTS])
        r_route = sb("r_route", [P, 1])

        ident = sb("ident", [P, P])
        ident_h = sb("ident_h", [P, P], F16)
        mask_q = sb("mask_q", [P, NT, TOK], BF16)
        mask_k = sb("mask_k", [P, P], BF16)
        block16 = sb("block16", [P, 8, 16])
        minus2c = sb("minus2c", [P, KT, P])
        parity = sb("parity", [P, 2])
        spread = sb("spread", [TOP_EXPERTS, HID // P, P], F16)
        zero_one = sb("zero_one", [P, 33], F16)
        inv_var = sb("inv_var", [P, KT])
        w_bias = sb("w_bias", [P, KT])
        k_scale = sb("k_scale", [P, 2, KT])
        s_small = sb("s_small", [P, 16])
        cen = sb("cen", [P, 2, KT, 16])
        dlt = sb("dlt", [P, 2, KT, 16])
        minus_half = sb("minus_half", [P, NT])
        p_log = sb("p_log", [P, 1])

        x = [sb(f"x{s}", [P, NT, DM]) for s in range(STREAMS)]
        xa = [sb(f"xa{s}", [P, NT, DM]) for s in range(STREAMS)]
        xo = [sb(f"xo{s}", [P, NT, DM]) for s in range(STREAMS)]
        z = [sb(f"z{s}", [P, NT, DM]) for s in range(STREAMS)]
        cx = [sb(f"cx{s}", [P, CTX_DIM]) for s in range(STREAMS)]
        cxT = [sb(f"cxT{s}", [P, CTX_TOK]) for s in range(STREAMS)]
        qT = [pair(f"q{s}", 4, TOK) for s in range(STREAMS)]
        kT = [pair(f"k{s}", 4, TOK) for s in range(STREAMS)]
        val = [pair(f"v{s}", NT * HEADS, 33) for s in range(STREAMS)]
        oT = pair("oT", 4, TOK)
        raw = sb("raw", [P, 8, TOK])
        o_tok = sb("o_tok", [P, NT, 512])
        p32 = sb("p32", [P, PBUF32, NT * TOK])
        prob = sb("prob", [P, 2, PBUF, NT * TOK], F16)
        hidT = pair("hidT", 4, TOK)

        def buffers_of(k, s):
            o, hid = (oT, hidT) if k < len(ATTNS) else (qT[s], kT[s])
            return o, o[:, :, 0:KT, :], o[:, :, KT:2 * KT, :], hid

        probm = sb("probm", [P, 2, MBUF, NT, P], F16)
        negm = sb("negm", [P, HEADS * NT], F16)
        recip = sb("recip", [P, NT, HEADS // 2])
        stats = sb("stats", [P, NT, 6])
        mv = sb("mv", [P, NT, 2])
        veps = sb("veps", [P, NT])
        rstd = sb("rstd", [P, NT])
        lg = sb("lg", [P, NT, 16])
        lgv = sb("lgv", [P, NT, 8])
        top8 = sb("top8", [P, NT, 8])
        mr = sb("mr", [P, NT, 24])
        nmax = sb("nmax", [P, NT])
        esum = sb("esum", [P, NT])
        ex = sb("ex", [P, NT, 16])
        gate = sb("gate", [P, NT])
        gm = sb("gm", [P, NT, 16])
        gmw = sb("gmw", [P, NT, EXPERTS])
        gm_parts = sb("gm_parts", [P, 2, NT, 16], F16)
        gmT = sb("gmT", [16, 2, TOK], F16)
        pe16 = sb("pe16", [P, NT, 24])
        pv = sb("pv", [P, NT, 8])

        bank = [ctx.enter_context(nc.psum_tensor(f"bank{i}", [P, 512], F32)) for i in range(8)]

        ring_a, ring_v, o_bank = bank[0:3], bank[3:6], bank[6:8]

        w_ready = [semaphore("setup_loaded"), semaphore("rows_loaded")]
        w_count = [0] * 2
        staged = [semaphore(f"staged{b}") for b in range(STAGING)]
        high_made = semaphore("high_made")
        low_made = semaphore("low_made")
        s_const = semaphore("s_const")
        first = semaphore("first_of_loop")
        a_full, v_full, o_full = semaphore("a_full"), semaphore("v_full"), semaphore("o_full")
        a_done, v_done, o_done = semaphore("a_done"), semaphore("v_done"), semaphore("o_done")
        x_in, c_in = semaphore("x_in"), semaphore("c_in")
        split_done = semaphore("split_done")
        ps_ready = semaphore("ps_ready")
        pm_ready = semaphore("pm_ready")
        z_ready = semaphore("z_ready")
        zo_ready = semaphore("zo_ready")
        zc_ready = semaphore("zc_ready")
        var_ready = semaphore("var_ready")
        rstd_ready = semaphore("rstd_ready")
        nmax_ready = semaphore("nmax_ready")
        exps_ready = semaphore("exps_ready")
        gm_ready = semaphore("gm_ready")
        xa_ready = semaphore("xa_ready")
        dve_step = semaphore("dve_step")
        out_ready, out_done = semaphore("out_ready"), semaphore("out_done")
        last_sem = semaphore("last_of_loop")
        loop_sems = range(first.num, last_sem.num + 1)
        counts = Counts()
        one, sent, upcoming, bank_of = counts.one, counts.sent, counts.upcoming, counts.bank_of

        def load(e, i, dst, src):
            e.dma_start(dst, src).then_inc(w_ready[i], 16)
            w_count[i] += 16

        def rows(ap, kt):
            return ap.rearrange("(t p) n -> p t n", p=P) if kt > 1 else ap

        def spread_row(ap):
            return ap.rearrange("(a n) -> a n", a=1).broadcast_to([P, ap.shape[0]])

        buffers = [t[s] for t in (x, xa, xo, z) for s in range(STREAMS)]

        def staging(n, tiles, cols):
            flat = buffers[n % STAGING][:, :, :].rearrange("p a b -> p (a b)")
            return flat[:, 0:tiles * cols].rearrange("p (a b) -> p a b", b=cols)

        chunks = []

        def add_weight(w, src, first=0):
            tiles, n = src.shape[0] // P, src.shape[1]
            view = src.rearrange("(t p) n -> p t n", p=P)
            step_t, step_n = max(1, 512 // n), min(n, 512)
            for t in range(0, tiles, step_t):
                nt = min(step_t, tiles - t)
                for c in range(0, n, step_n):
                    m = min(step_n, n - c)
                    chunks.append((w[:, :, first + t:first + t + nt, c:c + m], view[:, t:t + nt, c:c + m], nt, m))

        for w, name in ((w_qkv0, "qkv0"), (w_o0, "o0"), (w_q1, "q1"), (w_kv1, "kv1"), (w_o1, "o1"),
                        (w_router, "router")):
            add_weight(w, io[name])
        for n in range(EXPERTS):
            add_weight(w_exp, io["expert_w"][n], n * KT)
        for w, name in ((w_qkv2, "qkv2"), (w_o2, "o2")):
            add_weight(w, io[name])
        for a in range(2):
            for w, name in ((w_aq, f"wq{a}"), (w_ak, f"wk{a}"), (w_av, f"wv{a}"), (w_li1, f"li1_{a}"),
                            (w_li2, f"li2_{a}"), (w_li3, f"li3_{a}")):
                add_weight(w[a], io[name])
        for w, name in ((w_sel, "sel"), (w_keys, "keys"), (w_vals, "values")):
            add_weight(w, io[name])
        with nc.Block() as block:
            @block.sync
            def _(e):
                load(e, 0, cen[:, 0], io["centers"].rearrange("(t p) d -> p t d", p=P))
                load(e, 0, cen[:, 1], io["centers_t"].rearrange("(t p) d -> p t d", p=P))
                load(e, 0, dlt[:, 0], io["deltas"].rearrange("(t p) d -> p t d", p=P))
                load(e, 0, dlt[:, 1], io["deltas_t"].rearrange("(t p) d -> p t d", p=P))
                load(e, 0, s_small[:, 0:2], io["log_scales"])
                load(e, 0, s_small[:, 2:4], io["log_amps"])
                load(e, 0, s_small[:, 4:5], spread_row(io["movement"]))
                load(e, 0, s_small[:, 5:6], spread_row(io["temperature"]))
                load(e, 0, p32[0:EXPERTS, 1, 0:DM], io["expert_b"])
                load(e, 1, r_router[:, :], spread_row(io["router_b"]))
                load(e, 1, bq2[:, :], io["bqkv2"])
                for r, name in enumerate(("bo2", "li1_b0", "li1_b1", "li3_b0", "li3_b1")):
                    load(e, 0, p32[r:r + 1, 0, 0:DM], io[name].rearrange("(a n) -> a n", a=1))
                load(e, 1, r_route[:, :], spread_row(io["route"]))
                for a in range(2):
                    for dst, src in ((gx, "lnx_g"), (bx, "lnx_b"), (gy, "lny_g"), (by, "lny_b"),
                                     (g3, "ln3_g"), (b3, "ln3_b"), (b_li2, "li2_b")):
                        load(e, 1, dst[a][:, :], io[f"{src}{a}"])
                    for dst, src in ((r_g, "ln_g"), (r_b, "ln_b")):
                        load(e, 1, dst[a][:, :], spread_row(io[f"{src}{a}"]))
                for n, (_, src, tiles, cols) in enumerate(chunks):
                    if n >= STAGING:
                        e.wait_ge(low_made, n + 1 - STAGING)
                    e.dma_start(staging(n, tiles, cols), src).then_inc(staged[n % STAGING], 16)
                e.wait_ge(w_ready[0], w_count[0])
                e.wait_ge(w_ready[1], w_count[1])

            @block.gpsimd
            def _(e):
                g = nc.gpsimd
                made = [0]

                def step(instruction):
                    made[0] += 1
                    instruction.then_inc(s_const, 1)
                    e.wait_ge(s_const, made[0])

                for t in (ident, ident_h, mask_k, mask_q):
                    step(g.memset(t[:], 0.0))
                for t in (block16, spread, minus_half, zero_one):
                    step(g.memset(t[:], 1.0))
                for t in (ident, ident_h):
                    step(g.affine_select(out=t[:, :], in_=t[:, :], compare_op=ALU.not_equal, fill=1.0,
                                         base=0, pattern=[[-1, P]], channel_multiplier=1))
                step(g.affine_select(out=mask_k[:, :], in_=mask_k[:, :], compare_op=ALU.is_ge, fill=NEG,
                                     base=0, pattern=[[1, P]], channel_multiplier=-1))
                step(g.affine_select(out=mask_q[:, :, :], in_=mask_q[:, :, :], compare_op=ALU.is_ge, fill=NEG,
                                     base=0, pattern=[[P, NT], [-1, TOK]], channel_multiplier=1))
                step(g.affine_select(out=block16[:, :, :], in_=block16[:, :, :], compare_op=ALU.is_ge, fill=0.0,
                                     base=0, pattern=[[-16, 8], [0, 16]], channel_multiplier=1))
                step(g.affine_select(out=block16[:, :, :], in_=block16[:, :, :], compare_op=ALU.is_ge, fill=0.0,
                                     base=15, pattern=[[16, 8], [0, 16]], channel_multiplier=-1))
                step(g.affine_select(out=spread[:, :, :], in_=spread[:, :, :], compare_op=ALU.is_ge, fill=0.0,
                                     base=0, pattern=[[P, HID // P], [1, P]], channel_multiplier=-TOP_DIM))
                step(g.affine_select(out=spread[:, :, :], in_=spread[:, :, :], compare_op=ALU.is_ge, fill=0.0,
                                     base=TOP_DIM - 1, pattern=[[-P, HID // P], [-1, P]],
                                     channel_multiplier=TOP_DIM))
                step(g.memset(zero_one[:, 0:32], 0.0))
                step(g.memset(minus_half[:, :], -0.5))
                step(g.memset(p_log[:, :], P_LOG))
                for part in range(2):
                    for s in range(STREAMS):
                        step(g.memset(val[s][:, part, :, 32:33], 1.0 - part))
                step(g.memset(lg[:, :, 8:16], LOW))
                step(g.memset(lgv[:, :, :], LOW))
                step(g.memset(pe16[:, :, 16:24], -1.0))
                step(g.memset(pv[:, :, :], -1.0))
                step(g.memset(gm[:, :, :], 0.0))
            n_const = len("ident ident_h mask_k mask_q".split()) + 4 + 2 + 6

            s_act = semaphore("s_act")
            s_dv = semaphore("s_dv")

            @block.scalar
            def _(e):
                e.wait_ge(w_ready[0], w_count[0])
                nc.scalar.activation(s_small[:, 6:10], s_small[:, 0:4], ACT.Exp).then_inc(s_act, 1)
                nc.scalar.activation(s_small[:, 10:11], s_small[:, 4:5], ACT.Exp, scale=-1.0).then_inc(s_act, 1)
                for n, (parts, _, tiles, cols) in enumerate(chunks):
                    e.wait_ge(staged[n % STAGING], 16 * (n // STAGING + 1))
                    nc.scalar.activation(parts[:, 0], staging(n, tiles, cols), ACT.Copy, scale=W_SCALE
                                         ).then_inc(high_made, 1)

            @block.vector
            def _(e):
                v = nc.vector
                made = [0]

                def step(instruction):
                    made[0] += 1
                    instruction.then_inc(s_dv, 1)
                    e.wait_ge(s_dv, made[0])

                e.wait_ge(s_const, n_const)
                e.wait_ge(w_ready[0], w_count[0])
                e.wait_ge(s_act, 2)
                step(v.tensor_scalar(s_small[:, 6:8], s_small[:, 6:8], 0.01, 2.0, ALU.max, ALU.min))
                step(v.tensor_scalar(s_small[:, 8:10], s_small[:, 8:10], 1e-6, 10.0, ALU.max, ALU.min))
                step(v.tensor_tensor(s_small[:, 6:8], s_small[:, 6:8], s_small[:, 6:8], ALU.mult))
                step(v.tensor_scalar(s_small[:, 6:8], s_small[:, 6:8], 1e-8, None, ALU.add))
                step(v.reciprocal(s_small[:, 6:8], s_small[:, 6:8]))
                step(v.tensor_scalar(inv_var[:, :], s_small[:, 6:8], -0.5, None, ALU.mult))
                step(v.tensor_scalar(s_small[:, 10:11], s_small[:, 10:11], 1.0, None, ALU.add))
                step(v.reciprocal(s_small[:, 10:11], s_small[:, 10:11]))
                step(v.tensor_scalar(dlt[:, :, :, :], dlt[:, :, :, :], s_small[:, 10:11], 0.2, ALU.mult, ALU.mult))
                step(v.tensor_tensor(cen[:, :, :, :], cen[:, :, :, :], dlt[:, :, :, :], ALU.add))
                step(v.tensor_tensor(dlt[:, 0], cen[:, 0], cen[:, 0], ALU.mult))
                step(v.tensor_reduce(w_bias[:, :], dlt[:, 0], AX.X, ALU.add))
                step(v.tensor_tensor(w_bias[:, :], w_bias[:, :], inv_var[:, :], ALU.mult))
                step(v.tensor_scalar(s_small[:, 5:6], s_small[:, 5:6], 0.1, 10.0, ALU.max, ALU.min))
                step(v.reciprocal(s_small[:, 5:6], s_small[:, 5:6]))
                step(v.tensor_scalar(s_small[:, 8:10], s_small[:, 8:10], s_small[:, 5:6], None, ALU.mult))
                for o in range(2):
                    step(v.tensor_reduce(parity[:, o:o + 1], block16[:, o::2, 0], AX.X, ALU.add))
                    step(v.tensor_scalar(k_scale[:, o], s_small[:, 8:10], parity[:, o:o + 1], None, ALU.mult))
                step(v.tensor_scalar(cen[:, 1], cen[:, 1], -2.0, None, ALU.mult))
                for t in range(KT):
                    step(v.tensor_tensor(minus2c[:, t].rearrange("p (h s) -> p h s", s=16), block16[:, :, :],
                                         cen[:, 1, t:t + 1, :].broadcast_to([P, 8, 16]), ALU.mult))
                step(v.tensor_scalar(b_rows[:, 0, :], p32[0:5, 0, 0:DM], W_SCALE, None, ALU.mult))
                step(v.scalar_tensor_tensor(b_rows[:, 1, :], p32[0:5, 0, 0:DM], W_SCALE, b_rows[:, 0, :],
                                            ALU.mult, ALU.subtract))
                step(v.tensor_scalar(b_exp[:, 0, :], p32[0:EXPERTS, 1, 0:DM], W_SCALE, None, ALU.mult))
                step(v.scalar_tensor_tensor(b_exp[:, 1, :], p32[0:EXPERTS, 1, 0:DM], W_SCALE, b_exp[:, 0, :],
                                            ALU.mult, ALU.subtract))
                for n, (parts, _, tiles, cols) in enumerate(chunks):
                    e.wait_ge(staged[n % STAGING], 16 * (n // STAGING + 1))
                    e.wait_ge(high_made, n + 1)
                    v.scalar_tensor_tensor(parts[:, 1], staging(n, tiles, cols), W_SCALE, parts[:, 0],
                                           ALU.mult, ALU.subtract).then_inc(low_made, 1)

        with nc.Fori(0, BATCH // STREAMS) as pass_:
            with nc.Block() as block:
                @block.sync
                def _(e):
                    for s in range(STREAMS):
                        b = pass_ * STREAMS + s
                        e.dma_start(x[s][:, :, :], io["x"][bass.ds(b, 1)].rearrange("a (t p) f -> p (a t) f", p=P)
                                    ).then_inc(x_in, 16)
                        e.dma_start(cxT[s][:, :], io["ctx_t"][bass.ds(b, 1)].rearrange("a f t -> f (a t)")
                                    ).then_inc(c_in, 16)
                        e.dma_start(cx[s][0:CTX_TOK, :], io["ctx"][bass.ds(b, 1)].rearrange("a t f -> (a t) f")
                                    ).then_inc(c_in, 16)
                    for s in range(STREAMS):
                        b = pass_ * STREAMS + s
                        e.wait_ge(out_ready, upcoming(e, out_ready))
                        e.dma_start(out[bass.ds(b, 1)].rearrange("a (t p) f -> p (a t) f", p=P), x[s][:, :, :]
                                    ).then_inc(out_done, 16)
                    e.wait_ge(out_done, 16 * STREAMS)

                number, half = {}, {}

                def moved(*what):
                    return number[what] + 1

                def was_split(*what):
                    return half[what] + 1

                @block.tensor
                def _(e):
                    mm = nc.tensor.matmul
                    used = {"a": 0, "v": 0}

                    def slot(which, *what):
                        n = used[which]
                        used[which] += 1
                        number[what] = n
                        if which == "a":
                            if n >= RING:
                                e.wait_ge(a_done, n + 1 - RING)
                            return ring_a[n % RING]
                        if n >= RING:
                            e.wait_ge(v_done, n + 1 - RING)
                        return ring_v[n % RING]

                    def to_raw(*what):
                        half[what] = len(half)

                    def product(o, stationary, moving, n_in, more=False, start=True):
                        for n in range(n_in):
                            for a_, b_ in PARTS:
                                last = mm(o, stationary(a_, n), moving(b_, n), start=start and (n, a_, b_) == (0, 0, 0),
                                          stop=n == n_in - 1 and (a_, b_) == PARTS[-1] and not more)
                        return last

                    def transposes(src, n_feat, *what, first=0):
                        ps = slot("a", *what)
                        for f in range(n_feat):
                            for t in range(NT):
                                c = (first + f) * P
                                last = nc.tensor.transpose(ps[:, f * TOK + t * P:f * TOK + t * P + P],
                                                           src[:, t, c:c + P], ident[:, :])
                        last.then_inc(a_full, one(a_full))

                    def to_xT(src, ready, *what):
                        to_raw(*what)
                        if ready is not None:
                            e.wait_ge(ready, upcoming(e, ready))
                        transposes(src, KT, *what)

                    def feature_major(ws, col, tiles, src, n_in, n_tok, *what):
                        to_raw(*what)
                        for m in range(0, tiles, 2):
                            ps = slot("a", *what)
                            for i in range(2):
                                c = col + (m + i) * P
                                last = product(ps[:, i * TOK:i * TOK + n_tok],
                                               lambda wp, n: ws[:, wp, n, c:c + P],
                                               lambda xp, n: src[:, xp, n, 0:n_tok], n_in)
                            last.then_inc(a_full, one(a_full))

                    def token_major(ws, col, cols, src, n_in, tiles, which, *what, k0=0, bias=None):
                        ps = slot(which, *what)
                        for i, (t0, n) in enumerate(tiles):
                            o = ps[0:n, i * cols:(i + 1) * cols]
                            if bias is not None:
                                for part in range(2):
                                    mm(o, ident_h[0:5, bias:bias + 1].broadcast_to([5, n]), b_rows[:, part, :],
                                       start=part == 0, stop=False)
                            last = product(o, lambda xp, m: src[:, xp, m, t0:t0 + n],
                                           lambda wp, m: ws[:, wp, k0 + m, col:col + cols], n_in,
                                           start=bias is None)
                        full = a_full if which == "a" else v_full
                        last.then_inc(full, one(full))

                    token_tiles = [(t * P, P) for t in range(NT)]

                    def values(a, ws, col, src, n_in, *what):
                        to_raw(*what)
                        if a.dim == 16:
                            token_major(ws, col, 256, src, n_in, a.key_tiles, "a", *what)
                        else:
                            for tile in a.key_tiles:
                                token_major(ws, col, 512, src, n_in, [tile], "a", *what)

                    def row_scores(g):
                        k, s, h = ORDER[g]
                        a = ATTNS[k]
                        if h == 0:
                            e.wait_ge(split_done, was_split("k", k, s))
                        t, q0, kx = a.at(h)
                        ps = slot("v", "max", g)
                        for i in range(NT):
                            o = ps[:, i * TOK:i * TOK + a.keys]
                            last = mm(o, qT[s][q0:q0 + 32, 0, t, i * P:i * P + P], kT[s][q0:q0 + 32, 0, kx, 0:a.keys],
                                      start=True, stop=not a.causal)
                            if a.causal:
                                last = mm(o, ident_h[:, :], mask_q[:, i, :], start=False, stop=True)
                        last.then_inc(v_full, one(v_full))

                    def exact_scores(g):
                        k, s, h = ORDER[g]
                        a = ATTNS[k]
                        t, q0, kx = a.at(h)
                        ps = slot("a", "p", g)
                        e.wait_ge(v_done, moved("max", g))
                        for j, (k0, n) in enumerate(a.key_tiles):
                            i0 = j * P if a.causal else 0
                            c0 = j * TOK
                            o = ps[0:n, c0:c0 + TOK - i0]
                            for kp, qp in PARTS:
                                mm(o, kT[s][q0:q0 + 32, kp, kx, k0:k0 + n], qT[s][q0:q0 + 32, qp, t, i0:TOK],
                                   start=(kp, qp) == (0, 0), stop=False)
                            if a.causal:
                                mm(ps[0:n, c0:c0 + P], ident_h[:, :], mask_k[:, :], start=False, stop=False)
                            for i in range(i0 // P, NT):
                                c = c0 + i * P - i0
                                last = mm(ps[0:n, c:c + P], negm[:, h * NT + i:h * NT + i + 1].broadcast_to([P, n]),
                                          ident_h[:, :], start=False, stop=i == NT - 1)
                        last.then_inc(a_full, one(a_full))

                    def weighted_values(g):
                        k, s, h = ORDER[g]
                        a = ATTNS[k]
                        D = a.dim
                        group = sent(o_full)
                        if h % a.group == 0 and group >= 2:
                            e.wait_ge(o_done, group - 1)
                        if h == 0:
                            e.wait_ge(split_done, was_split("v", k, s))
                        e.wait_ge(ps_ready, g + 1)
                        if a.keep_after:
                            e.wait_ge(pm_ready, upcoming(e, pm_ready))

                        def pr(part, n, c):
                            return prob[0:n, part, g % PBUF, c:c + P]

                        for i in range(NT):
                            c = i * TOK + (h % a.group) * (D + 1)
                            o = o_bank[group % 2][:, c:c + D + 1]
                            if a.keep_after:
                                for part in range(2):
                                    mm(o, pr(part, P, i * P), zero_one[:, :], start=part == 0, stop=False)
                                if i == 0:
                                    for pp, vp in PARTS:
                                        mm(o, pr(pp, P, TOK), val[s][:, vp, HEADS + h, :], start=False, stop=False)
                                else:
                                    for part in range(2):
                                        mm(o, pr(part, P, TOK + P), zero_one[:, :], start=False, stop=False)
                                for pp, vp in PARTS:
                                    last = mm(o_bank[group % 2][:, c:c + D], probm[:, pp, g % MBUF, i, :],
                                              val[s][:, vp, i * HEADS + h, 0:D], start=False,
                                              stop=(pp, vp) == PARTS[-1])
                                continue
                            js = [j for j in range(len(a.key_tiles)) if not (a.causal and j > i)]
                            for j in js:
                                n = a.key_tiles[j][1]
                                c1 = j * TOK + i * P - (j * P if a.causal else 0)
                                for pp, vp in PARTS:
                                    last = mm(o, pr(pp, n, c1), val[s][0:n, vp, j * HEADS + h, 32 - D:33],
                                              start=(j, pp, vp) == (0, 0, 0),
                                              stop=j == js[-1] and (pp, vp) == PARTS[-1])
                        if ends_group(a, h):
                            last.then_inc(o_full, one(o_full))
                            number["group", k, s] = group

                    def gates_transposed(k, s):
                        ps = slot("a", "gmT", k, s)
                        for part in range(2):
                            for t in range(NT):
                                c = part * TOK + t * P
                                last = mm(ps[0:16, c:c + P], gm_parts[:, part, t, :], ident_h[:, :],
                                          start=True, stop=True)
                        last.then_inc(a_full, one(a_full))

                    def hidden_layer(w1, w2, name, k, s, xT, hidT, bias=None, gates=None):
                        for part in range(2):
                            feature_major(w1, part * 4 * P, 4, xT, KT, TOK, name + str(part), k, s)
                            if part == 1:
                                e.wait_ge(split_done, was_split(name + "0", k, s))
                                token_major(w2, 0, DM, hidT, 4, token_tiles, "v", bias=bias)
                            if gates is not None:
                                for m in range(part * 4, part * 4 + 4, 2):
                                    ps = slot("v", "mix")
                                    for i in range(2):
                                        for p_ in range(2):
                                            last = mm(ps[:, i * TOK:(i + 1) * TOK], gates[:, m + i, :], gmT[:, p_, :],
                                                      start=p_ == 0, stop=p_ == 1)
                                    last.then_inc(v_full, one(v_full))
                            if part == 0:
                                yield from turns(k, name[0] + "0")
                        yield from turns(k, name[0] + "1")
                        e.wait_ge(split_done, was_split(name + "1", k, s))
                        token_major(w2, 0, DM, hidT, 4, token_tiles, "v", k0=4)
                        yield from turns(k, name[0] + "2")

                    def between_attentions(k, s):
                        oT, xT, yT, hidT = buffers_of(k, s)
                        if k > 0:
                            a = ATTNS[k - 1]
                            e.wait_ge(o_done, number["group", k - 1, s] + 1)
                            to_raw("oT", k, s)
                            for f in range(0, a.tiles, 2):
                                transposes(o_tok, 2, "oT", k, s, first=f)
                            yield from turns(k, "oT")
                            e.wait_ge(split_done, was_split("oT", k, s))
                            w_out = (w_o0, w_o1, w_o2, w_li1[0], w_li1[1])[k - 1]
                            token_major(w_out, 0, DM, oT, a.tiles, token_tiles, "v",
                                        bias=(None, None, 0, 1, 2)[k - 1])
                            yield from turns(k, "out")
                            if k == 3:
                                yield from turns(k, "norm2")
                                yield from turns(k, "norm3")
                        if k == 2:
                            to_xT(x[s], z_ready, "xT_e", k, s)
                            yield from turns(k, "xT_e")
                            e.wait_ge(split_done, was_split("xT_e", k, s))
                            token_major(w_router, 0, EXPERTS, xT, KT, token_tiles, "v")
                            yield from turns(k, "router")
                            e.wait_ge(gm_ready, upcoming(e, gm_ready))
                            gates_transposed(k, s)
                            for n in range(EXPERTS):
                                if n in (1, 4):
                                    yield from turns(k, ("best", "experts")[n == 4])
                                if n == 1:
                                    e.wait_ge(a_done, moved("gmT", k, s))
                                    ps = slot("v")
                                    for t in range(NT):
                                        last = product(ps[:, t * DM:(t + 1) * DM],
                                                       lambda gp, _: gmT[0:EXPERTS, gp, t * P:t * P + P],
                                                       lambda bp, _: b_exp[:, bp, :], 1)
                                    last.then_inc(v_full, one(v_full))
                                token_major(w_exp, 0, DM, xT, KT, token_tiles, "v", k0=n * KT)
                            yield from turns(k, "experts2")
                        if k >= 4:
                            i = k - 4
                            to_xT(z[s], zo_ready, "xoT", k, s)
                            yield from turns(k, "xoT")
                            e.wait_ge(split_done, was_split("xoT", k, s))
                            yield from hidden_layer(w_li2[i], w_li3[i], "hidden", k, s, xT, hidT, bias=3 + i)
                            if k == 4:
                                yield from turns(k, "norm3")
                        if k == 5:
                            to_xT(x[s], z_ready, "xT", k, s)
                            yield from turns(k, "xT")
                            e.wait_ge(split_done, was_split("xT", k, s))
                            token_major(w_sel, 0, TOP_EXPERTS, xT, KT, token_tiles, "a", "sel", k, s)
                            yield from turns(k, "sel")
                            e.wait_ge(gm_ready, upcoming(e, gm_ready))
                            gates_transposed(k, s)
                            yield from turns(k, "gates")
                            e.wait_ge(a_done, moved("gmT", k, s))
                            yield from hidden_layer(w_keys, w_vals, "relu", k, s, xT, hidT, gates=spread)
                            return
                        a = ATTNS[k]
                        if k == 0:
                            e.wait_ge(x_in, 16 * STREAMS)
                            to_xT(x[s], None, "xT", k, s)
                        elif k < 3:
                            to_xT(x[s], z_ready, "xT", k, s)
                        else:
                            to_xT(z[s], z_ready, "xT", k, s)
                        if k == 4:
                            e.wait_ge(zc_ready, upcoming(e, zc_ready))
                            ps = slot("a", "yT", k, s)
                            nc.tensor.transpose(ps[:, 0:CTX_TOK], cx[s][0:CTX_TOK, 0:CTX_DIM],
                                                ident[0:CTX_TOK, 0:CTX_TOK]).then_inc(a_full, one(a_full))
                        yield from turns(k, "xT")
                        e.wait_ge(split_done, was_split("xT", k, s))
                        w_q, col_q, w_k, col_k, w_v, col_v, y, n_in = (
                            (w_qkv0, 0, w_qkv0, DM, w_qkv0, 2 * DM, xT, KT),
                            (w_q1, 0, w_kv1, 0, w_kv1, DM, yT, 1),
                            (w_qkv2, 0, w_qkv2, DM, w_qkv2, 2 * DM, xT, KT),
                            (w_aq[0], 0, w_ak[0], 0, w_av[0], 0, yT, KT),
                            (w_aq[1], 0, w_ak[1], 0, w_av[1], 0, yT, 1))[k]
                        for what, w, col, source, n, tok in (("q", w_q, col_q, xT, KT, TOK),
                                                             ("k", w_k, col_k, y, n_in, a.keys)):
                            if a.splat:
                                feature_major(w, col, a.tiles, source, n, tok, what + "_raw", k, s)
                                yield from turns(k, what + "_raw")
                                to_raw(what, k, s)
                                e.wait_ge(split_done, was_split(what + "_raw", k, s))
                                r0 = 4 * (half[what + "_raw", k, s] % 2)
                                ps = slot("a", what, k, s)
                                for t in range(KT):
                                    o = ps[:, t * TOK:(t + 1) * TOK]
                                    mm(o, minus2c[:, t], raw[:, r0 + t, :], start=True, stop=False)
                                    last = mm(o, block16[:, :, :].rearrange("p a b -> p (a b)"),
                                              (z if what == "q" else xo)[s][:, t, :], start=False, stop=True)
                                last.then_inc(a_full, one(a_full))
                            else:
                                feature_major(w, col, a.tiles, source, n, tok, what, k, s)
                            yield from turns(k, what)
                        values(a, w_v, col_v, y, n_in, "v", k, s)
                        yield from turns(k, "v")

                    between = {(k, s): between_attentions(k, s) for k in range(6) for s in range(STREAMS)}
                    for _ in between[0, 0]:
                        pass
                    for n in range(STEPS):
                        if n < len(ORDER):
                            row_scores(n)
                        if 0 <= n - EXACT_LAG < len(ORDER):
                            exact_scores(n - EXACT_LAG)
                        if 0 <= n - PV_LAG < len(ORDER):
                            weighted_values(n - PV_LAG)
                        turn(between, n)
                        turn(between, n, last=True)
                    finish(between)

                @block.scalar
                def _(e):
                    act = nc.scalar.activation
                    moves = [0]

                    def next_half():
                        n = moves[0]
                        moves[0] += 1
                        if n >= 2:
                            e.wait_ge(split_done, n - 1)
                        return 4 * (n % 2)

                    def to_features(ps, high, at, gain=None, offset=None):
                        src = ps[:, :].rearrange("p (t n) -> p t n", t=KT)
                        if offset is None:
                            act(high[:, 0], src, ACT.Copy)
                            return act(raw[:, at:at + KT, :], src, ACT.Copy)
                        for f in range(KT):
                            for dst in (high[:, 0, f, :], raw[:, at + f, :]):
                                last = act(dst, src[:, f, :], ACT.Identity, bias=offset[:, f:f + 1],
                                           scale=1.0 if gain is None else gain[:, f:f + 1])
                        return last

                    def next_features(xT, gain=None, offset=None):
                        at = next_half()
                        e.wait_ge(a_full, upcoming(e, a_full))
                        to_features(ring_a[bank_of(e, a_full)], xT, at, gain, offset).then_inc(a_done, one(a_done))

                    def raw_tiles(tiles, n_tok, high=None, bias=None):
                        at = next_half()
                        for m in range(0, tiles, 2):
                            e.wait_ge(a_full, upcoming(e, a_full))
                            ps = ring_a[bank_of(e, a_full)]
                            src = ps[:, :].rearrange("p (t n) -> p t n", t=2)[:, :, 0:n_tok]
                            outs = [raw[:, at + m:at + m + 2, 0:n_tok]]
                            if high is not None:
                                outs.insert(0, high[:, 0, m:m + 2, 0:n_tok])
                            for dst in outs:
                                if bias is None:
                                    last = act(dst, src, ACT.Copy, scale=1 / W_SCALE)
                                else:
                                    for i in range(2):
                                        last = act(dst[:, i, :], src[:, i, :], ACT.Identity,
                                                   bias=bias[:, m + i:m + i + 1], scale=1 / W_SCALE)
                            last.then_inc(a_done, one(a_done))

                    def value_tiles(a, s):
                        cols = HEADS * a.dim
                        at = next_half()
                        flat = raw[:, at:at + 4, :].rearrange("p t n -> p (t n)")
                        for group in ([a.key_tiles] if a.dim == 16 else [[t] for t in a.key_tiles]):
                            e.wait_ge(a_full, upcoming(e, a_full))
                            ps = ring_a[bank_of(e, a_full)]
                            for i, (k0, n) in enumerate(group):
                                j = k0 // P
                                src = ps[0:n, i * cols:(i + 1) * cols]
                                act(val[s][0:n, 0, j * HEADS:(j + 1) * HEADS, 32 - a.dim:32],
                                    src.rearrange("p (h d) -> p h d", d=a.dim), ACT.Copy, scale=1 / W_SCALE)
                                last = act(flat[0:n, j * 512:j * 512 + cols], src, ACT.Copy, scale=1 / W_SCALE)
                            last.then_inc(a_done, one(a_done))

                    def exponentials(g):
                        a = ATTNS[ORDER[g][0]]
                        e.wait_ge(a_full, upcoming(e, a_full))
                        ps = ring_a[bank_of(e, a_full)]
                        if g >= PBUF32:
                            e.wait_ge(ps_ready, g + 1 - PBUF32)
                        n = a.key_tiles[0][1]
                        cols = TOK * len(a.key_tiles) - (P if a.causal else 0)
                        act(p32[0:n, g % PBUF32, 0:cols], ps[0:n, 0:cols], ACT.Exp, bias=p_log[0:n, :], scale=a.scale)
                        act(prob[0:n, 0, g % PBUF, 0:cols], ps[0:n, 0:cols], ACT.Exp, bias=p_log[0:n, :],
                            scale=a.scale).then_inc(a_done, one(a_done))

                    def hidden_layer(k, name, function, bias=None):
                        for part in range(2):
                            at = next_half()
                            for m in range(0, 4, 2):
                                e.wait_ge(a_full, upcoming(e, a_full))
                                ps = ring_a[bank_of(e, a_full)]
                                if bias is None:
                                    last = act(raw[:, at + m:at + m + 2, :], ps[:, :].rearrange("p (t n) -> p t n", t=2),
                                               function, scale=1 / W_SCALE)
                                else:
                                    for i in range(2):
                                        f = part * 4 + m + i
                                        last = act(raw[:, at + m + i, :], ps[:, i * TOK:(i + 1) * TOK], function,
                                                   bias=bias[:, f:f + 1], scale=1 / W_SCALE)
                                last.then_inc(a_done, one(a_done))
                            yield from turns(k, name + str(part))
                        yield from turns(k, name + "2")

                    def between_attentions(k, s):
                        oT, xT, yT, hidT = buffers_of(k, s)
                        if k > 0:
                            a = ATTNS[k - 1]
                            at = next_half()
                            for f0 in range(0, a.tiles, 2):
                                e.wait_ge(a_full, upcoming(e, a_full))
                                ps = ring_a[bank_of(e, a_full)]
                                if a.causal:
                                    last = to_features(ps, oT, at, offset=bq2[:, 4:6])
                                else:
                                    last = to_features(ps, oT[:, :, f0:f0 + 2, :], at + f0)
                                last.then_inc(a_done, one(a_done))
                            yield from turns(k, "oT")
                            yield from turns(k, "out")
                            if k == 3:
                                yield from turns(k, "norm2")
                                yield from turns(k, "norm3")
                        if k == 2:
                            next_features(xT)
                            yield from turns(k, "xT_e")
                            e.wait_ge(nmax_ready, upcoming(e, nmax_ready))
                            for t in range(NT):
                                last = act(ex[:, t, 0:EXPERTS], lg[:, t, 0:EXPERTS], ACT.Exp,
                                           bias=nmax[:, t:t + 1], accum_out=esum[:, t:t + 1])
                            last.then_inc(exps_ready, one(exps_ready))
                            yield from turns(k, "router")
                            e.wait_ge(a_full, upcoming(e, a_full))
                            act(gmT[:, :, :], ring_a[bank_of(e, a_full)][0:16, :].rearrange("p (c n) -> p c n", c=2),
                                ACT.Copy).then_inc(a_done, one(a_done))
                            yield from turns(k, "best")
                            yield from turns(k, "experts")
                            yield from turns(k, "experts2")
                        if k >= 4:
                            i = k - 4
                            next_features(xT, g3[i], b3[i])
                            yield from turns(k, "xoT")
                            yield from hidden_layer(k, "h", ACT.Gelu, b_li2[i])
                            if k == 4:
                                yield from turns(k, "norm3")
                        if k == 5:
                            next_features(xT)
                            yield from turns(k, "xT")
                            e.wait_ge(a_full, upcoming(e, a_full))
                            act(ex[:, :, :], ring_a[bank_of(e, a_full)][:, 0:NT * TOP_EXPERTS].rearrange(
                                "p (t n) -> p t n", t=NT), ACT.Exp, scale=-1 / W_SCALE).then_inc(a_done, one(a_done))
                            yield from turns(k, "sel")
                            e.wait_ge(a_full, upcoming(e, a_full))
                            act(gmT[:, :, :], ring_a[bank_of(e, a_full)][0:16, :].rearrange("p (c n) -> p c n", c=2),
                                ACT.Copy).then_inc(a_done, one(a_done))
                            yield from turns(k, "gates")
                            yield from hidden_layer(k, "r", ACT.Relu)
                            return
                        a = ATTNS[k]
                        if k < 3:
                            next_features(xT)
                        else:
                            i = k - 3
                            at = next_half()
                            e.wait_ge(a_full, upcoming(e, a_full))
                            ps = ring_a[bank_of(e, a_full)]
                            last = to_features(ps, xT, at, gx[i], bx[i])
                            if i == 0:
                                last = to_features(ps, yT, at + 2, gy[i], by[i])
                            last.then_inc(a_done, one(a_done))
                            if i == 1:
                                e.wait_ge(a_full, upcoming(e, a_full))
                                ps = ring_a[bank_of(e, a_full)]
                                for dst in (yT[:, 0, 0, 0:CTX_TOK], raw[:, at + 2, 0:CTX_TOK]):
                                    last = act(dst, ps[:, 0:CTX_TOK], ACT.Identity, bias=by[i][:, 0:1],
                                               scale=gy[i][:, 0:1])
                                last.then_inc(a_done, one(a_done))
                        yield from turns(k, "xT")
                        if a.splat:
                            for part in range(2):
                                raw_tiles(2, TOK)
                                yield from turns(k, ("q", "k")[part] + "_raw")
                                at = next_half()
                                e.wait_ge(a_full, upcoming(e, a_full))
                                ps = ring_a[bank_of(e, a_full)]
                                for t in range(KT):
                                    last = act(raw[:, at + t, :], ps[:, t * TOK:(t + 1) * TOK], ACT.Exp,
                                               bias=w_bias[:, t:t + 1], scale=inv_var[:, t:t + 1])
                                last.then_inc(a_done, one(a_done))
                                yield from turns(k, ("q", "k")[part])
                        else:
                            raw_tiles(a.tiles, TOK, qT[s], bq2[:, 0:2] if a.causal else None)
                            yield from turns(k, "q")
                            raw_tiles(a.tiles, a.keys, kT[s] if a.dim == 32 else None, bq2[:, 2:4] if a.causal else None)
                            yield from turns(k, "k")
                        value_tiles(a, s)
                        yield from turns(k, "v")

                    between = {(k, s): between_attentions(k, s) for k in range(6) for s in range(STREAMS)}
                    for _ in between[0, 0]:
                        pass
                    for n in range(STEPS):
                        if 0 <= n - EXACT_LAG < len(ORDER):
                            exponentials(n - EXACT_LAG)
                        turn(between, n)
                        turn(between, n, last=True)
                    finish(between)

                @block.vector
                def _(e):
                    v = nc.vector
                    moves = [0]

                    def flat(t):
                        return t[:, :, :].rearrange("p t f -> p (t f)")

                    def norm(src, dst, ready=dve_step, n=P, nt=NT):
                        for t in range(nt):
                            v.bn_stats(stats[0:n, t], src[0:n, t, :]).then_inc(dve_step, one(dve_step))
                        e.wait_ge(dve_step, sent(dve_step))
                        for t in range(nt):
                            v.bn_aggr(mv[0:n, t], stats[0:n, t]).then_inc(dve_step, one(dve_step))
                        e.wait_ge(dve_step, sent(dve_step))
                        v.tensor_scalar(veps[0:n, 0:nt], mv[0:n, 0:nt, 1], EPS, None, ALU.add).then_inc(var_ready, one(var_ready))
                        e.wait_ge(rstd_ready, upcoming(e, rstd_ready))
                        for t in range(nt):
                            signal = dve_step if t < nt - 1 else ready
                            v.tensor_scalar(dst[0:n, t, :], src[0:n, t, :], mv[0:n, t, 0:1], rstd[0:n, t:t + 1],
                                            ALU.subtract, ALU.mult).then_inc(signal, one(signal))
                        e.wait_ge(dve_step, sent(dve_step))
                        e.wait_ge(ready, sent(ready))

                    def gain(s, i):
                        for op, row in ((ALU.mult, r_g[i]), (ALU.add, r_b[i])):
                            v.tensor_tensor(xa[s][:, :, :], xa[s][:, :, :],
                                            row[:, :].rearrange("p (a n) -> p a n", a=1)
                                            .broadcast_to([P, NT, DM]), op).then_inc(dve_step, one(dve_step))
                            e.wait_ge(dve_step, sent(dve_step))

                    def low_part(low, src, high):
                        return v.tensor_tensor(low, src, high, ALU.subtract)

                    def split(src, high, low, scale=None):
                        if scale is None:
                            v.tensor_copy(high, src).then_inc(dve_step, one(dve_step))
                            e.wait_ge(dve_step, sent(dve_step))
                            return v.tensor_tensor(low, src, high, ALU.subtract)
                        v.tensor_scalar(high, src, scale, None, ALU.mult).then_inc(dve_step, one(dve_step))
                        e.wait_ge(dve_step, sent(dve_step))
                        return v.scalar_tensor_tensor(low, src, scale, high, ALU.mult, ALU.subtract)

                    def next_half(*what):
                        e.wait_ge(a_done, moved(*what))
                        moves[0] += 1
                        return 4 * ((moves[0] - 1) % 2)

                    def split_xT(xT, *what):
                        at = next_half(*what)
                        low_part(xT[:, 1], raw[:, at:at + KT, :], xT[:, 0]).then_inc(split_done, one(split_done))

                    def split_queries(a, k, s):
                        at = next_half("q", k, s)
                        n = a.tiles
                        if a.splat:
                            last = split(raw[:, at:at + n, :], qT[s][:, 0, 0:n, :], qT[s][:, 1, 0:n, :])
                        else:
                            last = low_part(qT[s][:, 1, 0:n, :], raw[:, at:at + n, :], qT[s][:, 0, 0:n, :])
                        last.then_inc(split_done, one(split_done))

                    def split_keys(a, k, s):
                        at = next_half("k", k, s)
                        n = a.keys
                        src = raw[:, at:at + a.tiles, 0:n]
                        kk = kT[s]
                        if a.dim == 32:
                            last = low_part(kk[:, 1, :, 0:n], src, kk[:, 0, :, 0:n])
                        else:
                            for o in range(2):
                                if a.splat:
                                    for t in range(KT):
                                        last = split(raw[:, at + t, 0:n], kk[:, 0, 2 * o + t, 0:n],
                                                     kk[:, 1, 2 * o + t, 0:n], k_scale[:, o, t:t + 1])
                                else:
                                    last = split(src, kk[:, 0, 2 * o:2 * o + 2, 0:n], kk[:, 1, 2 * o:2 * o + 2, 0:n],
                                                 parity[:, o:o + 1])
                        last.then_inc(split_done, one(split_done))

                    def split_values(a, k, s):
                        at = next_half("v", k, s)
                        for j, (_, n) in enumerate(a.key_tiles):
                            to = val[s][0:n, :, j * HEADS:(j + 1) * HEADS, 32 - a.dim:32]
                            src = raw[0:n, at + 2 * j:at + 2 * j + 2, :].rearrange("p t n -> p (t n)")
                            last = low_part(to[:, 1], src[:, 0:HEADS * a.dim].rearrange("p (h d) -> p h d", d=a.dim),
                                            to[:, 0])
                        last.then_inc(split_done, one(split_done))

                    def row_maxima(g):
                        k, s, h = ORDER[g]
                        e.wait_ge(v_full, upcoming(e, v_full))
                        v.tensor_reduce(
                            negm[:, h * NT:(h + 1) * NT],
                            ring_v[bank_of(e, v_full)][:, :].rearrange("p (t n) -> p t n", t=NT)[:, :, 0:ATTNS[k].keys],
                            AX.X, ALU.max, negate=True).then_inc(v_done, one(v_done))

                    def low_exponentials(g):
                        a = ATTNS[ORDER[g][0]]
                        e.wait_ge(a_done, moved("p", g))
                        rows = a.key_tiles[0][1]
                        cols = TOK * len(a.key_tiles) - (P if a.causal else 0)
                        low_part(prob[0:rows, 1, g % PBUF, 0:cols], p32[0:rows, g % PBUF32, 0:cols],
                                 prob[0:rows, 0, g % PBUF, 0:cols]).then_inc(ps_ready, one(ps_ready))

                    def normalise(g):
                        k, s, h = ORDER[g]
                        a = ATTNS[k]
                        D, first = a.dim, h // a.group * a.group
                        n = h + 1 - first
                        if sent(o_done) > 0:
                            e.wait_ge(o_done, sent(o_done))
                        e.wait_ge(o_full, upcoming(e, o_full))
                        o = o_bank[(sent(o_done)) % 2][:, :].rearrange("p (t c) -> p t c", t=NT)[:, :, 0:n * (D + 1)]
                        o = o.rearrange("p t (h d) -> p t h d", d=D + 1)
                        v.reciprocal(recip[:, :, 0:n], o[:, :, :, D]).then_inc(dve_step, one(dve_step))
                        e.wait_ge(dve_step, sent(dve_step))
                        dst = o_tok[:, :, first * D:(h + 1) * D].rearrange("p t (h d) -> p t h d", d=D)
                        v.tensor_tensor(dst, o[:, :, :, 0:D], recip[:, :, 0:n].rearrange(
                            "p t (h a) -> p t h a", a=1).broadcast_to([P, NT, n, D]), ALU.mult
                                        ).then_inc(o_done, one(o_done))

                    def add_bank(dst, other, scale=1 / W_SCALE):
                        e.wait_ge(v_full, upcoming(e, v_full))
                        v.scalar_tensor_tensor(flat(dst), ring_v[bank_of(e, v_full)][:, :], scale, flat(other),
                                               ALU.mult, ALU.add).then_inc(v_done, one(v_done))
                        e.wait_ge(v_done, sent(v_done))

                    def hidden_layer(name, k, s, hidT, dst, gated=False):
                        for part in range(2):
                            if part == 1:
                                add_bank(dst, dst)
                            at = next_half(name + str(part), k, s)
                            if gated:
                                for m in range(0, 4, 2):
                                    r = raw[:, at + m:at + m + 2, :].rearrange("p t n -> p (t n)")
                                    e.wait_ge(v_full, upcoming(e, v_full))
                                    v.tensor_tensor(r, ring_v[bank_of(e, v_full)][:, :], r, ALU.mult
                                                    ).then_inc(v_done, one(v_done))
                                e.wait_ge(v_done, sent(v_done))
                            split(raw[:, at:at + 4, :], hidT[:, 0], hidT[:, 1]).then_inc(split_done, one(split_done))
                            yield from turns(k, name[0] + str(part))
                        add_bank(dst, dst)

                    def choose_best():
                        e.wait_ge(v_full, upcoming(e, v_full))
                        v.scalar_tensor_tensor(
                            lg[:, :, 0:EXPERTS], ring_v[bank_of(e, v_full)][:, 0:NT * EXPERTS].rearrange(
                                "p (t n) -> p t n", t=NT), 1 / W_SCALE,
                            r_router[:, :].rearrange("p (a n) -> p a n", a=1).broadcast_to([P, NT, EXPERTS]),
                            ALU.mult, ALU.add).then_inc(v_done, one(v_done))
                        e.wait_ge(v_done, sent(v_done))
                        for t in range(NT):
                            v.max(top8[:, t], lg[:, t, 0:EXPERTS]).then_inc(dve_step, one(dve_step))
                        e.wait_ge(dve_step, sent(dve_step))
                        v.tensor_copy(lgv[:, :, 0:1], top8[:, :, 0:1]).then_inc(dve_step, one(dve_step))
                        v.tensor_scalar(nmax[:, :], top8[:, :, 0], -1.0, None, ALU.mult).then_inc(nmax_ready, one(nmax_ready))
                        e.wait_ge(dve_step, sent(dve_step))
                        for t in range(NT):
                            v.match_replace(mr[:, t, 0:16], lgv[:, t], lg[:, t], MARK).then_inc(dve_step, one(dve_step))
                        e.wait_ge(dve_step, sent(dve_step))
                        v.tensor_scalar(gm[:, :, 0:EXPERTS], mr[:, :, 0:EXPERTS], MARK, None, ALU.is_equal).then_inc(dve_step, one(dve_step))
                        e.wait_ge(exps_ready, upcoming(e, exps_ready))
                        v.reciprocal(gate[:, :], esum[:, :]).then_inc(dve_step, one(dve_step))
                        e.wait_ge(dve_step, sent(dve_step))
                        for t in range(NT):
                            v.tensor_scalar(gm[:, t, 0:EXPERTS], gm[:, t, 0:EXPERTS], gate[:, t:t + 1],
                                            None, ALU.mult).then_inc(dve_step, one(dve_step))
                        e.wait_ge(dve_step, sent(dve_step))
                        split(gm[:, :, :], gm_parts[:, 0], gm_parts[:, 1]).then_inc(gm_ready, one(gm_ready))
                        v.tensor_scalar(gmw[:, :, :], gm[:, :, 0:EXPERTS], 1 / W_SCALE, None, ALU.mult
                                        ).then_inc(dve_step, one(dve_step))
                        e.wait_ge(dve_step, sent(dve_step))

                    def choose_four(k, s):
                        e.wait_ge(a_done, moved("sel", k, s))
                        v.tensor_scalar(ex[:, :, :], ex[:, :, :], 1.0, None, ALU.add).then_inc(dve_step, one(dve_step))
                        e.wait_ge(dve_step, sent(dve_step))
                        v.reciprocal(pe16[:, :, 0:16], ex[:, :, :]).then_inc(dve_step, one(dve_step))
                        e.wait_ge(dve_step, sent(dve_step))
                        for t in range(NT):
                            v.max(top8[:, t], pe16[:, t, 0:16]).then_inc(dve_step, one(dve_step))
                        e.wait_ge(dve_step, sent(dve_step))
                        v.tensor_copy(pv[:, :, 0:TOP_K], top8[:, :, 0:TOP_K]).then_inc(dve_step, one(dve_step))
                        v.tensor_reduce(gate[:, :], top8[:, :, 0:TOP_K], AX.X, ALU.add).then_inc(dve_step, one(dve_step))
                        e.wait_ge(dve_step, sent(dve_step))
                        for t in range(NT):
                            v.match_replace(mr[:, t], pv[:, t], pe16[:, t], 2.0).then_inc(dve_step, one(dve_step))
                        v.tensor_scalar(gate[:, :], gate[:, :], 1e-9, None, ALU.max).then_inc(dve_step, one(dve_step))
                        e.wait_ge(dve_step, sent(dve_step))
                        v.reciprocal(gate[:, :], gate[:, :]).then_inc(dve_step, one(dve_step))
                        e.wait_ge(dve_step, sent(dve_step))
                        v.tensor_scalar(gate[:, :], gate[:, :], r_route[:, 0:1], None, ALU.mult).then_inc(dve_step, one(dve_step))
                        v.scalar_tensor_tensor(gm[:, :, :], mr[:, :, 0:16], 2.0, pe16[:, :, 0:16],
                                               ALU.is_equal, ALU.mult).then_inc(dve_step, one(dve_step))
                        e.wait_ge(dve_step, sent(dve_step))
                        for t in range(NT):
                            v.tensor_scalar(gm[:, t, :], gm[:, t, :], gate[:, t:t + 1], None, ALU.mult
                                            ).then_inc(dve_step, one(dve_step))
                        e.wait_ge(dve_step, sent(dve_step))
                        split(gm[:, :, :], gm_parts[:, 0], gm_parts[:, 1]).then_inc(gm_ready, one(gm_ready))

                    def between_attentions(k, s):
                        oT, xT, yT, hidT = buffers_of(k, s)
                        if k > 0:
                            a = ATTNS[k - 1]
                            at = next_half("oT", k, s)
                            low_part(oT[:, 1, 0:a.tiles, :], raw[:, at:at + a.tiles, :], oT[:, 0, 0:a.tiles, :]
                                     ).then_inc(split_done, one(split_done))
                            yield from turns(k, "oT")
                            if k <= 2:
                                add_bank(x[s], x[s])
                                norm(x[s], x[s], z_ready)
                            elif k == 3:
                                add_bank(x[s], x[s])
                                norm(x[s], x[s])
                            else:
                                add_bank(xo[s], xa[s])
                                norm(xo[s], z[s], zo_ready)
                            yield from turns(k, "out")
                            if k == 3:
                                norm(x[s], xa[s])
                                gain(s, 0)
                                yield from turns(k, "norm2")
                                norm(xa[s], z[s], z_ready)
                                yield from turns(k, "norm3")
                        if k == 2:
                            split_xT(xT, "xT_e", k, s)
                            yield from turns(k, "xT_e")
                            choose_best()
                            yield from turns(k, "router")
                            for n in range(EXPERTS):
                                if n in (1, 4):
                                    yield from turns(k, ("best", "experts")[n == 4])
                                if n == 1:
                                    add_bank(x[s], x[s])
                                e.wait_ge(v_full, upcoming(e, v_full))
                                ps = ring_v[bank_of(e, v_full)]
                                for t in range(NT):
                                    signal = dve_step if t < NT - 1 else v_done
                                    v.scalar_tensor_tensor(x[s][:, t, :], ps[:, t * DM:(t + 1) * DM],
                                                           gmw[:, t, n:n + 1], x[s][:, t, :],
                                                           ALU.mult, ALU.add).then_inc(signal, one(signal))
                                e.wait_ge(dve_step, sent(dve_step))
                                e.wait_ge(v_done, sent(v_done))
                            norm(x[s], x[s], z_ready)
                            yield from turns(k, "experts2")
                        if k >= 4:
                            split_xT(xT, "xoT", k, s)
                            yield from turns(k, "xoT")
                            e.wait_ge(xa_ready, upcoming(e, xa_ready))
                            yield from hidden_layer("hidden", k, s, hidT, xa[s])
                            if k == 4:
                                norm(xa[s], xa[s])
                                gain(s, 1)
                                yield from turns(k, "h2")
                                norm(xa[s], z[s], z_ready)
                                yield from turns(k, "norm3")
                            else:
                                v.tensor_tensor(flat(x[s]), flat(x[s]), flat(xa[s]), ALU.add).then_inc(dve_step, one(dve_step))
                                e.wait_ge(dve_step, sent(dve_step))
                                norm(x[s], x[s], z_ready)
                                yield from turns(k, "h2")
                        if k == 5:
                            split_xT(xT, "xT", k, s)
                            yield from turns(k, "xT")
                            choose_four(k, s)
                            yield from turns(k, "sel")
                            yield from turns(k, "gates")
                            yield from hidden_layer("relu", k, s, hidT, x[s], gated=True)
                            norm(x[s], x[s], out_ready)
                            yield from turns(k, "r2")
                            return
                        a = ATTNS[k]
                        if k == 1:
                            e.wait_ge(c_in, 32 * STREAMS)
                            split(cxT[s][:, :], yT[:, 0, 0, 0:CTX_TOK], yT[:, 1, 0, 0:CTX_TOK]
                                  ).then_inc(dve_step, one(dve_step))
                        if k == 4:
                            own = cx[s][:, :].rearrange("p (a f) -> p a f", a=1)
                            norm(own, own, zc_ready, n=CTX_TOK, nt=1)
                        if k < 3:
                            split_xT(xT, "xT", k, s)
                        elif k == 3:
                            at = next_half("xT", k, s)
                            low_part(oT[:, 1], raw[:, at:at + 4, :], oT[:, 0]).then_inc(split_done, one(split_done))
                        else:
                            at = next_half("yT", k, s)
                            low_part(xT[:, 1], raw[:, at:at + KT, :], xT[:, 0]).then_inc(dve_step, one(dve_step))
                            low_part(yT[:, 1, 0, 0:CTX_TOK], raw[:, at + 2, 0:CTX_TOK], yT[:, 0, 0, 0:CTX_TOK]
                                     ).then_inc(split_done, one(split_done))
                        yield from turns(k, "xT")
                        for what in ("q", "k"):
                            if a.splat:
                                at = next_half(what + "_raw", k, s)
                                v.tensor_tensor((z if what == "q" else xo)[s][:, :, :], raw[:, at:at + 2, :],
                                                raw[:, at:at + 2, :], ALU.mult).then_inc(split_done, one(split_done))
                                yield from turns(k, what + "_raw")
                            if what == "q":
                                split_queries(a, k, s)
                            else:
                                split_keys(a, k, s)
                            yield from turns(k, what)
                        split_values(a, k, s)
                        yield from turns(k, "v")

                    between = {(k, s): between_attentions(k, s) for k in range(6) for s in range(STREAMS)}
                    for _ in between[0, 0]:
                        pass
                    for n in range(STEPS):
                        if n < len(ORDER):
                            row_maxima(n)
                        if 0 <= n - LOW_LAG < len(ORDER):
                            low_exponentials(n - LOW_LAG)
                        turn(between, n)
                        g = n - NORM_LAG
                        if g >= 0 and ends_group(ATTNS[ORDER[g][0]], ORDER[g][2]):
                            normalise(g)
                        turn(between, n, last=True)
                    finish(between)

                @block.gpsimd
                def _(e):
                    g = nc.gpsimd

                    def root(n=P, nt=NT):
                        e.wait_ge(var_ready, upcoming(e, var_ready))
                        g.tensor_tensor(rstd[0:n, 0:nt], veps[0:n, 0:nt],
                                        minus_half[0:n, 0:nt], ALU.pow).then_inc(rstd_ready, one(rstd_ready))

                    def masked_exponentials(n):
                        e.wait_ge(ps_ready, n + 1)
                        for part in range(2):
                            for t in range(NT):
                                c = t * TOK + t * P
                                last = g.affine_select(out=probm[:, part, n % MBUF, t, :],
                                                       in_=prob[:, part, n % PBUF, c:c + P],
                                                       compare_op=ALU.is_gt, fill=0.0, base=0,
                                                       pattern=[[-1, P]], channel_multiplier=1)
                        last.then_inc(pm_ready, one(pm_ready))

                    def between_attentions(k, s):
                        if k > 0:
                            yield from turns(k, "oT")
                            root()
                            if k >= 4:
                                e.wait_ge(zo_ready, upcoming(e, zo_ready))
                                g.tensor_tensor(xa[s][:, :, :], xa[s][:, :, :], xo[s][:, :, :],
                                                ALU.add).then_inc(xa_ready, one(xa_ready))
                            yield from turns(k, "out")
                            if k == 3:
                                root()
                                yield from turns(k, "norm2")
                                root()
                                yield from turns(k, "norm3")
                        if k == 2:
                            for step in ("xT_e", "router", "best", "experts"):
                                yield from turns(k, step)
                            root()
                            yield from turns(k, "experts2")
                        if k >= 4:
                            for step in ("xoT", "h0", "h1"):
                                yield from turns(k, step)
                            root()
                            yield from turns(k, "h2")
                            if k == 4:
                                root()
                                yield from turns(k, "norm3")
                        if k == 5:
                            for step in ("xT", "sel", "gates", "r0", "r1"):
                                yield from turns(k, step)
                            root()
                            yield from turns(k, "r2")
                            return
                        if k == 4:
                            root(CTX_TOK, 1)
                        for step in ("xT", "q_raw", "q", "k_raw", "k", "v"):
                            if ATTNS[k].splat or "raw" not in step:
                                yield from turns(k, step)

                    between = {(k, s): between_attentions(k, s) for k in range(6) for s in range(STREAMS)}
                    for _ in between[0, 0]:
                        pass
                    for n in range(STEPS):
                        if 0 <= n - LOW_LAG < len(ORDER) and ATTNS[ORDER[n - LOW_LAG][0]].keep_after:
                            masked_exponentials(n - LOW_LAG)
                        turn(between, n)
                        turn(between, n, last=True)
                    finish(between)


            nc.gpsimd.sem_clear(loop_sems)
            nc.all_engine_barrier()


def laid_out(i):
    import numpy as np

    def np_(name):
        return np.asarray(i[name])

    def per_head(name):
        w = np_(name)
        return w.transpose(1, 0, 2).reshape(w.shape[1], -1)

    d = {
        "x": np_("x"),
        "ctx": np_("ctx_512"),
        "ctx_t": np_("ctx_512").transpose(0, 2, 1),
        "centers": np_("L0_attn_splat_centers").reshape(DM, 16),
        "centers_t": np_("L0_attn_splat_centers").transpose(0, 2, 1).reshape(DM, 16),
        "deltas": np_("L0_attn_splat_deltas").reshape(DM, 16),
        "deltas_t": np_("L0_attn_splat_deltas").transpose(0, 2, 1).reshape(DM, 16),
        "log_scales": np_("L0_attn_splat_log_scales").reshape(-1),
        "log_amps": np_("L0_attn_splat_log_amplitudes").reshape(-1),
        "movement": np_("L0_attn_movement_scale").reshape(1),
        "temperature": np_("L0_attn_temperature").reshape(1),
        "qkv0": np_("L0_attn_qkv_w").T,
        "o0": np_("L0_attn_out_w").T,
        "q1": np_("L0_xattn_Wq").T,
        "kv1": np_("L0_xattn_Wkv").T,
        "o1": np_("L0_xattn_Wo").T,
        "router": np_("L0_ffn_router_w"),
        "router_b": np_("L0_ffn_router_b"),
        "expert_w": np_("L0_ffn_expert_w"),
        "expert_b": np_("L0_ffn_expert_b"),
        "qkv2": np_("L1_attn_w_qkv"),
        "bqkv2": np_("L1_attn_b_qkv"),
        "o2": np_("L1_attn_w_out"),
        "bo2": np_("L1_attn_b_out"),
        "sel": np_("L1_ffn_expert_sel").T,
        "keys": per_head("L1_ffn_keys"),
        "values": np_("L1_ffn_values").reshape(HID, DM),
        "route": np_("L1_ffn_route_scale"),
    }
    for a in range(2):
        pre = f"L1_xattn_a{a + 1}_"
        d[f"ln_g{a}"] = np_(f"L1_xattn_ln{a + 1}_g")
        d[f"ln_b{a}"] = np_(f"L1_xattn_ln{a + 1}_b")
        for w in ("wq", "wk", "wv"):
            d[f"{w}{a}"] = per_head(pre + w)
        for w in ("li1", "li2", "li3"):
            d[f"{w}_{a}"] = np_(f"{pre}{w}_w")
            d[f"{w}_b{a}"] = np_(f"{pre}{w}_b")
        for w in ("lnx", "lny", "ln3"):
            d[f"{w}_g{a}"] = np_(f"{pre}{w}_g")
            d[f"{w}_b{a}"] = np_(f"{pre}{w}_b")
    for name in ["log_scales", "log_amps", "bqkv2"] + [
            f"{n}{a}" for n in ("lnx_g", "lnx_b", "lny_g", "lny_b", "ln3_g", "ln3_b", "li2_b") for a in range(2)]:
        d[name] = d[name].reshape(-1, P).T
    return {k: np.ascontiguousarray(v) for k, v in d.items()}


def kernel(**inputs):
    import concourse.bacc as _bacc
    from concourse import mybir as _mybir
    from concourse.bass_utils import run_bass_kernel_spmd as _run

    nc = _bacc.Bacc("TRN2", target_bir_lowering=False, num_devices=1)
    data = laid_out(inputs)
    arrays = {f"in_{name}": a for name, a in data.items()}
    io = {name: nc.dram_tensor(f"in_{name}", a.shape, _mybir.dt.from_np(a.dtype), kind="ExternalInput").ap()
          for name, a in data.items()}
    out = nc.dram_tensor("out_0", (BATCH, TOK, DM), _mybir.dt.float32, kind="ExternalOutput").ap()
    decoder(nc, io, out)
    r = _run(nc, [arrays], core_ids=[0])
    return r.results[0]["out_0"]
```
